# Optimizing a Trainium2 kernel written in Bass

```python
import numpy as np
import jax
import jax.numpy as jnp

def _softmax(x, axis=-1):
    return jax.nn.softmax(x, axis=axis)

def _gelu(x):
    return jax.nn.gelu(x, approximate=True)

def _silu(x):
    return jax.nn.silu(x)

def _sigmoid(x):
    return jax.nn.sigmoid(x)

def _layernorm(x, axis=-1, eps=1e-05):
    m = jnp.mean(x, axis=axis, keepdims=True)
    v = jnp.var(x, axis=axis, keepdims=True)
    return (x - m) / jnp.sqrt(v + eps)

def _scatter_add(tgt, idx, src, axis=0):
    return tgt.at[idx].add(src)

def _segment_sum(src, seg, n):
    return jax.ops.segment_sum(src, seg, n)
kernel_name = 'mk_gnn_preln_d4_gnn_r16_e433c6'

def setup_inputs(seed: int=0):
    np.random.seed(seed)
    _w = jnp.asarray

    def _rec_inputs():
        import jax
        import jax.numpy as jnp
        _gk = jax.random.key(seed)
        x = -0.0005121 + 1.001 * jax.random.normal(jax.random.fold_in(_gk, 1), (6250, 32), jnp.float32)
        _s = jax.random.randint(jax.random.fold_in(_gk, 2), (50000,), 0, 6250, jnp.int32)
        _d = jax.random.randint(jax.random.fold_in(_gk, 3), (50000,), 0, 6250, jnp.int32)
        _loop = jnp.arange(6250, dtype=jnp.int32)
        src = jnp.concatenate([_s, _d, _loop])
        dst = jnp.concatenate([_d, _s, _loop])
        _o = jnp.argsort(dst, stable=True)
        src = src[_o]
        dst = dst[_o]
        edge_weight = jax.random.uniform(jax.random.fold_in(_gk, 14), (106250,), jnp.float32, 0.0, 0.999999)
        return (x, src, dst, edge_weight)
    x, src, dst, edge_weight = _rec_inputs()

    def _L0_gnn_setup():
        import jax, jax.numpy as jnp
        import numpy as np
        N_NODES = 6250
        N_EDGES = 200000
        D_IN = 32
        N_HEADS = 4
        D_HEAD = 8
        key = jax.random.key(seed)
        k1, k2, k3, k4, k5, k6, k7 = jax.random.split(key, 7)
        scale = 1.0 / np.sqrt(D_IN)
        x = jax.random.normal(k1, (N_NODES, D_IN), dtype=jnp.float32)
        Wq = jax.random.normal(k2, (D_IN, N_HEADS * D_HEAD), dtype=jnp.float32) * scale
        Wk = jax.random.normal(k3, (D_IN, N_HEADS * D_HEAD), dtype=jnp.float32) * scale
        Wv = jax.random.normal(k4, (D_IN, N_HEADS * D_HEAD), dtype=jnp.float32) * scale
        Wo = jax.random.normal(k5, (N_HEADS * D_HEAD, D_IN), dtype=jnp.float32) * scale
        src = jax.random.randint(k6, (N_EDGES,), 0, N_NODES)
        dst = jax.random.randint(k7, (N_EDGES,), 0, N_NODES)
        edge_index = jnp.stack([src, dst], axis=0).astype(jnp.int64)
        return {'x': x, 'Wq': Wq, 'Wk': Wk, 'Wv': Wv, 'Wo': Wo, 'edge_index': edge_index}
    _L0_gnn_all = _L0_gnn_setup()
    _L0_gnn_in = {k: v for k, v in _L0_gnn_all.items() if k in ('Wq', 'Wk', 'Wv', 'Wo')}
    del _L0_gnn_all

    def _L1_gnn_setup():
        import jax, jax.numpy as jnp
        import numpy as np
        N = 6250
        E = 100000
        G = 64
        IN, H, OUT = (32, 64, 32)
        EPS = 1e-05

        def _gnn_forward(x, edge_index, edge_weight, batch, layers):
            n = x.shape[0]
            src, dst = (edge_index[0], edge_index[1])
            loop = jnp.arange(n)
            s = jnp.concatenate([src, loop])
            t = jnp.concatenate([dst, loop])
            w = jnp.concatenate([edge_weight, jnp.ones((n,), edge_weight.dtype)])
            deg = jax.ops.segment_sum(w, t, num_segments=n)
            dis = jnp.where(deg > 0, jax.lax.rsqrt(jnp.maximum(deg, 1e-12)), 0.0)
            coef = (dis[s] * w * dis[t])[:, None]
            counts = jnp.maximum(jax.ops.segment_sum(jnp.ones((n,), x.dtype), batch, num_segments=G), 1.0)[:, None]

            def gcn(h, W, b):
                h = h @ W
                return jax.ops.segment_sum(h[s] * coef, t, num_segments=n) + b

            def gnorm(h, gw, gb, ga):
                mean = jax.ops.segment_sum(h, batch, num_segments=G) / counts
                hc = h - ga * mean[batch]
                var = jax.ops.segment_sum(hc * hc, batch, num_segments=G) / counts
                return gw * hc * jax.lax.rsqrt(var[batch] + EPS) + gb
            n_layers = len(layers)
            for i, (W, b, gw, gb, ga) in enumerate(layers):
                x = gnorm(gcn(x, W, b), gw, gb, ga)
                if i < n_layers - 1:
                    x = jax.nn.relu(x)
            return x
        key = jax.random.key(seed)
        ks = jax.random.split(key, 16)
        d = {'x': jax.random.normal(ks[0], (N, IN), jnp.float32), 'edge_index': jax.random.randint(ks[1], (2, E), 0, N, jnp.int32), 'edge_weight': jax.random.uniform(ks[2], (E,), jnp.float32), 'batch': jnp.sort(jax.random.randint(ks[3], (N,), 0, G, jnp.int32))}
        dims = [(IN, H), (H, H), (H, H), (H, H), (H, OUT)]
        for i, (di, do) in enumerate(dims, start=1):
            k = jax.random.fold_in(key, i)
            d[f'W{i}'] = jax.random.normal(k, (di, do), jnp.float32) * (1.0 / np.sqrt(di))
            d[f'b{i}'] = jnp.zeros((do,), jnp.float32)
            d[f'g{i}w'] = jnp.ones((do,), jnp.float32)
            d[f'g{i}b'] = jnp.zeros((do,), jnp.float32)
            d[f'g{i}a'] = jnp.ones((do,), jnp.float32)
        return d
    _L1_gnn_all = _L1_gnn_setup()
    _L1_gnn_in = {k: v for k, v in _L1_gnn_all.items() if k in ('W1', 'b1', 'g1w', 'g1b', 'g1a', 'W2', 'b2', 'g2w', 'g2b', 'g2a', 'W3', 'b3', 'g3w', 'g3b', 'g3a', 'W4', 'b4', 'g4w', 'g4b', 'g4a', 'W5', 'b5', 'g5w', 'g5b', 'g5a')}
    del _L1_gnn_all

    def _L2_gnn_setup():
        import jax, jax.numpy as jnp
        import numpy as np
        N, E, IN_DIM, HID, HOUT = (1250, 20000, 32, 64, 64)

        def _mlp3(h, w0, b0, w1, b1, w2, b2):
            h = jnp.tanh(h @ w0.T + b0)
            h = jax.nn.relu(h @ w1.T + b1)
            return h @ w2.T + b2
        key = jax.random.key(seed)
        ks = jax.random.split(key, 26)
        f = lambda i, shape, s=0.1: jax.random.normal(ks[i], shape, jnp.float32) * s
        return {'x': f(0, (N, IN_DIM), 1.0), 'src': jax.random.randint(ks[1], (E,), 0, N), 'dst': jax.random.randint(ks[2], (E,), 0, N), 'W_fc': f(3, (HID, IN_DIM), 0.2), 'W_attn': f(4, (1, 2 * HID), 0.2), 'W_encK': f(5, (HID, HID)), 'b_encK': f(6, (HID,), 0.01), 'W_p1': f(7, (HID, HID)), 'b_p1': f(8, (HID,), 0.01), 'W_p2': f(9, (HID, HID)), 'b_p2': f(10, (HID,), 0.01), 'K_w0': f(11, (HOUT, HID)), 'K_b0': f(12, (HOUT,), 0.01), 'K_w1': f(13, (HOUT, HOUT)), 'K_b1': f(14, (HOUT,), 0.01), 'K_w2': f(15, (HOUT, HOUT)), 'K_b2': f(16, (HOUT,), 0.01), 'U_w0': f(17, (HOUT, HID)), 'U_b0': f(18, (HOUT,), 0.01), 'U_w1': f(19, (HOUT, HOUT)), 'U_b1': f(20, (HOUT,), 0.01), 'U_w2': f(21, (HOUT, HOUT)), 'U_b2': f(22, (HOUT,), 0.01), 'D': jax.random.uniform(ks[23], (IN_DIM, IN_DIM), jnp.float32)}
    _L2_gnn_all = _L2_gnn_setup()
    _L2_gnn_in = {k: v for k, v in _L2_gnn_all.items() if k in ('W_fc', 'W_attn', 'W_encK', 'b_encK', 'W_p1', 'b_p1', 'W_p2', 'b_p2', 'K_w0', 'K_b0', 'K_w1', 'K_b1', 'K_w2', 'K_b2', 'U_w0', 'U_b0', 'U_w1', 'U_b1', 'U_w2', 'U_b2', 'D')}
    del _L2_gnn_all

    def _L3_gnn_setup():
        import jax, jax.numpy as jnp
        import numpy as np
        N = 6250
        E = 100000
        F_IN = 32
        F_OUT = 32
        key = jax.random.key(seed)
        k1, k2, k3, k4, k5 = jax.random.split(key, 5)
        x = jax.random.normal(k1, (N, F_IN), dtype=jnp.float32)
        edge_src = jax.random.randint(k2, (E,), 0, N, dtype=jnp.int32)
        edge_dst = jax.random.randint(k3, (E,), 0, N, dtype=jnp.int32)
        bound = 1.0 / np.sqrt(2 * F_IN)
        W = jax.random.uniform(k4, (2 * F_IN, F_OUT), minval=-bound, maxval=bound, dtype=jnp.float32)
        b = jax.random.uniform(k5, (F_OUT,), minval=-bound, maxval=bound, dtype=jnp.float32)
        return {'x': x, 'W': W, 'b': b, 'edge_src': edge_src, 'edge_dst': edge_dst}
    _L3_gnn_all = _L3_gnn_setup()
    _L3_gnn_in = {k: v for k, v in _L3_gnn_all.items() if k in ('W', 'b')}
    del _L3_gnn_all
    return {'x': x, 'src': src, 'dst': dst, 'edge_weight': edge_weight, 'L0_gnn_Wq': _L0_gnn_in['Wq'], 'L0_gnn_Wk': _L0_gnn_in['Wk'], 'L0_gnn_Wv': _L0_gnn_in['Wv'], 'L0_gnn_Wo': _L0_gnn_in['Wo'], 'L1_gnn_W1': _L1_gnn_in['W1'], 'L1_gnn_b1': _L1_gnn_in['b1'], 'L1_gnn_g1w': _L1_gnn_in['g1w'], 'L1_gnn_g1b': _L1_gnn_in['g1b'], 'L1_gnn_g1a': _L1_gnn_in['g1a'], 'L1_gnn_W2': _L1_gnn_in['W2'], 'L1_gnn_b2': _L1_gnn_in['b2'], 'L1_gnn_g2w': _L1_gnn_in['g2w'], 'L1_gnn_g2b': _L1_gnn_in['g2b'], 'L1_gnn_g2a': _L1_gnn_in['g2a'], 'L1_gnn_W3': _L1_gnn_in['W3'], 'L1_gnn_b3': _L1_gnn_in['b3'], 'L1_gnn_g3w': _L1_gnn_in['g3w'], 'L1_gnn_g3b': _L1_gnn_in['g3b'], 'L1_gnn_g3a': _L1_gnn_in['g3a'], 'L1_gnn_W4': _L1_gnn_in['W4'], 'L1_gnn_b4': _L1_gnn_in['b4'], 'L1_gnn_g4w': _L1_gnn_in['g4w'], 'L1_gnn_g4b': _L1_gnn_in['g4b'], 'L1_gnn_g4a': _L1_gnn_in['g4a'], 'L1_gnn_W5': _L1_gnn_in['W5'], 'L1_gnn_b5': _L1_gnn_in['b5'], 'L1_gnn_g5w': _L1_gnn_in['g5w'], 'L1_gnn_g5b': _L1_gnn_in['g5b'], 'L1_gnn_g5a': _L1_gnn_in['g5a'], 'L2_gnn_W_fc': _L2_gnn_in['W_fc'], 'L2_gnn_W_attn': _L2_gnn_in['W_attn'], 'L2_gnn_W_encK': _L2_gnn_in['W_encK'], 'L2_gnn_b_encK': _L2_gnn_in['b_encK'], 'L2_gnn_W_p1': _L2_gnn_in['W_p1'], 'L2_gnn_b_p1': _L2_gnn_in['b_p1'], 'L2_gnn_W_p2': _L2_gnn_in['W_p2'], 'L2_gnn_b_p2': _L2_gnn_in['b_p2'], 'L2_gnn_K_w0': _L2_gnn_in['K_w0'], 'L2_gnn_K_b0': _L2_gnn_in['K_b0'], 'L2_gnn_K_w1': _L2_gnn_in['K_w1'], 'L2_gnn_K_b1': _L2_gnn_in['K_b1'], 'L2_gnn_K_w2': _L2_gnn_in['K_w2'], 'L2_gnn_K_b2': _L2_gnn_in['K_b2'], 'L2_gnn_U_w0': _L2_gnn_in['U_w0'], 'L2_gnn_U_b0': _L2_gnn_in['U_b0'], 'L2_gnn_U_w1': _L2_gnn_in['U_w1'], 'L2_gnn_U_b1': _L2_gnn_in['U_b1'], 'L2_gnn_U_w2': _L2_gnn_in['U_w2'], 'L2_gnn_U_b2': _L2_gnn_in['U_b2'], 'L2_gnn_D': _L2_gnn_in['D'], 'L3_gnn_W': _L3_gnn_in['W'], 'L3_gnn_b': _L3_gnn_in['b']}

def reference(x, src, dst, edge_weight, L0_gnn_Wq, L0_gnn_Wk, L0_gnn_Wv, L0_gnn_Wo, L1_gnn_W1, L1_gnn_b1, L1_gnn_g1w, L1_gnn_g1b, L1_gnn_g1a, L1_gnn_W2, L1_gnn_b2, L1_gnn_g2w, L1_gnn_g2b, L1_gnn_g2a, L1_gnn_W3, L1_gnn_b3, L1_gnn_g3w, L1_gnn_g3b, L1_gnn_g3a, L1_gnn_W4, L1_gnn_b4, L1_gnn_g4w, L1_gnn_g4b, L1_gnn_g4a, L1_gnn_W5, L1_gnn_b5, L1_gnn_g5w, L1_gnn_g5b, L1_gnn_g5a, L2_gnn_W_fc, L2_gnn_W_attn, L2_gnn_W_encK, L2_gnn_b_encK, L2_gnn_W_p1, L2_gnn_b_p1, L2_gnn_W_p2, L2_gnn_b_p2, L2_gnn_K_w0, L2_gnn_K_b0, L2_gnn_K_w1, L2_gnn_K_b1, L2_gnn_K_w2, L2_gnn_K_b2, L2_gnn_U_w0, L2_gnn_U_b0, L2_gnn_U_w1, L2_gnn_U_b1, L2_gnn_U_w2, L2_gnn_U_b2, L2_gnn_D, L3_gnn_W, L3_gnn_b):
    import jax
    import jax.numpy as jnp

    def _L0_gnn_ref(x, Wq, Wk, Wv, Wo, edge_index):
        import jax, jax.numpy as jnp
        import numpy as np
        N_NODES = 6250
        N_EDGES = 200000
        D_IN = 32
        N_HEADS = 4
        D_HEAD = 8
        N = x.shape[0]
        src, dst = (edge_index[0], edge_index[1])
        q = (x @ Wq).reshape(N, N_HEADS, D_HEAD)
        k = (x @ Wk).reshape(N, N_HEADS, D_HEAD)
        v = (x @ Wv).reshape(N, N_HEADS, D_HEAD)
        inv_sqrt_d = jnp.asarray(1.0 / np.sqrt(D_HEAD), dtype=x.dtype)
        scores = jnp.einsum('ehd,ehd->eh', q[dst], k[src]) * inv_sqrt_d
        m = jax.ops.segment_max(scores, dst, num_segments=N)
        m = jnp.where(jnp.isfinite(m), m, jnp.zeros_like(m))
        e = jnp.exp(scores - m[dst])
        denom = jax.ops.segment_sum(e, dst, num_segments=N)
        msg = jax.ops.segment_sum(e[:, :, None] * v[src], dst, num_segments=N)
        attn_out = msg / jnp.maximum(denom, 1e-16)[:, :, None]
        out = attn_out.reshape(N, N_HEADS * D_HEAD) @ Wo
        return x + out

    def _L1_gnn_ref(x, edge_index, edge_weight, batch, W1, b1, g1w, g1b, g1a, W2, b2, g2w, g2b, g2a, W3, b3, g3w, g3b, g3a, W4, b4, g4w, g4b, g4a, W5, b5, g5w, g5b, g5a):
        import jax, jax.numpy as jnp
        import numpy as np
        N = 6250
        E = 100000
        G = 64
        IN, H, OUT = (32, 64, 32)
        EPS = 1e-05

        def _gnn_forward(x, edge_index, edge_weight, batch, layers):
            n = x.shape[0]
            src, dst = (edge_index[0], edge_index[1])
            loop = jnp.arange(n)
            s = jnp.concatenate([src, loop])
            t = jnp.concatenate([dst, loop])
            w = jnp.concatenate([edge_weight, jnp.ones((n,), edge_weight.dtype)])
            deg = jax.ops.segment_sum(w, t, num_segments=n)
            dis = jnp.where(deg > 0, jax.lax.rsqrt(jnp.maximum(deg, 1e-12)), 0.0)
            coef = (dis[s] * w * dis[t])[:, None]
            counts = jnp.maximum(jax.ops.segment_sum(jnp.ones((n,), x.dtype), batch, num_segments=G), 1.0)[:, None]

            def gcn(h, W, b):
                h = h @ W
                return jax.ops.segment_sum(h[s] * coef, t, num_segments=n) + b

            def gnorm(h, gw, gb, ga):
                mean = jax.ops.segment_sum(h, batch, num_segments=G) / counts
                hc = h - ga * mean[batch]
                var = jax.ops.segment_sum(hc * hc, batch, num_segments=G) / counts
                return gw * hc * jax.lax.rsqrt(var[batch] + EPS) + gb
            n_layers = len(layers)
            for i, (W, b, gw, gb, ga) in enumerate(layers):
                x = gnorm(gcn(x, W, b), gw, gb, ga)
                if i < n_layers - 1:
                    x = jax.nn.relu(x)
            return x
        layers = [(W1, b1, g1w, g1b, g1a), (W2, b2, g2w, g2b, g2a), (W3, b3, g3w, g3b, g3a), (W4, b4, g4w, g4b, g4a), (W5, b5, g5w, g5b, g5a)]
        return _gnn_forward(x, edge_index, edge_weight, batch, layers)

    def _L2_gnn_ref(x, src, dst, W_fc, W_attn, W_encK, b_encK, W_p1, b_p1, W_p2, b_p2, K_w0, K_b0, K_w1, K_b1, K_w2, K_b2, U_w0, U_b0, U_w1, U_b1, U_w2, U_b2, D):
        import jax, jax.numpy as jnp
        import numpy as np
        N, E, IN_DIM, HID, HOUT = (1250, 20000, 32, 64, 64)

        def _mlp3(h, w0, b0, w1, b1, w2, b2):
            h = jnp.tanh(h @ w0.T + b0)
            h = jax.nn.relu(h @ w1.T + b1)
            return h @ w2.T + b2
        n, d = x.shape

        def get_H(xx):
            z = xx @ W_fc.T
            e = jax.nn.sigmoid(jnp.concatenate([z[src], z[dst]], axis=-1) @ W_attn.T)
            emax = jax.ops.segment_max(e, dst, num_segments=n)
            w = jnp.exp(e - emax[dst])
            denom = jax.ops.segment_sum(w, dst, num_segments=n)
            h = jax.ops.segment_sum(w / denom[dst] * z[src], dst, num_segments=n)
            h1 = jax.ops.segment_sum((h @ W_encK.T + b_encK)[src], dst, num_segments=n)
            K = _mlp3(h1, K_w0, K_b0, K_w1, K_b1, K_w2, K_b2)
            ue = (h @ W_p1.T + b_p1)[src] + (h @ W_p2.T + b_p2)[dst]
            U = _mlp3(ue, U_w0, U_b0, U_w1, U_b1, U_w2, U_b2)
            E_new = jax.ops.segment_sum(K[src] * U, dst, num_segments=n)
            return jnp.sum(E_new)
        dHdx = jax.grad(get_H)(x)
        eye = jnp.eye(d, dtype=x.dtype)
        J = jnp.concatenate([eye[d // 2:], -eye[:d // 2]], axis=0)
        return dHdx @ J.T - dHdx @ D.T

    def _L3_gnn_ref(x, W, b, edge_src, edge_dst):
        import jax, jax.numpy as jnp
        import numpy as np
        N = 6250
        E = 100000
        F_IN = 32
        F_OUT = 32
        n = x.shape[0]
        msgs = x[edge_src]
        summed = jax.ops.segment_sum(msgs, edge_dst, num_segments=n)
        cnt = jax.ops.segment_sum(jnp.ones_like(edge_dst, dtype=x.dtype), edge_dst, num_segments=n)
        neigh_mean = summed / jnp.maximum(cnt, 1.0)[:, None]
        h = jnp.concatenate([x, neigh_mean], axis=1)
        return jax.nn.relu(h @ W + b)
    edge_index = jnp.stack([src, dst])
    batch0 = jnp.zeros((6250,), jnp.int32)
    h = jnp.maximum(_layernorm(x, axis=-1), 0.0)
    x = x + _L0_gnn_ref(h, L0_gnn_Wq, L0_gnn_Wk, L0_gnn_Wv, L0_gnn_Wo, edge_index)
    h = jnp.maximum(_layernorm(x, axis=-1), 0.0)
    x = x + _L1_gnn_ref(h, edge_index, edge_weight, batch0, L1_gnn_W1, L1_gnn_b1, L1_gnn_g1w, L1_gnn_g1b, L1_gnn_g1a, L1_gnn_W2, L1_gnn_b2, L1_gnn_g2w, L1_gnn_g2b, L1_gnn_g2a, L1_gnn_W3, L1_gnn_b3, L1_gnn_g3w, L1_gnn_g3b, L1_gnn_g3a, L1_gnn_W4, L1_gnn_b4, L1_gnn_g4w, L1_gnn_g4b, L1_gnn_g4a, L1_gnn_W5, L1_gnn_b5, L1_gnn_g5w, L1_gnn_g5b, L1_gnn_g5a)
    h = jnp.maximum(_layernorm(x, axis=-1), 0.0)
    x = x + _L2_gnn_ref(h, src, dst, L2_gnn_W_fc, L2_gnn_W_attn, L2_gnn_W_encK, L2_gnn_b_encK, L2_gnn_W_p1, L2_gnn_b_p1, L2_gnn_W_p2, L2_gnn_b_p2, L2_gnn_K_w0, L2_gnn_K_b0, L2_gnn_K_w1, L2_gnn_K_b1, L2_gnn_K_w2, L2_gnn_K_b2, L2_gnn_U_w0, L2_gnn_U_b0, L2_gnn_U_w1, L2_gnn_U_b1, L2_gnn_U_w2, L2_gnn_U_b2, L2_gnn_D)
    h = jnp.maximum(_layernorm(x, axis=-1), 0.0)
    x = x + _L3_gnn_ref(h, L3_gnn_W, L3_gnn_b, src, dst)
    return x

_drawn_inputs = setup_inputs


def setup_inputs(seed=0):
    import zlib

    import numpy as np

    out = dict(_drawn_inputs(seed))
    spreads = {'L1_gnn_b1': (0.0, 0.414),
     'L1_gnn_g1w': (1.0, 0.2),
     'L1_gnn_g1b': (0.0, 0.308),
     'L1_gnn_g1a': (1.0, 0.2),
     'L1_gnn_b2': (0.0, 0.411),
     'L1_gnn_g2w': (1.0, 0.2),
     'L1_gnn_g2b': (0.0, 0.334),
     'L1_gnn_g2a': (1.0, 0.2),
     'L1_gnn_b3': (0.0, 0.1),
     'L1_gnn_g3w': (1.0, 0.2),
     'L1_gnn_g3b': (0.0, 0.1),
     'L1_gnn_g3a': (1.0, 0.2),
     'L1_gnn_b4': (0.0, 0.1),
     'L1_gnn_g4w': (1.0, 0.2),
     'L1_gnn_g4b': (0.0, 0.1),
     'L1_gnn_g4a': (1.0, 0.2),
     'L1_gnn_b5': (0.0, 0.1),
     'L1_gnn_g5w': (1.0, 0.2),
     'L1_gnn_g5b': (0.0, 0.1),
     'L1_gnn_g5a': (1.0, 0.2)}
    factors = {'L2_gnn_b_p1': 5.522,
     'L2_gnn_b_p2': 3.861,
     'L2_gnn_K_b0': 8.0,
     'L2_gnn_K_b1': 4.854,
     'L2_gnn_K_b2': 3.903,
     'L3_gnn_W': 4.708,
     'L3_gnn_b': 23.387}
    for name, (base, spread) in spreads.items():
        noise = np.random.default_rng([zlib.crc32(name.encode()), seed]).standard_normal(out[name].shape)
        drawn = base * np.exp(spread * noise) if base else spread * noise
        out[name] = jnp.asarray(drawn.astype(out[name].dtype))
    for name, factor in factors.items():
        out[name] = (out[name] * factor).astype(out[name].dtype)
    return out
```

```python
from contextlib import ExitStack

import concourse.bass as bass
from concourse import mybir

F32, I32 = mybir.dt.float32, mybir.dt.int32
ALU, ACT, AX = mybir.AluOpType, mybir.ActivationFunctionType, mybir.AxisListType

P = 128
N = 6250
NT = 52
NR = P * NT
E = 106250
J = 832
EP = P * J
PAD = NR - 1
CJ = 32
IT = J // CJ // 2
ER = EP + 1 + NR
ZERO_ROW, SPARE_ROW = EP, EP + 1
HEADS, DH = 4, 8
BIG = 1.0e30
LO, HI = 64, NR // 64
EPS = 1e-5


def weight_plan():
    two = [(f"L1_W{i}", f"L1_gnn_W{i}", False, 64, 64) for i in (2, 3, 4)]
    sq = [("encK_T", "L2_gnn_W_encK", True), ("p1_T", "L2_gnn_W_p1", True), ("p2_T", "L2_gnn_W_p2", True),
          ("K0_T", "L2_gnn_K_w0", True), ("K1_T", "L2_gnn_K_w1", True), ("K2_T", "L2_gnn_K_w2", True),
          ("U0_T", "L2_gnn_U_w0", True), ("U1_T", "L2_gnn_U_w1", True), ("U2_T", "L2_gnn_U_w2", True),
          ("encK", "L2_gnn_W_encK", False), ("p1", "L2_gnn_W_p1", False), ("p2", "L2_gnn_W_p2", False),
          ("K0", "L2_gnn_K_w0", False), ("K1", "L2_gnn_K_w1", False), ("K2", "L2_gnn_K_w2", False),
          ("U0", "L2_gnn_U_w0", False), ("U1", "L2_gnn_U_w1", False), ("U2", "L2_gnn_U_w2", False)]
    return ([("kvq", ("L0_gnn_Wk", "L0_gnn_Wv", "L0_gnn_Wq"), False, 32, 96),
             ("Wo", "L0_gnn_Wo", False, 32, 32), ("L1_W1", "L1_gnn_W1", False, 32, 64)] + two
            + [("L1_W5", "L1_gnn_W5", False, 64, 32), ("fc_T", "L2_gnn_W_fc", True, 32, 64),
               ("fc", "L2_gnn_W_fc", False, 64, 32), ("D_T", "L2_gnn_D", True, 32, 32),
               ("L3_W", "L3_gnn_W", False, 64, 32)]
            + [(n, i, t, 64, 64) for n, i, t in sq])


def weight_places():
    at, out = 0, {}
    for name, _, _, rows, cols in weight_plan():
        width = (P // rows) * cols
        out[name] = (at, width)
        at += width
    return out, at


FOUR = ("L2_gnn_b", "L2_gnn_K_b", "L2_gnn_U_b")
VECTORS = ([f"L1_gnn_{v}{i}{w}" for i in range(1, 6) for v, w in (("b", ""), ("g", "w"), ("g", "b"), ("g", "a"))]
           + ["L2_gnn_W_attn", "L2_gnn_b_encK", "L2_gnn_b_p1", "L2_gnn_b_p2", "L2_gnn_K_b0", "L2_gnn_K_b1",
              "L2_gnn_K_b2", "L2_gnn_U_b0", "L2_gnn_U_b1", "L2_gnn_U_b2", "L3_gnn_b"])


def vector_places():
    at, out = 0, {}
    for name in VECTORS:
        size = 128 if name == "L2_gnn_W_attn" else 32 if (name.startswith("L1_gnn") and "5" in name) or name == "L3_gnn_b" else 64
        copies = 4 if name.startswith(FOUR) else 1
        out[name] = (at, size)
        at += size * copies
    return out, at


def build(nc, x_in, src_in, dst_in, w_in, weights_in, vectors_in, out):
    ctx = ExitStack()
    with ctx:
        WAT, WCOLS = weight_places()
        VAT, VCOLS = vector_places()

        class Semaphores(dict):
            def __missing__(self, name):
                self[name] = ctx.enter_context(nc.semaphore(name))
                return self[name]

        S = Semaphores()

        def sb(name, shape, dt=F32):
            return ctx.enter_context(nc.sbuf_tensor(name, shape, dt))

        def dram(name, shape, dt=F32):
            return nc.dram_tensor(name, shape, dt).ap()

        weights = sb("weights", [P, WCOLS])
        vectors = sb("vectors", [P, VCOLS])
        ident = sb("ident", [P, P])
        ones = sb("ones", [P, P])
        below = sb("below", [P, P])
        zeros = sb("zeros", [P, J])
        node_id = sb("node_id", [P, NT + 1])
        part_id = sb("part_id", [P, 1])
        valid = sb("valid", [P, NT])
        src_d = sb("src_d", [P, J], I32)
        dst_s = sb("dst_s", [P, J], I32)
        pos_s = sb("pos_s", [P, J], I32)
        w_d = sb("w_d", [P, J])
        score = sb("score", [P, J * HEADS])
        tanh_d, wexp_d = score[:, 0:J], score[:, J:2 * J]
        payload = score[:, :].bitcast(I32)
        arena = sb("arena", [P, 2 * (2 * 2048 + 2 * 4096 + 66 * CJ)])
        half = sb("half", [P, 1])
        digits = sb("digits", [P, P])

        at = [0]

        def take(n):
            at[0] += n
            return arena[:, at[0] - n:at[0]]

        G = [take(4096) for _ in range(2)]
        M = [take(4096) for _ in range(2)]
        X = [take(66 * CJ) for _ in range(2)]
        H = [take(2048) for _ in range(2)]
        T = [take(2048) for _ in range(2)]
        SLOT = NT * 67
        NODE = [arena[:, i * SLOT:(i + 1) * SLOT] for i in range(8)]
        key = H[1][:, 0:J]

        class Order:
            def __init__(self, k, n):
                self.k, self.n = k, n
                self.key = key
                self.same = sb(f"same_{k}", [P, J])
                self.ends = sb(f"ends_{k}", [P, 8])
                self.equal = sb(f"equal_{k}", [P, P])
                self.all_equal = sb(f"all_equal_{k}", [P, P])
                self.last_row = sb(f"last_row_{k}", [P, P])
                self.join = sb(f"join_{k}", [P, 1], I32)
                self.first = sb(f"first_{k}", [P, 1], I32)
                self.last = sb(f"last_{k}", [P, 1], I32)
                self.end = sb(f"end_{k}", [P, NT], I32)
                self.start = sb(f"start_{k}", [P, NT], I32)
                self.count = sb(f"count_{k}", [P, NT])
                self.upto = sb(f"upto_{k}", [P, NT + 1])
                self.part = sb(f"part_{k}", [P, NT + 1])
                self.part_i = sb(f"part_i_{k}", [P, NT + 1], I32)
                self.keys = dram(f"keys_{k}", (P, J))
                self.upto_rows = dram(f"upto_rows_{k}", (NR, 1))

        OD, OS = Order("d", 1), Order("s", 0)
        idx = [sb(f"idx{b}", [P, CJ], I32) for b in range(2)]
        mask = [sb(f"mask{b}", [P, CJ]) for b in range(2)]
        side = [sb(f"side{b}", [P, CJ * 8]) for b in range(2)]
        narrow = [sb(f"narrow{b}", [P, CJ * 4]) for b in range(2)]
        carry = sb("carry", [P, P])
        spread_carry = sb("spread_carry", [P, P])
        joined = sb("joined", [P, P])
        small = sb("small", [P, 16 * NT])
        spread_carry2 = sb("spread_carry2", [P, 66])
        sums = sb("sums", [P, 8 * 64])
        packT = [sb(f"packT{b}", [P, 256]) for b in range(2)]
        packB = [sb(f"packB{b}", [P, 256]) for b in range(2)]
        dis = sb("dis", [P, NT])
        rden = sb("rden", [P, NT])

        psT = [ctx.enter_context(nc.psum_tensor(f"psT{b}", [P, 512], F32)) for b in range(2)]
        psO = [ctx.enter_context(nc.psum_tensor(f"psO{b}", [P, 512], F32)) for b in range(2)]
        psB = [ctx.enter_context(nc.psum_tensor(f"psB{b}", [P, 512], F32)) for b in range(2)]
        psD = [ctx.enter_context(nc.psum_tensor(f"psD{b}", [P, 512], F32)) for b in range(2)]

        def rows(buf, f, n=CJ):
            return buf[:, 0:n * f].rearrange("p (j f) -> p j f", f=f)

        def nodes(i, f, off=0):
            return NODE[i][:, off:off + NT * f].rearrange("p (t f) -> p t f", f=f)

        def scalars(i):
            return small[:, i * NT:(i + 1) * NT]

        def over(col, f):
            return col.unsqueeze(2).broadcast_to([P, col.shape[1], f])

        def vec(name, n=NT, off=0, size=None):
            a, s = VAT[name]
            s = size or s
            return vectors[:, a + off:a + off + s].unsqueeze(1).broadcast_to([P, n, s])

        def edge_table(name, f):
            return dram(name, (ER, f))

        R = {f: dram(f"runs{f}", (EP + 1 + P, f)) for f in (1, 5, 32, 36, 64, 65, 128)}
        XQ, XM, XA, XA2, XF, XS = (edge_table(n, f) for n, f in
                                   (("xq", 32), ("xm", 4), ("xa", 1), ("xa2", 64), ("xf", 66), ("xs", 65)))
        KV, ZA, UD = dram("kv_rows", (EP, 64)), dram("za_rows", (EP, 65)), dram("ud_rows", (EP, 128))
        TB = {n: dram("t_" + n, (NR, f)) for n, f in
              (("kv", 64), ("q", 32), ("m", 4), ("za", 65), ("ad", 1), ("h", 64),
               ("ka", 128), ("a2", 64), ("k0", 64), ("k1", 64), ("dh1", 64), ("dp", 64), ("dst", 67), ("f", 66),
               ("res0", 32), ("res1", 32), ("res2", 32), ("res3", 32), ("hin", 32), ("w2", 64), ("gs", 65),
               ("gcn1", 32), ("gcn2", 64), ("gcn3", 64), ("gcn4", 64), ("gcn5", 32))}
        SPREADS = [(XQ, 32), (XM, 4), (XA, 1), (XA2, 64), (XF, 66), (XS, 65)]
        FILLS = len(SPREADS) + 2 * len(R) - 6
        UG = CJ // 4
        SORT = [dram(f"sorted{i}", (EP, 4), I32) for i in range(2)]

        def by_edge(t, f):
            return t[0:EP, :].rearrange("(p j) f -> p j f", j=J)

        def by_node(t):
            return t.rearrange("(p t) f -> p (t f)", t=NT)

        def chunk(t, f, it, b):
            return by_edge(t, f)[:, bass.ds(it * (2 * CJ) + b * CJ, CJ), :]

        def cols(t, it, b, f=1):
            return t[:, bass.ds(it * (2 * CJ * f) + b * CJ * f, CJ * f)]

        PASSES = [("scores", 1, 1), ("soft", 2, 1), ("gcn1", 0, 1), ("gcn2", 0, 1), ("gcn3", 0, 1), ("gcn4", 0, 1),
                  ("gcn5", 0, 1), ("attend", 1, 1), ("hsum", 0, 1), ("umlp", 1, 2), ("upair", 0, 1), ("dh1", 0, 1),
                  ("grad", 1, 1), ("back", 2, 1), ("mean", 0, 1)]
        TURN = {n: k for k, (n, _, _) in enumerate(PASSES)}
        FREE = {n: TURN[n] * (IT + 1) for n in TURN}
        SCANNED = {n: TURN[n] * 2 * IT for n in TURN}
        LOADED = {n: 16 * IT * sum(a for _, a, _ in PASSES[:TURN[n]]) for n in TURN}
        CREDIT = 16
        STORED = {n: CREDIT + 16 * IT * sum(a for _, _, a in PASSES[:TURN[n]]) for n in TURN}

        LOADS = ["x", "res0", "gcn1", "gcn2", "gcn3", "gcn4", "gcn5", "res1", "k1", "k0", "dpd", "dhu", "h", "za",
                 "gs", "res2", "hin", "res3"]
        GATHERS = ["scores", "gcn1", "gcn2", "gcn3", "gcn4", "gcn5", "attend", "hsum", "umlp", "upair", "dh1", "grad", "mean"]
        ROWS = {n: (k // 4, k % 4 * 16 * CJ * IT) for k, n in enumerate(GATHERS)}

        PRODUCTS = [("kvq", 32), ("Wo", 32), ("L1_W1", 32), ("L1_W2", 64), ("L1_W3", 64), ("L1_W4", 64),
                    ("L1_W5", 64), ("fc_T", 32), ("h_p1", 64), ("A1", 64), ("h_p2", 64), ("A2", 64),
                    ("enc", 64), ("K_0", 64), ("K_1", 64), ("K_2", 64), ("KW", 64),
                    ("b_U2", 64), ("b_K2", 64), ("b_K1", 64), ("b_K0", 64), ("b_U0s", 64), ("b_p1", 64),
                    ("b_U0d", 64), ("b_p2", 64), ("b_enc", 64), ("b_fc", 64), ("b_D", 32), ("L3", 64)]
        ORDINAL = {n: k for k, (n, _) in enumerate(PRODUCTS)}
        FIRST, total = {}, 0
        for name, rows_in in PRODUCTS:
            FIRST[name] = total
            total += NT // (P // rows_in)

        def groups(name):
            return NT // (P // dict(PRODUCTS)[name])

        def product_pe(pe, name, weight, source, bias=None):
            k = FIRST[name]
            a, width = WAT[weight]
            pe.wait_ge(S["product_in"], ORDINAL[name] + 1)
            n = groups(name)
            for g in range(n + 1):
                if g < n:
                    if k + g >= 2:
                        pe.wait_ge(S["turned_copied"], k + g - 1)
                    pe.transpose(psT[(k + g) % 2][:, 0:P], source[:, g * P:(g + 1) * P], ident[:]).then_inc(S["turned"], 1)
                if g >= 1:
                    h = k + g - 1
                    pe.wait_ge(S["turned_copied"], h + 1)
                    if h >= 2:
                        pe.wait_ge(S["product_taken"], h - 1)
                    last = pe.matmul(psO[h % 2][:, 0:width], packT[h % 2][:, 0:P], weights[:, a:a + width],
                                     start=True, stop=bias is None)
                    if bias is not None:
                        v, _ = VAT[bias]
                        last = pe.matmul(psO[h % 2][:, 0:width], ones[0:1, :], vectors[0:1, v:v + width],
                                         start=False, stop=True)
                    last.then_inc(S["product"], 1)

        def product_act(act, name):
            k = FIRST[name]
            for g in range(groups(name)):
                act.wait_ge(S["turned"], k + g + 1)
                if k + g >= 2:
                    act.wait_ge(S["product"], k + g - 1)
                act.copy(packT[(k + g) % 2][:, 0:P], psT[(k + g) % 2][:, 0:P]).then_inc(S["turned_copied"], 1)

        def product_dve(dve, name, take_out, cols_out):
            k, n = FIRST[name], P // dict(PRODUCTS)[name]
            for g in range(groups(name)):
                dve.wait_ge(S["product"], k + g + 1)
                ps = psO[(k + g) % 2][:, 0:n * cols_out].rearrange("p (t f) -> p t f", f=cols_out)
                take_out(slice(g * n, (g + 1) * n), ps).then_inc(S["product_taken"], 1)

        def plain(dst):
            return lambda t, ps: nc.vector.tensor_copy(dst[:, t, :], ps)

        def relu_to(dst):
            return lambda t, ps: nc.vector.tensor_scalar(dst[:, t, :], ps, 0.0, None, ALU.max)

        def order_dve(dve, o):
            n = o.n
            dve.wait_ge(S["ends_read"], 16 * 3 * (n + 1))
            dve.tensor_tensor(o.same[:, 1:J], o.key[:, 1:J], o.key[:, 0:J - 1], ALU.is_equal)
            dve.tensor_tensor(o.same[:, 0:1], o.key[:, 0:1], o.ends[:, 0:1], ALU.is_equal)
            dve.tensor_copy(o.first[:], o.key[:, 0:1])
            dve.tensor_copy(o.last[:], o.key[:, J - 1:J])
            dve.tensor_tensor(o.ends[:, 3:4], o.key[:, J - 1:J], o.ends[:, 1:2], ALU.is_equal)
            dve.tensor_tensor(o.ends[:, 4:5], o.key[:, J - 1:J], o.ends[:, 2:3], ALU.not_equal)
            dve.tensor_scalar(joined[:], ident[:], o.key[:, J - 1:J], None, ALU.mult).then_inc(S["order_diag"], 1)
            dve.wait_ge(S["order_last_row"], n + 1)
            dve.tensor_copy(o.last_row[:], psB[0][:, 0:P])
            dve.drain()
            dve.tensor_scalar(o.all_equal[:], o.last_row[:], o.key[:, J - 1:J], None, ALU.is_equal)
            dve.tensor_scalar(o.equal[:], o.last_row[:], o.key[:, J - 1:J], o.ends[:, 3:4], ALU.is_equal, ALU.mult)
            dve.tensor_tensor(o.ends[:, 4:5], o.ends[:, 4:5], o.ends[:, 3:4], ALU.mult)
            for t in range(NT + 1):
                dve.tensor_scalar(carry[:], o.last_row[:], node_id[:, t:t + 1], 0.0, ALU.is_le, ALU.add,
                                  accum_out=o.part[:, t:t + 1])
                dve.drain()
            dve.tensor_scalar(o.part[:], o.part[:], float(P - 1), None, ALU.min)
            dve.drain()
            dve.tensor_copy(o.part_i[:], o.part[:]).then_inc(S["order_part"], 1)
            for t in range(NT + 1):
                dve.wait_ge(S[f"search{t % 4}"], 16 * (t // 4 + 1 + n * len(range(t % 4, NT + 1, 4))))
                dve.tensor_scalar(T[0][:, 0:J], NODE[0][:, (t % 4) * J:(t % 4 + 1) * J], node_id[:, t:t + 1], 0.0,
                                  ALU.is_le, ALU.add, accum_out=o.upto[:, t:t + 1]).then_inc(S["searched"], 1)
                dve.drain()
            dve.scalar_tensor_tensor(o.upto[:], o.part[:], float(J), o.upto[:], ALU.mult, ALU.add)
            dve.drain()
            dve.tensor_tensor(o.count[:], o.upto[:, 1:], o.upto[:, 0:NT], ALU.subtract).then_inc(S["order_upto"], 1)
            dve.drain()
            has, a, b = scalars(0), scalars(1), scalars(2)
            spare, spares = scalars(3)[:, 0:1], scalars(4)
            dve.tensor_scalar(has, o.count[:], 0.0, None, ALU.is_gt)
            dve.tensor_scalar(spare, part_id[:], float(SPARE_ROW), None, ALU.add)
            dve.drain()
            dve.tensor_scalar(a, o.upto[:, 1:], float(-1 - ZERO_ROW), None, ALU.add)
            dve.tensor_scalar(spares, node_id[:, 1:], float(SPARE_ROW), None, ALU.add)
            dve.drain()
            dve.tensor_tensor(b, o.upto[:, 0:NT], spares, ALU.subtract)
            dve.drain()
            dve.tensor_tensor(a, a, has, ALU.mult)
            dve.tensor_tensor(b, b, has, ALU.mult)
            dve.drain()
            dve.tensor_scalar(o.end[:], a, float(ZERO_ROW), None, ALU.add)
            dve.tensor_tensor(o.start[:], b, spares, ALU.add)
            dve.wait_ge(S["order_join_end"], 16 * (n + 1))
            dve.tensor_scalar(o.ends[:, 5:6], o.ends[:, 6:7], -1.0, spare, ALU.add, ALU.subtract)
            dve.drain()
            dve.tensor_tensor(o.ends[:, 5:6], o.ends[:, 5:6], o.ends[:, 4:5], ALU.mult)
            dve.drain()
            dve.tensor_scalar(o.join[:], o.ends[:, 5:6], spare, None, ALU.add).then_inc(S["order_built"], 1)
            dve.drain()

        def order_sp(sp, o):
            n = o.n
            sp.wait_ge(S["order_key"], n + 1)
            sp.dma_start(o.keys, o.key[:]).then_inc(S["order_keys"], 16)
            sp.wait_ge(S["order_keys"], 16 * (n + 1))
            sp.dma_start(o.ends[1:P, 0:1], o.keys[0:P - 1, J - 1:J], allow_slow_non_contiguous=True).then_inc(S["ends_read"], 16)
            sp.dma_start(o.ends[0:P - 1, 1:2], o.keys[1:P, 0:1], allow_slow_non_contiguous=True).then_inc(S["ends_read"], 16)
            sp.dma_start(o.ends[0:P - 1, 2:3], o.keys[1:P, J - 1:J], allow_slow_non_contiguous=True).then_inc(S["ends_read"], 16)
            sp.wait_ge(S["order_upto"], n + 1)
            sp.dma_start(by_node(o.upto_rows), o.upto[:, 1:]).then_inc(S["order_upto_rows"], 16)

        def order_pe(pe, o):
            n = o.n
            pe.wait_ge(S["order_diag"], n + 1)
            pe.matmul(psB[0][:, 0:P], ones[:], joined[:], start=True, stop=True).then_inc(S["order_last_row"], 1)

        def order_pool(pool, o):
            n = o.n
            pool.wait_ge(S["order_keys"], 16 * (n + 1))
            pool.wait_ge(S["order_part"], n + 1)
            for t in range(NT + 1):
                if t >= 4:
                    pool.wait_ge(S["searched"], t - 3 + n * (NT + 1))
                fetch(pool, NODE[0][:, (t % 4) * J:(t % 4 + 1) * J], o.keys, o.part_i[:, t:t + 1]).then_inc(S[f"search{t % 4}"], 16)
            pool.wait_ge(S["order_upto_rows"], 16 * (n + 1))
            fetch(pool, o.ends[:, 6:7], o.upto_rows, o.last[:]).then_inc(S["order_join_end"], 16)
            pool.wait_ge(S["order_built"], n + 1)

        def fetch(pool, dst, table, index):
            return pool.indirect_dma_start(dst, None, table, bass.IndirectOffsetOnAxis(ap=index, axis=0))

        def put(pool, table, index, source):
            return pool.indirect_dma_start(table, bass.IndirectOffsetOnAxis(ap=index, axis=0), source, None)

        def gather_pool(pool, name, table, f, rows_of, saved=False):
            with pool.Fori(0, IT) as it:
                for b in range(2):
                    pool.wait_ge(S[f"free{b}"], it + (FREE[name] + 1))
                    if saved:
                        pool.wait_ge(S[f"{name}_saved{b}"], it * 16 + CREDIT)
                    pool.tensor_copy(idx[b][:], cols(rows_of, it, b))
                    pool.drain()
                    for j in range(CJ):
                        fetch(pool, G[b][:, j * f:(j + 1) * f], table, idx[b][:, j:j + 1]).then_inc(S[f"rows{ROWS[name][0]}{b}"], 16)

        def load_sp(sp, name, loads):
            with sp.Fori(0, IT) as it:
                for b in range(2):
                    sp.wait_ge(S[f"free{b}"], it + (FREE[name] + 1))
                    for table, f, buf in loads:
                        sp.dma_start(rows(buf[b], f), chunk(table, f, it, b)).then_inc(S[f"loaded{b}"], 16)

        def store_chunk(q, name, it, b, stores):
            q.wait_ge(S["scanned"], it * 2 + (SCANNED[name] + b + 1))
            for table, f, buf in stores:
                q.dma_start(chunk(table, f, it, b), rows(buf[b], f)).then_inc(S[f"stored{b}"], 16)

        def store_act(act, name, stores):
            with act.Fori(0, IT) as it:
                for b in range(2):
                    store_chunk(act, name, it, b, stores)

        def scan_rows(dve, dst, source, f0, f1, b, kept, maxima=0):
            for f in range(f0, f1):
                top = f < maxima
                last = dve.tensor_tensor_scan(dst[:, :, f], narrow[b][:, 0:CJ] if top else mask[b][:], source[:, :, f],
                                              kept[:, f:f + 1], ALU.add if top else ALU.mult, ALU.max if top else ALU.add)
            return last

        def keep_last(dve, dst, f, kept):
            dve.drain()
            return dve.tensor_copy(kept[:, 0:f], dst[:, CJ - 1, 0:f])

        def begin(dve, name, kept, kept_from=-BIG, maxima=0):
            dve.drain()
            dve.memset(kept, 0.0)
            if maxima:
                dve.drain()
                dve.memset(kept[:, 0:maxima], kept_from)
            for b in range(2):
                dve.sem_inc(S[f"free{b}"], 1)

        def take_mask(dve, o, it, b, maxima=False):
            dve.tensor_copy(mask[b][:], cols(o.same, it, b))
            if maxima:
                dve.tensor_scalar(narrow[b][:, 0:CJ], cols(o.same, it, b), BIG, -BIG, ALU.mult, ALU.add)

        def plain_pass_dve(dve, name, o, f, weighted=False):
            begin(dve, name, carry[:, 0:f])
            dve.drain()
            with dve.Fori(0, IT) as it:
                for b in range(2):
                    take_mask(dve, o, it, b)
                    g, m = rows(G[b], f), rows(M[b], f)
                    if weighted:
                        dve.tensor_copy(side[b][:, 0:CJ], cols(w_d, it, b))
                    dve.drain()
                    dve.wait_ge(S[f"rows{ROWS[name][0]}{b}"], it * (16 * CJ) + (ROWS[name][1] + 16 * CJ))
                    dve.wait_ge(S[f"stored{b}"], it * 16 + STORED[name])
                    if weighted:
                        dve.tensor_tensor(m, g, over(side[b][:, 0:CJ], f), ALU.mult).then_inc(S[f"free{b}"], 1)
                        dve.drain()
                        scan_rows(dve, m, m, 0, f, b, carry)
                    else:
                        scan_rows(dve, m, g, 0, f, b, carry).then_inc(S[f"free{b}"], 1)
                    keep_last(dve, m, f, carry).then_inc(S["scanned"], 1)
                    dve.drain()

        def ends_dve(dve, name, o, f, stores=1, maxima=0):
            for b in range(2):
                dve.wait_ge(S[f"stored{b}"], STORED[name] + 16 * IT * stores)
            if maxima:
                for h in range(maxima):
                    dve.tensor_scalar(T[0][:, h * P:(h + 1) * P], ident[:], carry[:, h:h + 1], None, ALU.mult)
                dve.tensor_scalar(T[1][:, 0:P], o.all_equal[:], BIG, -BIG, ALU.mult, ALU.add)
                dve.drain()
            dve.sem_inc(S["carried"], 1)
            dve.wait_ge(S["crossed"], TURN[name] + 1)
            dve.wait_ge(S["join_read"], 16 * (TURN[name] + 1))
            if maxima:
                for h in range(maxima):
                    dve.tensor_tensor(T[0][:, h * P:(h + 1) * P], psB[0][:, h * P:(h + 1) * P], T[1][:, 0:P], ALU.add)
                dve.drain()
                dve.tensor_reduce(sums[:, 0:maxima], T[0][:, 0:maxima * P].rearrange("p (h q) -> p h q", h=maxima),
                                  AX.X, ALU.max)
                dve.drain()
                dve.tensor_tensor(joined[:, 0:maxima], joined[:, 0:maxima], sums[:, 0:maxima], ALU.max)
            dve.tensor_tensor(joined[:, maxima:f], joined[:, maxima:f], psB[1][:, maxima:f], ALU.add)
            dve.drain()
            dve.sem_inc(S["join"], 1)
            dve.wait_ge(S["ends"], 16 * NT * (TURN[name] + 1))

        def ends_pe(pe, name, o, f, maxima=0):
            pe.wait_ge(S["carried"], TURN[name] + 1)
            if maxima:
                pe.matmul(psB[0][:, 0:maxima * P], ones[:], T[0][:, 0:maxima * P], start=True, stop=True)
            pe.matmul(psB[1][:, 0:f], o.equal[:], carry[:, 0:f], start=True, stop=True).then_inc(S["crossed"], 1)

        def ends_pool(pool, name, o, f, slot=0):
            pool.wait_ge(S["carried"], TURN[name] + 1)
            fetch(pool, joined[:, 0:f], R[f], o.join[:]).then_inc(S["join_read"], 16)
            pool.wait_ge(S["join"], TURN[name] + 1)
            put(pool, R[f], o.join[:], joined[:, 0:f]).then_inc(S["joined"], 16)
            pool.wait_ge(S["joined"], 16 * (TURN[name] + 1))
            for t in range(NT):
                fetch(pool, arena[:, slot * SLOT + t * f:slot * SLOT + (t + 1) * f], R[f], o.end[:, t:t + 1]).then_inc(S["ends"], 16)

        def spread_pool(pool, name, o, f, source, xtable):
            for t in range(NT):
                put(pool, xtable, o.start[:, t:t + 1], source[:, t * f:(t + 1) * f]).then_inc(S[f"{name}_spread"], 16)

        def spread_first_pool(pool, name, o, f, table, kept):
            fetch(pool, kept[:, 0:f], table, o.first[:]).then_inc(S[f"{name}_first"], 16)

        pay = payload.rearrange("p (j f) -> p j f", f=4)
        digit, hits = T[1][:, 0:J], T[0][:, 0:J]
        hit_i, running = H[1][:, 0:J].bitcast(I32), M[0][:, 0:J]
        rank, rank_i = H[0][:, 0:J], G[0][:, 0:J].bitcast(I32)
        digit_i = G[1][:, 0:J].bitcast(I32)
        all_ones = X[0][:, 0:J]

        def sort_dve(dve, n, values):
            if n == 0:
                dve.wait_ge(S["edges"], 16 * 3)
                dve.wait_ge(S["places"], 1)
                dve.tensor_copy(pay[:, :, 0], src_d[:])
                dve.tensor_copy(pay[:, :, 1], H[0][:, 0:J].bitcast(I32))
                dve.tensor_copy(pay[:, :, 2], M[1][:, 0:J].bitcast(I32))
                dve.memset(pay[:, :, 3], 0)
                dve.memset(all_ones, 1.0)
                dve.drain()
                dve.tensor_scalar(digit_i, pay[:, :, 0], LO - 1, None, ALU.bitwise_and)
            else:
                dve.wait_ge(S["reloaded"], 16)
                dve.tensor_scalar(digit_i, pay[:, :, 0], LO.bit_length() - 1, None, ALU.arith_shift_right)
            dve.drain()
            dve.tensor_copy(digit, digit_i)
            dve.drain()
            with dve.Fori(0, values) as d:
                dve.tensor_scalar(hits, digit, digits[:, bass.ds(d, 1)], 0.0, ALU.is_equal, ALU.add,
                                  accum_out=carry[:, bass.ds(d, 1)])
                dve.drain()
            dve.sem_inc(S["counted"], 1)
            dve.wait_ge(S["summed"], n + 1)
            tot, run = joined[:, 0:values], sums[:, 0:values]
            dve.tensor_copy(tot, psB[1][:, 0:values])
            dve.drain()
            dve.tensor_tensor_scan(run, ones[:, 0:values], tot, 0.0, ALU.mult, ALU.add)
            dve.drain()
            dve.tensor_tensor(run, run, tot, ALU.subtract)
            dve.drain()
            dve.tensor_tensor(run, run, psB[0][:, 0:values], ALU.add)
            dve.drain()
            with dve.Fori(0, values) as d:
                dve.tensor_scalar(hit_i, digit, digits[:, bass.ds(d, 1)], None, ALU.is_equal)
                dve.drain()
                dve.tensor_tensor_scan(running, all_ones, hit_i, sums[:, bass.ds(d, 1)], ALU.mult, ALU.add)
                dve.drain()
                dve.copy_predicated(rank, hit_i, running)
                dve.drain()
            dve.tensor_scalar(rank_i, rank, -1.0, None, ALU.add)
            dve.drain()
            dve.sem_inc(S["ranked"], 1)

        def sort_pe(pe, n, values):
            pe.wait_ge(S["counted"], n + 1)
            pe.matmul(psB[0][:, 0:values], below[:], carry[:, 0:values], start=True, stop=True)
            pe.matmul(psB[1][:, 0:values], ones[:], carry[:, 0:values], start=True, stop=True).then_inc(S["summed"], 1)

        def sort_pool(pool, n):
            pool.wait_ge(S["ranked"], n + 1)
            with pool.Fori(0, IT) as it:
                for b in range(2):
                    pool.tensor_copy(idx[b][:], cols(rank_i, it, b))
                    pool.tensor_copy(side[b][:, 0:4 * CJ].bitcast(I32), cols(payload, it, b, 4))
                    pool.drain()
                    for j in range(CJ):
                        put(pool, SORT[n], idx[b][:, j:j + 1], side[b][:, 4 * j:4 * j + 4].bitcast(I32))\
                            .then_inc(S[f"scattered{n}{b}"], 16)
                for b in range(2):
                    pool.wait_ge(S[f"scattered{n}{b}"], it * (16 * CJ) + 16 * CJ)

        def sort_sp(sp, n):
            for b in range(2):
                sp.wait_ge(S[f"scattered{n}{b}"], 16 * CJ * IT)
            sp.dma_start(payload, SORT[n].rearrange("(p j) f -> p (j f)", j=J)).then_inc(S["reloaded"], 16)

        def norm_relu(dve, n, dst, src, tmp):
            s0, s1, s2 = scalars(0), scalars(1), scalars(2)
            dve.tensor_reduce(s0, src, AX.X, ALU.add)
            dve.drain()
            dve.tensor_scalar(s0, s0, 1.0 / 32, None, ALU.mult)
            dve.drain()
            dve.tensor_tensor(dst, src, over(s0, 32), ALU.subtract)
            dve.drain()
            dve.tensor_tensor(tmp, dst, dst, ALU.mult)
            dve.drain()
            dve.tensor_reduce(s1, tmp, AX.X, ALU.add)
            dve.drain()
            dve.tensor_scalar(s1, s1, 1.0 / 32, EPS, ALU.mult, ALU.add).then_inc(S["variance"], 1)
            dve.wait_ge(S["deviation"], n)
            dve.reciprocal(s2, s2)
            dve.drain()
            dve.tensor_tensor(dst, dst, over(s2, 32), ALU.mult)
            dve.drain()
            dve.tensor_scalar(dst, dst, 0.0, None, ALU.max)
            dve.drain()

        def deviation_act(act, n):
            act.wait_ge(S["variance"], n)
            act.activation(scalars(2), scalars(1), ACT.Sqrt).then_inc(S["deviation"], 1)

        def graph_norm(dve, layer, v, f, tmp):
            i = f"{layer}"
            col = lambda k: sums[:, k * 64:k * 64 + f]
            row = lambda k: col(k).unsqueeze(1).broadcast_to([P, NT, f])
            by_feature = lambda a: a.rearrange("p t f -> p f t")
            dve.tensor_tensor(v, v, vec(f"L1_gnn_b{i}"), ALU.add)
            dve.drain()
            dve.tensor_tensor(tmp, v, over(valid[:], f), ALU.mult)
            dve.drain()
            dve.tensor_reduce(col(0), by_feature(tmp), AX.X, ALU.add).then_inc(S["part_sum"], 1)
            dve.wait_ge(S["node_sum"], 2 * layer - 1)
            a, _ = VAT[f"L1_gnn_g{i}a"]
            w, _ = VAT[f"L1_gnn_g{i}w"]
            dve.scalar_tensor_tensor(col(1), psD[0][:, 0:f], 1.0 / N, vectors[:, a:a + f], ALU.mult, ALU.mult)
            dve.drain()
            dve.tensor_tensor(v, v, row(1), ALU.subtract)
            dve.drain()
            dve.tensor_tensor(tmp, v, over(valid[:], f), ALU.mult)
            dve.drain()
            dve.tensor_tensor(tmp, tmp, tmp, ALU.mult)
            dve.drain()
            dve.tensor_reduce(col(0), by_feature(tmp), AX.X, ALU.add).then_inc(S["part_sum"], 1)
            dve.wait_ge(S["node_sum"], 2 * layer)
            dve.tensor_scalar(col(2), psD[0][:, 0:f], 1.0 / N, EPS, ALU.mult, ALU.add).then_inc(S["graph_var"], 1)
            dve.wait_ge(S["graph_std"], layer)
            dve.reciprocal(col(3), col(3))
            dve.drain()
            dve.tensor_tensor(col(3), col(3), vectors[:, w:w + f], ALU.mult)
            dve.drain()
            dve.tensor_tensor(v, v, row(3), ALU.mult)
            dve.drain()
            dve.tensor_tensor(v, v, vec(f"L1_gnn_g{i}b"), ALU.add)
            dve.drain()

        def graph_norm_pe(pe, layer, f):
            for k in (2 * layer - 1, 2 * layer):
                pe.wait_ge(S["part_sum"], k)
                pe.matmul(psD[0][:, 0:f], ones[:], sums[:, 0:f], start=True, stop=True).then_inc(S["node_sum"], 1)

        def graph_norm_act(act, layer, f):
            act.wait_ge(S["graph_var"], layer)
            act.activation(sums[:, 192:192 + f], sums[:, 128:128 + f], ACT.Sqrt).then_inc(S["graph_std"], 1)

        def ready(dve, name):
            dve.drain()
            dve.sem_inc(S[name], 1)

        def flat(i, f):
            return NODE[i][:, 0:NT * f]

        def store_node(sp, name, table, i, f, nth=1):
            sp.wait_ge(S[f"{name}_made"], nth)
            sp.dma_start(by_node(table), flat(i, f)).then_inc(S[f"{name}_kept"], 16)

        def load_node(sp, name, table, i, f, kept, nth=1):
            sp.wait_ge(S[kept], 16 * nth)
            sp.wait_ge(S["room"], LOADS.index(name) + 1)
            sp.dma_start(flat(i, f), by_node(table)).then_inc(S["back"], 16)

        def fetch_back(dve, name):
            ready(dve, "room")
            dve.wait_ge(S["back"], 16 * (LOADS.index(name) + 1))

        W_SRC = VAT["L2_gnn_W_attn"][0]

        block = ctx.enter_context(nc.Block())

        @block.vector
        def _(dve):
            dve.wait_ge(S["weights"], 32)
            dve.memset(ones[:], 1.0)
            dve.memset(zeros[:], 0.0)
            dve.memset(half[:], 0.5)
            for o in (OD, OS):
                dve.memset(o.ends[:], -1.0)
            dve.wait_ge(S["iotas"], 1)
            dve.tensor_scalar(valid[:], node_id[:, 1:], float(N), None, ALU.is_lt)
            dve.tensor_scalar(below[:], digits[:], part_id[:], None, ALU.is_gt)
            dve.tensor_scalar(ident[:], digits[:], part_id[:], None, ALU.is_equal)
            ready(dve, "zeros")
            sort_dve(dve, 0, LO)
            sort_dve(dve, 1, HI)
            dve.wait_ge(S["reloaded"], 32)
            dve.tensor_copy(dst_s[:], pay[:, :, 1])
            dve.tensor_copy(pos_s[:], pay[:, :, 2])
            dve.tensor_copy(key, pay[:, :, 0])
            ready(dve, "order_key")
            order_dve(dve, OS)
            dve.wait_ge(S["dst_again"], 16)
            dve.tensor_copy(key, T[1][:, 0:J].bitcast(I32))
            ready(dve, "order_key")
            order_dve(dve, OD)

            fetch_back(dve, "x")
            x, h = nodes(0, 32), nodes(1, 32)
            norm_relu(dve, 1, h, x, nodes(2, 32))
            ready(dve, "product_in")
            kv, q = nodes(2, 64), nodes(3, 32)

            def split_kvq(t, ps):
                dve.tensor_copy(kv[:, t, :], ps[:, :, 0:64])
                return dve.tensor_copy(q[:, t, :], ps[:, :, 64:96])
            product_dve(dve, "kvq", split_kvq, 96)
            dve.tensor_tensor(x, x, h, ALU.add)
            ready(dve, "kv_made")
            ready(dve, "q_made")
            ready(dve, "res0_made")
            for name in ("kv_kept", "q_kept", "res0_kept"):
                dve.wait_ge(S[name], 16)
            dve.wait_ge(S["scores_spread"], 16 * NT)
            dve.wait_ge(S["scores_first"], 16)

            begin(dve, "scores", carry[:, 0:5], maxima=4)
            dve.drain()
            with dve.Fori(0, IT) as it:
                for b in range(2):
                    take_mask(dve, OD, it, b, maxima=True)
                    dve.drain()
                    dve.wait_ge(S[f"rows{ROWS["scores"][0]}{b}"], it * (16 * CJ) + (ROWS["scores"][1] + 16 * CJ))
                    dve.wait_ge(S[f"loaded{b}"], it * 16 + (LOADED["scores"] + 16))
                    dve.wait_ge(S[f"stored{b}"], it * 16 + STORED["scores"])
                    qe, g, m = rows(X[b], 32), rows(G[b], 64), rows(M[b], 5)
                    scan_rows(dve, qe, qe, 0, 32, b, spread_carry)
                    keep_last(dve, qe, 32, spread_carry)
                    dve.tensor_tensor(rows(H[b], 32), qe, g[:, :, 0:32], ALU.mult).then_inc(S[f"free{b}"], 1)
                    dve.drain()
                    dve.tensor_reduce(side[b][:, 0:CJ * HEADS],
                                      H[b][:, 0:CJ * 32].rearrange("p (n d) -> p n d", d=DH), AX.X, ALU.add)
                    dve.drain()
                    dve.tensor_scalar(side[b][:, 0:CJ * HEADS], side[b][:, 0:CJ * HEADS], float(DH ** -0.5), None, ALU.mult)
                    dve.drain()
                    dve.tensor_copy(cols(score, it, b, HEADS), side[b][:, 0:CJ * HEADS])
                    dve.tensor_copy(m[:, :, 0:HEADS], rows(side[b], HEADS))
                    dve.tensor_copy(m[:, :, 4], cols(w_d, it, b))
                    dve.drain()
                    scan_rows(dve, m, m, 0, 5, b, carry, maxima=4)
                    keep_last(dve, m, 5, carry).then_inc(S["scanned"], 1)
                    dve.drain()
            for b in range(2):
                dve.wait_ge(S[f"scores_saved{b}"], CREDIT + 16 * IT)
            ends_dve(dve, "scores", OD, 5, maxima=4)
            ends = nodes(0, 5)
            s0, s1 = scalars(0), scalars(1)
            dve.tensor_copy(nodes(1, 4), ends[:, :, 0:4])
            dve.tensor_scalar(s0, ends[:, :, 4], 1.0, None, ALU.add)
            ready(dve, "m_made")
            dve.tensor_scalar(s1, s0, 1e-12, None, ALU.max)
            dve.tensor_scalar(scalars(3), s0, 0.0, None, ALU.is_gt)
            ready(dve, "degree")
            dve.wait_ge(S["degree_root"], 1)
            dve.reciprocal(scalars(2), scalars(2))
            dve.drain()
            dve.tensor_tensor(dis[:], scalars(2), scalars(3), ALU.mult)
            dve.drain()
            dve.wait_ge(S["m_kept"], 16)
            dve.wait_ge(S["soft_spread"], 16 * NT)
            dve.wait_ge(S["soft_first"], 16)

            begin(dve, "soft", carry[:, 0:36])
            dve.drain()
            with dve.Fori(0, IT) as it:
                for b in range(2):
                    take_mask(dve, OD, it, b)
                    dve.drain()
                    dve.wait_ge(S[f"loaded{b}"], it * 32 + (LOADED["soft"] + 32))
                    dve.wait_ge(S[f"stored{b}"], it * 16 + STORED["soft"])
                    me, g, m = rows(X[b], 4), rows(G[b], 64), rows(M[b], 36)
                    scan_rows(dve, me, me, 0, 4, b, spread_carry)
                    keep_last(dve, me, 4, spread_carry)
                    dve.tensor_tensor(side[b][:, 0:CJ * HEADS], cols(score, it, b, HEADS), X[b][:, 0:CJ * HEADS],
                                      ALU.subtract).then_inc(S["soft_shifted"], 1)
                    dve.wait_ge(S["soft_exp"], it * 2 + (b + 1))
                    dve.tensor_tensor(m[:, :, 0:32].rearrange("p j (h d) -> p j h d", d=DH),
                                      g[:, :, 32:64].rearrange("p j (h d) -> p j h d", d=DH),
                                      rows(side[b], HEADS).unsqueeze(3).broadcast_to([P, CJ, HEADS, DH]), ALU.mult)
                    dve.tensor_copy(m[:, :, 32:36], rows(side[b], HEADS)).then_inc(S[f"free{b}"], 1)
                    dve.drain()
                    scan_rows(dve, m, m, 0, 36, b, carry)
                    keep_last(dve, m, 36, carry).then_inc(S["scanned"], 1)
                    dve.drain()
            ends_dve(dve, "soft", OD, 36)
            ends, attn = nodes(0, 36), nodes(1, 32)
            den = nodes(2, 4)
            dve.tensor_scalar(den, ends[:, :, 32:36], 1e-16, None, ALU.max)
            dve.drain()
            dve.reciprocal(den, den)
            dve.drain()
            dve.tensor_tensor(attn.rearrange("p t (h d) -> p t h d", d=DH),
                              ends[:, :, 0:32].rearrange("p t (h d) -> p t h d", d=DH),
                              den.unsqueeze(3).broadcast_to([P, NT, HEADS, DH]), ALU.mult)
            ready(dve, "product_in")
            x1, h = nodes(3, 32), nodes(5, 32)
            product_dve(dve, "Wo", plain(nodes(2, 32)), 32)
            fetch_back(dve, "res0")
            dve.tensor_tensor(x1, x1, nodes(2, 32), ALU.add)
            dve.drain()
            dve.sem_inc(S["res1_made"], 1)
            norm_relu(dve, 2, h, x1, nodes(6, 32))

            dve.tensor_tensor(nodes(1, 32), h, over(dis[:], 32), ALU.mult)
            ready(dve, "gcn_made")
            dve.wait_ge(S["gcn_kept"], 16)
            dve.wait_ge(S["res1_kept"], 16)
            for layer in range(1, 6):
                f = 32 if layer in (1, 5) else 64
                name = f"gcn{layer}"
                plain_pass_dve(dve, name, OD, f, weighted=True)
                ends_dve(dve, name, OD, f)
                fetch_back(dve, name)
                agg = nodes(2, f)
                dve.tensor_tensor(agg, nodes(0, f), nodes(1, f), ALU.add)
                dve.drain()
                dve.tensor_tensor(agg, agg, over(dis[:], f), ALU.mult)
                dve.drain()
                if layer == 1:
                    ready(dve, "product_in")
                    agg = nodes(3, 64)
                    product_dve(dve, "L1_W1", plain(agg), 64)
                    dve.drain()
                    f = 64
                graph_norm(dve, layer, agg, f, nodes(4, f))
                if layer < 5:
                    dve.tensor_scalar(nodes(5, 64), agg, 0.0, None, ALU.max)
                    nxt = layer + 1
                    fo = 32 if nxt == 5 else 64
                    ready(dve, "product_in")
                    product_dve(dve, f"L1_W{nxt}", plain(nodes(6, fo)), fo)
                    dve.drain()
                    dve.tensor_tensor(nodes(1, fo), nodes(6, fo), over(dis[:], fo), ALU.mult)
                    ready(dve, "gcn_made")
                    dve.wait_ge(S["gcn_kept"], 16 * nxt)
            fetch_back(dve, "res1")
            x2, h = nodes(3, 32), nodes(1, 32)
            dve.tensor_tensor(x2, x2, nodes(2, 32), ALU.add)
            dve.drain()
            dve.sem_inc(S["res2_made"], 1)
            norm_relu(dve, 3, h, x2, nodes(4, 32))

            ready(dve, "product_in")
            z, za = nodes(2, 64), nodes(4, 65)
            product_dve(dve, "fc_T", plain(z), 64)
            dve.drain()
            a_s, a_d = scalars(4), scalars(5)
            for part, a in ((0, a_s), (64, a_d)):
                dve.tensor_tensor(nodes(5, 64), z, vec("L2_gnn_W_attn", off=part, size=64), ALU.mult)
                dve.drain()
                dve.tensor_reduce(a, nodes(5, 64), AX.X, ALU.add)
                dve.drain()
            dve.tensor_copy(za[:, :, 0:64], z)
            dve.tensor_copy(za[:, :, 64], a_s)
            ready(dve, "za_made")
            for name in ("za_kept", "ad_kept", "res2_kept", "attend_first"):
                dve.wait_ge(S[name], 16)
            dve.wait_ge(S["attend_spread"], 16 * NT)
            begin(dve, "attend", carry[:, 0:65])
            dve.drain()
            with dve.Fori(0, IT) as it:
                for b in range(2):
                    take_mask(dve, OD, it, b)
                    dve.drain()
                    dve.wait_ge(S[f"rows{ROWS["attend"][0]}{b}"], it * (16 * CJ) + (ROWS["attend"][1] + 16 * CJ))
                    dve.wait_ge(S[f"loaded{b}"], it * 16 + (LOADED["attend"] + 16))
                    dve.wait_ge(S[f"stored{b}"], it * 16 + STORED["attend"])
                    ae, g, m = rows(X[b], 1), rows(G[b], 65), rows(M[b], 65)
                    scan_rows(dve, ae, ae, 0, 1, b, spread_carry)
                    keep_last(dve, ae, 1, spread_carry)
                    dve.tensor_tensor(side[b][:, 0:CJ], X[b][:, 0:CJ], g[:, :, 64], ALU.add).then_inc(S["attend_sum"], 1)
                    dve.wait_ge(S["attend_exp"], it * 2 + (b + 1))
                    dve.tensor_copy(cols(tanh_d, it, b), narrow[b][:, 0:CJ])
                    dve.tensor_copy(cols(wexp_d, it, b), narrow[b][:, CJ:2 * CJ])
                    dve.tensor_copy(m[:, :, 64], narrow[b][:, CJ:2 * CJ])
                    dve.tensor_tensor(m[:, :, 0:64], g[:, :, 0:64], over(narrow[b][:, CJ:2 * CJ], 64),
                                      ALU.mult).then_inc(S[f"free{b}"], 1)
                    dve.drain()
                    scan_rows(dve, m, m, 0, 65, b, carry)
                    keep_last(dve, m, 65, carry).then_inc(S["scanned"], 1)
                    dve.drain()
            for b in range(2):
                dve.wait_ge(S[f"attend_saved{b}"], CREDIT + 16 * IT)
            ends_dve(dve, "attend", OD, 65)
            ends, h = nodes(0, 65), nodes(1, 64)
            dve.tensor_scalar(rden[:], ends[:, :, 64], 1e-30, None, ALU.max)
            dve.drain()
            dve.reciprocal(rden[:], rden[:])
            dve.drain()
            dve.tensor_tensor(h, ends[:, :, 0:64], over(rden[:], 64), ALU.mult)
            ready(dve, "h_made")
            dve.sem_inc(S["product_in"], 1)
            product_dve(dve, "h_p1", plain(nodes(2, 64)), 64)
            ready(dve, "product_in")
            product_dve(dve, "A1", plain(nodes(3, 64)), 64)
            ready(dve, "A1_made")
            dve.sem_inc(S["product_in"], 1)
            product_dve(dve, "h_p2", plain(nodes(2, 64)), 64)
            ready(dve, "product_in")
            product_dve(dve, "A2", plain(nodes(4, 64)), 64)
            ready(dve, "A2_made")
            for name in ("h_kept", "A1_kept", "A2_kept", "umlp_first"):
                dve.wait_ge(S[name], 16)
            dve.wait_ge(S["umlp_spread"], 16 * NT)
            plain_pass_dve(dve, "hsum", OD, 64)
            ends_dve(dve, "hsum", OD, 64)
            ready(dve, "product_in")
            h1 = nodes(1, 64)
            product_dve(dve, "enc", plain(h1), 64)
            dve.tensor_tensor(nodes(2, 64), over(OD.count[:], 64), vec("L2_gnn_b_encK"), ALU.mult)
            dve.drain()
            dve.tensor_tensor(h1, h1, nodes(2, 64), ALU.add)
            ready(dve, "product_in")
            product_dve(dve, "K_0", plain(nodes(2, 64)), 64)
            ready(dve, "k0_raw")
            dve.wait_ge(S["product_in"], ORDINAL["K_1"] + 1)
            product_dve(dve, "K_1", relu_to(nodes(3, 64)), 64)
            ready(dve, "product_in")
            dve.sem_inc(S["k01_made"], 1)
            product_dve(dve, "K_2", plain(nodes(4, 64)), 64)
            ready(dve, "product_in")
            product_dve(dve, "KW", plain(nodes(5, 64)), 64)
            ready(dve, "KW_made")
            for name in ("k0_kept", "k1_kept", "KW_kept"):
                dve.wait_ge(S[name], 16)

            begin(dve, "umlp", carry[:, 0:64])
            dve.drain()
            with dve.Fori(0, IT) as it:
                for b in range(2):
                    take_mask(dve, OD, it, b)
                    dve.drain()
                    dve.wait_ge(S[f"rows{ROWS["umlp"][0]}{b}"], it * (16 * CJ) + (ROWS["umlp"][1] + 16 * CJ))
                    dve.wait_ge(S[f"loaded{b}"], it * 16 + (LOADED["umlp"] + 16))
                    dve.wait_ge(S[f"stored{b}"], it * 32 + STORED["umlp"])
                    a2, g, m, hb, tb = rows(X[b], 64), rows(G[b], 128), rows(M[b], 128), rows(H[b], 64), rows(T[b], 64)
                    scan_rows(dve, a2, a2, 0, 64, b, spread_carry)
                    keep_last(dve, a2, 64, spread_carry)
                    dve.tensor_tensor(tb, a2, g[:, :, 64:128], ALU.add).then_inc(S["umlp_pre"], 1)
                    dve.wait_ge(S["umlp_tanh"], it * 2 + (b + 1))
                    dve.tensor_tensor(a2, tb, tb, ALU.mult)
                    dve.drain()
                    dve.tensor_scalar(a2, a2, -1.0, 1.0, ALU.mult, ALU.add)
                    for u in range(UG):
                        k = b * UG + u
                        t = slice(4 * u, 4 * u + 4)
                        dve.wait_ge(S["umlp_relu"], it * (2 * UG) + (k + 3))
                        dve.scalar_tensor_tensor(hb[:, t, :], m[:, t, 0:64], 0.0, g[:, t, 0:64], ALU.is_gt,
                                                 ALU.mult).then_inc(S["umlp_slope"], 1)
                    for u in range(UG):
                        k = b * UG + u
                        t = slice(4 * u, 4 * u + 4)
                        dve.wait_ge(S["umlp_down"], it * (2 * UG) + (k + 1))
                        ps = psD[k % 2][:, 0:256].rearrange("p (j f) -> p j f", f=64)
                        dve.tensor_tensor(m[:, t, 64:128], ps, a2[:, t, :], ALU.mult).then_inc(S["umlp_taken"], 1)
                    dve.drain()
                    dve.sem_inc(S[f"free{b}"], 1)
                    scan_rows(dve, hb, m[:, :, 64:128], 0, 64, b, carry)
                    keep_last(dve, hb, 64, carry).then_inc(S["scanned"], 1)
                    dve.drain()
            ends_dve(dve, "umlp", OD, 64, stores=2)
            ready(dve, "dpd_made")
            dve.wait_ge(S["dpd_kept"], 16)

            plain_pass_dve(dve, "upair", OS, 128)
            ends_dve(dve, "upair", OS, 128)
            both = arena[:, 0:NT * 128].rearrange("p (t f) -> p t f", f=128)
            dve.tensor_copy(nodes(2, 64), both[:, :, 0:64])
            dve.tensor_copy(nodes(3, 64), both[:, :, 64:128])
            ready(dve, "product_in")
            product_dve(dve, "b_U2", plain(nodes(5, 64)), 64)
            dve.tensor_tensor(nodes(6, 64), over(OS.count[:], 64), vec("L2_gnn_U_b2"), ALU.mult)
            dve.drain()
            dve.tensor_tensor(nodes(5, 64), nodes(5, 64), nodes(6, 64), ALU.add)
            ready(dve, "product_in")
            product_dve(dve, "b_K2", plain(nodes(6, 64)), 64)
            fetch_back(dve, "k1")
            dve.scalar_tensor_tensor(nodes(6, 64), nodes(7, 64), 0.0, nodes(6, 64), ALU.is_gt, ALU.mult)
            ready(dve, "product_in")
            product_dve(dve, "b_K1", plain(nodes(2, 64)), 64)
            fetch_back(dve, "k0")
            dve.tensor_tensor(nodes(5, 64), nodes(5, 64), nodes(5, 64), ALU.mult)
            dve.drain()
            dve.tensor_scalar(nodes(5, 64), nodes(5, 64), -1.0, 1.0, ALU.mult, ALU.add)
            dve.drain()
            dve.tensor_tensor(nodes(2, 64), nodes(2, 64), nodes(5, 64), ALU.mult)
            ready(dve, "product_in")
            product_dve(dve, "b_K0", plain(nodes(6, 64)), 64)
            ready(dve, "dh1_made")
            dve.sem_inc(S["product_in"], 1)
            product_dve(dve, "b_U0s", plain(nodes(2, 64)), 64)
            ready(dve, "product_in")
            product_dve(dve, "b_p1", plain(nodes(5, 64)), 64)
            fetch_back(dve, "dpd")
            dve.sem_inc(S["product_in"], 1)
            product_dve(dve, "b_U0d", plain(nodes(2, 64)), 64)
            ready(dve, "product_in")
            product_dve(dve, "b_p2", plain(nodes(7, 64)), 64)
            dve.drain()
            dve.tensor_tensor(nodes(5, 64), nodes(5, 64), nodes(7, 64), ALU.add)
            ready(dve, "dhu_made")
            for name in ("dh1_kept", "dhu_kept"):
                dve.wait_ge(S[name], 16)
            plain_pass_dve(dve, "dh1", OS, 64)
            ends_dve(dve, "dh1", OS, 64)
            ready(dve, "product_in")
            dh = nodes(1, 64)
            product_dve(dve, "b_enc", plain(dh), 64)
            fetch_back(dve, "dhu")
            fetch_back(dve, "h")
            fetch_back(dve, "za")
            dve.tensor_tensor(dh, dh, nodes(2, 64), ALU.add)
            dve.drain()
            dve.tensor_tensor(nodes(3, 64), nodes(3, 64), dh, ALU.mult)
            dve.drain()
            c = scalars(6)
            dve.tensor_reduce(c, nodes(3, 64), AX.X, ALU.add)
            dve.drain()
            to_s, to_d = nodes(4, 67), nodes(5, 66)
            dve.tensor_copy(to_s[:, :, 0:64], dh)
            dve.tensor_copy(to_s[:, :, 64], a_d)
            dve.tensor_copy(to_s[:, :, 65], c)
            dve.tensor_copy(to_s[:, :, 66], rden[:])
            dve.tensor_copy(to_d[:, :, 0:64], dh)
            dve.tensor_copy(to_d[:, :, 64], c)
            dve.tensor_copy(to_d[:, :, 65], rden[:])
            ready(dve, "grad_made")
            for name in ("to_s_kept", "to_d_kept", "grad_first", "back_first"):
                dve.wait_ge(S[name], 16)
            for name in ("grad_spread", "back_spread"):
                dve.wait_ge(S[name], 16 * NT)

            begin(dve, "grad", carry[:, 0:65])
            dve.drain()

            def through_softmax(b, de, alpha_dst, w, t, c_e, rden_e, dst):
                u = side[b]
                dve.tensor_tensor(alpha_dst, w, rden_e, ALU.mult)
                dve.tensor_tensor(de, de, c_e, ALU.subtract)
                dve.tensor_tensor(u[:, 96:128], t, t, ALU.mult)
                dve.drain()
                dve.tensor_tensor(de, de, alpha_dst, ALU.mult)
                dve.tensor_scalar(u[:, 96:128], u[:, 96:128], -0.25, 0.25, ALU.mult, ALU.add)
                dve.drain()
                return dve.tensor_tensor(dst, de, u[:, 96:128], ALU.mult)

            with dve.Fori(0, IT) as it:
                for b in range(2):
                    take_mask(dve, OS, it, b)
                    dve.drain()
                    dve.wait_ge(S[f"rows{ROWS["grad"][0]}{b}"], it * (16 * CJ) + (ROWS["grad"][1] + 16 * CJ))
                    dve.wait_ge(S[f"loaded{b}"], it * 16 + (LOADED["grad"] + 16))
                    dve.wait_ge(S[f"stored{b}"], it * 16 + STORED["grad"])
                    ze, g, m, u = rows(X[b], 65), rows(G[b], 67), rows(M[b], 65), side[b]
                    scan_rows(dve, ze, ze, 0, 65, b, spread_carry)
                    keep_last(dve, ze, 65, spread_carry)
                    dve.tensor_tensor(u[:, 0:32], ze[:, :, 64], g[:, :, 64], ALU.add).then_inc(S["grad_sum"], 1)
                    dve.tensor_tensor(rows(H[b], 64), ze[:, :, 0:64], g[:, :, 0:64], ALU.mult)
                    dve.drain()
                    dve.tensor_reduce(u[:, 32:64], rows(H[b], 64), AX.X, ALU.add)
                    dve.drain()
                    dve.wait_ge(S["grad_exp"], it * 2 + (b + 1))
                    through_softmax(b, u[:, 32:64], u[:, 64:96], narrow[b][:, CJ:2 * CJ], narrow[b][:, 0:CJ],
                                    g[:, :, 65], g[:, :, 66], m[:, :, 64])
                    dve.tensor_tensor(m[:, :, 0:64], g[:, :, 0:64], over(u[:, 64:96], 64), ALU.mult)
                    dve.drain()
                    dve.sem_inc(S[f"free{b}"], 1)
                    scan_rows(dve, m, m, 0, 65, b, carry)
                    keep_last(dve, m, 65, carry).then_inc(S["scanned"], 1)
                    dve.drain()
            ends_dve(dve, "grad", OS, 65)
            ready(dve, "gs_made")
            dve.wait_ge(S["gs_kept"], 16)

            begin(dve, "back", carry[:, 0:1])
            dve.drain()
            with dve.Fori(0, IT) as it:
                for b in range(2):
                    take_mask(dve, OD, it, b)
                    dve.tensor_copy(narrow[b][:, 0:CJ], cols(tanh_d, it, b))
                    dve.tensor_copy(narrow[b][:, CJ:2 * CJ], cols(wexp_d, it, b))
                    dve.drain()
                    dve.wait_ge(S[f"loaded{b}"], it * 32 + (LOADED["back"] + 32))
                    dve.wait_ge(S[f"stored{b}"], it * 16 + STORED["back"])
                    de, g, m, u = rows(X[b], 66), rows(G[b], 65), rows(M[b], 1), side[b]
                    scan_rows(dve, de, de, 0, 66, b, spread_carry2)
                    keep_last(dve, de, 66, spread_carry2)
                    dve.tensor_tensor(rows(H[b], 64), de[:, :, 0:64], g[:, :, 0:64], ALU.mult)
                    dve.drain()
                    dve.tensor_reduce(u[:, 32:64], rows(H[b], 64), AX.X, ALU.add)
                    dve.drain()
                    through_softmax(b, u[:, 32:64], u[:, 64:96], narrow[b][:, CJ:2 * CJ], narrow[b][:, 0:CJ],
                                    de[:, :, 64], de[:, :, 65], m[:, :, 0]).then_inc(S[f"free{b}"], 1)
                    dve.drain()
                    scan_rows(dve, m, m, 0, 1, b, carry)
                    keep_last(dve, m, 1, carry).then_inc(S["scanned"], 1)
                    dve.drain()
            ends_dve(dve, "back", OD, 1)
            fetch_back(dve, "gs")
            gs, dz = nodes(1, 65), nodes(2, 64)
            dve.tensor_copy(scalars(7), gs[:, :, 64])
            dve.drain()
            dve.tensor_tensor(nodes(3, 64), over(scalars(7), 64), vec("L2_gnn_W_attn", off=0, size=64), ALU.mult)
            dve.tensor_tensor(nodes(4, 64), over(NODE[0][:, 0:NT], 64), vec("L2_gnn_W_attn", off=64, size=64), ALU.mult)
            dve.drain()
            dve.tensor_tensor(dz, gs[:, :, 0:64], nodes(3, 64), ALU.add)
            dve.drain()
            dve.tensor_tensor(dz, dz, nodes(4, 64), ALU.add)
            ready(dve, "product_in")
            y, yd, t2 = nodes(3, 32), nodes(4, 32), nodes(5, 32)
            product_dve(dve, "b_fc", plain(y), 32)
            ready(dve, "product_in")
            product_dve(dve, "b_D", plain(yd), 32)
            dve.drain()
            dve.tensor_tensor(t2[:, :, 0:16], y[:, :, 16:32], yd[:, :, 0:16], ALU.subtract)
            dve.scalar_tensor_tensor(t2[:, :, 16:32], y[:, :, 0:16], -1.0, yd[:, :, 16:32], ALU.mult, ALU.subtract)
            fetch_back(dve, "res2")
            x3, h = nodes(6, 32), nodes(1, 32)
            dve.tensor_tensor(x3, x3, t2, ALU.add)
            dve.drain()
            dve.sem_inc(S["res3_made"], 1)
            norm_relu(dve, 4, h, x3, nodes(2, 32))

            ready(dve, "hin_made")
            dve.wait_ge(S["hin_kept"], 16)
            dve.wait_ge(S["res3_kept"], 16)
            plain_pass_dve(dve, "mean", OD, 32)
            ends_dve(dve, "mean", OD, 32)
            fetch_back(dve, "hin")
            cat = nodes(2, 64)
            dve.tensor_scalar(scalars(0), OD.count[:], 1.0, None, ALU.max)
            dve.drain()
            dve.reciprocal(scalars(0), scalars(0))
            dve.drain()
            dve.tensor_tensor(cat[:, :, 32:64], nodes(0, 32), over(scalars(0), 32), ALU.mult)
            dve.tensor_copy(cat[:, :, 0:32], nodes(1, 32))
            ready(dve, "product_in")
            product_dve(dve, "L3", plain(nodes(4, 32)), 32)
            dve.drain()
            dve.tensor_tensor(nodes(4, 32), nodes(4, 32), vec("L3_gnn_b"), ALU.add)
            fetch_back(dve, "res3")
            dve.scalar_tensor_tensor(nodes(4, 32), nodes(4, 32), 0.0, nodes(5, 32), ALU.max, ALU.add)
            ready(dve, "result")

        @block.scalar
        def _(act):
            def save_chunks(name, table, f, it, b):
                act.wait_ge(S[f"rows{ROWS[name][0]}{b}"], it * (16 * CJ) + (ROWS[name][1] + 16 * CJ))
                act.dma_start(chunk(table, f, it, b), rows(G[b], f)).then_inc(S[f"{name}_saved{b}"], 16)

            def sigmoid_exp(name, it, b):
                act.wait_ge(S[f"{name}_sum"], it * 2 + (b + 1))
                act.activation(narrow[b][:, 0:CJ], side[b][:, 0:CJ], ACT.Tanh, scale=0.5)
                act.drain()
                act.activation(narrow[b][:, CJ:2 * CJ], narrow[b][:, 0:CJ], ACT.Exp, scale=0.5,
                               bias=half[:]).then_inc(S[f"{name}_exp"], 1)

            deviation_act(act, 1)
            product_act(act, "kvq")
            with act.Fori(0, IT) as it:
                for b in range(2):
                    save_chunks("scores", KV, 64, it, b)
                    store_chunk(act, "scores", it, b, [(R[5], 5, M)])
            act.wait_ge(S["degree"], 1)
            act.activation(scalars(2), scalars(1), ACT.Sqrt).then_inc(S["degree_root"], 1)
            with act.Fori(0, IT) as it:
                for b in range(2):
                    act.wait_ge(S["soft_shifted"], it * 2 + (b + 1))
                    act.activation(side[b][:, 0:CJ * HEADS], side[b][:, 0:CJ * HEADS], ACT.Exp).then_inc(S["soft_exp"], 1)
                    store_chunk(act, "soft", it, b, [(R[36], 36, M)])
            product_act(act, "Wo")
            deviation_act(act, 2)
            for layer in range(1, 6):
                f = 32 if layer in (1, 5) else 64
                store_act(act, f"gcn{layer}", [(R[f], f, M)])
                if layer == 1:
                    product_act(act, "L1_W1")
                graph_norm_act(act, layer, 32 if layer == 5 else 64)
                if layer < 5:
                    product_act(act, f"L1_W{layer + 1}")
            deviation_act(act, 3)
            product_act(act, "fc_T")
            with act.Fori(0, IT) as it:
                for b in range(2):
                    save_chunks("attend", ZA, 65, it, b)
                    sigmoid_exp("attend", it, b)
                    store_chunk(act, "attend", it, b, [(R[65], 65, M)])
            for name in ("h_p1", "A1", "h_p2", "A2"):
                product_act(act, name)
            store_act(act, "hsum", [(R[64], 64, M)])
            product_act(act, "enc")
            product_act(act, "K_0")
            act.wait_ge(S["k0_raw"], 1)
            act.activation(flat(2, 64), flat(2, 64), ACT.Tanh).then_inc(S["product_in"], 1)
            for name in ("K_1", "K_2", "KW"):
                product_act(act, name)
            with act.Fori(0, IT) as it:
                for b in range(2):
                    act.wait_ge(S["umlp_pre"], it * 2 + (b + 1))
                    act.activation(T[b], T[b], ACT.Tanh).then_inc(S["umlp_tanh"], 1)
                    for u in range(UG):
                        k = b * UG + u
                        act.wait_ge(S["umlp_turned"], it * (2 * UG) + (k + 1))
                        act.copy(packT[k % 2][:], psT[k % 2][:, 0:256]).then_inc(S["umlp_turned_copied"], 1)
                        act.wait_ge(S["umlp_up"], it * (2 * UG) + (k + 1))
                        act.activation(rows(M[b], 128)[:, 4 * u:4 * u + 4, 0:64],
                                       psO[k % 2][:, 0:256].rearrange("p (j f) -> p j f", f=64), ACT.Relu).then_inc(S["umlp_relu"], 1)
                    for u in range(UG):
                        k = b * UG + u
                        act.wait_ge(S["umlp_turned_down"], it * (2 * UG) + (k + 1))
                        act.copy(packB[k % 2][:], psB[k % 2][:, 0:256]).then_inc(S["umlp_down_copied"], 1)
                    store_chunk(act, "umlp", it, b, [(UD, 128, M), (R[64], 64, H)])
            store_act(act, "upair", [(R[128], 128, M)])
            for name in ("b_U2", "b_K2", "b_K1", "b_K0", "b_U0s", "b_p1", "b_U0d", "b_p2"):
                product_act(act, name)
            store_act(act, "dh1", [(R[64], 64, M)])
            product_act(act, "b_enc")
            with act.Fori(0, IT) as it:
                for b in range(2):
                    sigmoid_exp("grad", it, b)
                    store_chunk(act, "grad", it, b, [(R[65], 65, M)])
            store_act(act, "back", [(R[1], 1, M)])
            product_act(act, "b_fc")
            product_act(act, "b_D")
            deviation_act(act, 4)
            store_act(act, "mean", [(R[32], 32, M)])
            product_act(act, "L3")

        @block.tensor
        def _(pe):
            pe.wait_ge(S["weights"], 32)
            pe.wait_ge(S["zeros"], 1)
            sort_pe(pe, 0, LO)
            sort_pe(pe, 1, HI)
            order_pe(pe, OS)
            order_pe(pe, OD)
            product_pe(pe, "kvq", "kvq", NODE[1])
            ends_pe(pe, "scores", OD, 5, maxima=4)
            ends_pe(pe, "soft", OD, 36)
            product_pe(pe, "Wo", "Wo", NODE[1])
            for layer in range(1, 6):
                f = 32 if layer in (1, 5) else 64
                ends_pe(pe, f"gcn{layer}", OD, f)
                if layer == 1:
                    product_pe(pe, "L1_W1", "L1_W1", NODE[2])
                graph_norm_pe(pe, layer, 32 if layer == 5 else 64)
                if layer < 5:
                    product_pe(pe, f"L1_W{layer + 1}", f"L1_W{layer + 1}", NODE[5])
            product_pe(pe, "fc_T", "fc_T", NODE[1])
            ends_pe(pe, "attend", OD, 65)
            product_pe(pe, "h_p1", "p1_T", NODE[1], "L2_gnn_b_p1")
            product_pe(pe, "A1", "U0_T", NODE[2], "L2_gnn_U_b0")
            product_pe(pe, "h_p2", "p2_T", NODE[1], "L2_gnn_b_p2")
            product_pe(pe, "A2", "U0_T", NODE[2])
            ends_pe(pe, "hsum", OD, 64)
            product_pe(pe, "enc", "encK_T", NODE[0])
            product_pe(pe, "K_0", "K0_T", NODE[1], "L2_gnn_K_b0")
            product_pe(pe, "K_1", "K1_T", NODE[2], "L2_gnn_K_b1")
            product_pe(pe, "K_2", "K2_T", NODE[3], "L2_gnn_K_b2")
            product_pe(pe, "KW", "U2", NODE[4])
            for name in ("umlp_turned_copied", "umlp_relu", "umlp_down_copied", "umlp_taken"):
                pe.sem_inc(S[name], 2)
            up, down, bias = WAT["U1_T"][0], WAT["U1"][0], VAT["L2_gnn_U_b1"][0]
            with pe.Fori(0, IT) as it:
                for b in range(2):
                    n = 2 * UG
                    pe.wait_ge(S["umlp_tanh"], it * 2 + (b + 1))
                    for u in range(UG):
                        k = b * UG + u
                        pe.wait_ge(S["umlp_turned_copied"], it * n + (k + 1))
                        for i in range(2):
                            last = pe.transpose(psT[k % 2][:, i * P:(i + 1) * P], T[b][:, (2 * u + i) * P:(2 * u + i + 1) * P], ident[:])
                        last.then_inc(S["umlp_turned"], 1)
                        pe.wait_ge(S["umlp_turned_copied"], it * n + (k + 3))
                        pe.wait_ge(S["umlp_relu"], it * n + (k + 1))
                        for i in range(2):
                            pe.matmul(psO[k % 2][:, i * P:(i + 1) * P], packT[k % 2][:, i * P:(i + 1) * P],
                                      weights[:, up:up + P], start=True, stop=False)
                            last = pe.matmul(psO[k % 2][:, i * P:(i + 1) * P], ones[0:1, :], vectors[0:1, bias:bias + P],
                                             start=False, stop=True)
                        last.then_inc(S["umlp_up"], 1)
                    for u in range(UG):
                        k = b * UG + u
                        pe.wait_ge(S["umlp_slope"], it * n + (k + 1))
                        pe.wait_ge(S["umlp_down_copied"], it * n + (k + 1))
                        for i in range(2):
                            last = pe.transpose(psB[k % 2][:, i * P:(i + 1) * P], H[b][:, (2 * u + i) * P:(2 * u + i + 1) * P], ident[:])
                        last.then_inc(S["umlp_turned_down"], 1)
                        pe.wait_ge(S["umlp_down_copied"], it * n + (k + 3))
                        pe.wait_ge(S["umlp_taken"], it * n + (k + 1))
                        for i in range(2):
                            last = pe.matmul(psD[k % 2][:, i * P:(i + 1) * P], packB[k % 2][:, i * P:(i + 1) * P],
                                             weights[:, down:down + P], start=True, stop=True)
                        last.then_inc(S["umlp_down"], 1)
            ends_pe(pe, "umlp", OD, 64)
            ends_pe(pe, "upair", OS, 128)
            product_pe(pe, "b_U2", "U2_T", NODE[2])
            product_pe(pe, "b_K2", "K2", NODE[5])
            product_pe(pe, "b_K1", "K1", NODE[6])
            product_pe(pe, "b_K0", "K0", NODE[2])
            product_pe(pe, "b_U0s", "U0", NODE[3])
            product_pe(pe, "b_p1", "p1", NODE[2])
            product_pe(pe, "b_U0d", "U0", NODE[4])
            product_pe(pe, "b_p2", "p2", NODE[2])
            ends_pe(pe, "dh1", OS, 64)
            product_pe(pe, "b_enc", "encK", NODE[0])
            ends_pe(pe, "grad", OS, 65)
            ends_pe(pe, "back", OD, 1)
            product_pe(pe, "b_fc", "fc", NODE[2])
            product_pe(pe, "b_D", "D_T", NODE[3])
            ends_pe(pe, "mean", OD, 32)
            product_pe(pe, "L3", "L3_W", NODE[2])

        @block.gpsimd
        def _(pool):
            pool.iota(digits[:], [[1, P]], base=0, channel_multiplier=0, allow_small_or_imprecise_dtypes=True)
            pool.iota(part_id[:], [[0, 1]], base=0, channel_multiplier=1, allow_small_or_imprecise_dtypes=True)
            pool.iota(node_id[:], [[1, NT + 1]], base=-1, channel_multiplier=NT, allow_small_or_imprecise_dtypes=True)
            pool.drain()
            pool.sem_inc(S["iotas"], 1)
            pool.iota(M[1][:, 0:J].bitcast(I32), [[1, J]], base=0, channel_multiplier=J)
            pool.drain()
            pool.sem_inc(S["places"], 1)
            sort_pool(pool, 0)
            sort_pool(pool, 1)
            order_pool(pool, OS)
            order_pool(pool, OD)
            pool.wait_ge(S["filled"], 16 * FILLS)
            pool.wait_ge(S["q_made"], 1)
            spread_pool(pool, "scores", OD, 32, NODE[3], XQ)
            pool.wait_ge(S["q_kept"], 16)
            spread_first_pool(pool, "scores", OD, 32, TB["q"], spread_carry)
            pool.wait_ge(S["kv_kept"], 16)
            gather_pool(pool, "scores", TB["kv"], 64, src_d, saved=True)
            ends_pool(pool, "scores", OD, 5)
            pool.wait_ge(S["m_made"], 1)
            spread_pool(pool, "soft", OD, 4, NODE[1], XM)
            pool.wait_ge(S["m_kept"], 16)
            spread_first_pool(pool, "soft", OD, 4, TB["m"], spread_carry)
            ends_pool(pool, "soft", OD, 36)
            for layer in range(1, 6):
                f = 32 if layer in (1, 5) else 64
                pool.wait_ge(S["gcn_kept"], 16 * layer)
                gather_pool(pool, f"gcn{layer}", TB[f"gcn{layer}"], f, src_d)
                ends_pool(pool, f"gcn{layer}", OD, f)
            pool.wait_ge(S["za_made"], 1)
            spread_pool(pool, "attend", OD, 1, scalars(5), XA)
            pool.wait_ge(S["ad_kept"], 16)
            spread_first_pool(pool, "attend", OD, 1, TB["ad"], spread_carry)
            pool.wait_ge(S["za_kept"], 16)
            gather_pool(pool, "attend", TB["za"], 65, src_d, saved=True)
            ends_pool(pool, "attend", OD, 65)
            pool.wait_ge(S["A2_made"], 1)
            spread_pool(pool, "umlp", OD, 64, NODE[4], XA2)
            pool.wait_ge(S["A2_kept"], 16)
            spread_first_pool(pool, "umlp", OD, 64, TB["a2"], spread_carry)
            pool.wait_ge(S["h_kept"], 16)
            gather_pool(pool, "hsum", TB["h"], 64, src_d)
            ends_pool(pool, "hsum", OD, 64)
            pool.wait_ge(S["A1_kept"], 16)
            pool.wait_ge(S["KW_kept"], 16)
            gather_pool(pool, "umlp", TB["ka"], 128, src_d)
            ends_pool(pool, "umlp", OD, 64)
            gather_pool(pool, "upair", UD, 128, pos_s)
            ends_pool(pool, "upair", OS, 128)
            pool.wait_ge(S["dh1_kept"], 16)
            gather_pool(pool, "dh1", TB["dh1"], 64, dst_s)
            ends_pool(pool, "dh1", OS, 64)
            pool.wait_ge(S["grad_made"], 1)
            spread_pool(pool, "grad", OS, 65, NODE[6], XS)
            spread_pool(pool, "back", OD, 66, NODE[5], XF)
            spread_first_pool(pool, "grad", OS, 65, TB["za"], spread_carry)
            pool.wait_ge(S["to_d_kept"], 16)
            spread_first_pool(pool, "back", OD, 66, TB["f"], spread_carry2)
            pool.wait_ge(S["to_s_kept"], 16)
            gather_pool(pool, "grad", TB["dst"], 67, dst_s)
            ends_pool(pool, "grad", OS, 65)
            ends_pool(pool, "back", OD, 1)
            pool.wait_ge(S["hin_kept"], 16)
            gather_pool(pool, "mean", TB["hin"], 32, src_d)
            ends_pool(pool, "mean", OD, 32)

        @block.sync
        def _(sp):
            sp.dma_start(weights[:], weights_in).then_inc(S["weights"], 16)
            sp.dma_start(vectors[:], vectors_in.broadcast_to([P, VCOLS])).then_inc(S["weights"], 16)
            sp.dma_start(src_d[:], src_in).then_inc(S["edges"], 16)
            sp.dma_start(H[0][:, 0:J].bitcast(I32), dst_in).then_inc(S["edges"], 16)
            sp.dma_start(w_d[:], w_in).then_inc(S["edges"], 16)
            sp.wait_ge(S["zeros"], 1)
            for t, f in SPREADS:
                sp.dma_start(t[0:EP, :].rearrange("(p j) f -> p (j f)", j=J).rearrange("p (f j) -> p f j", j=J),
                             zeros[:].unsqueeze(1).broadcast_to([P, f, J])).then_inc(S["filled"], 16)
            firsts = ["stored0", "stored1", "scores_saved0", "scores_saved1", "attend_saved0", "attend_saved1"]
            for f in R:
                name = firsts.pop(0) if firsts else "filled"
                sp.dma_start(R[f][EP:EP + P, :], zeros[:, 0:f]).then_inc(S[name], CREDIT)
                sp.dma_start(R[f][EP + P:EP + P + 1, :], zeros[0:1, 0:f]).then_inc(S["filled"], 16)
            sort_sp(sp, 0)
            sp.wait_ge(S["reloaded"], 16)
            sort_sp(sp, 1)
            order_sp(sp, OS)
            sp.wait_ge(S["order_built"], 1)
            sp.dma_start(T[1][:, 0:J].bitcast(I32), dst_in).then_inc(S["dst_again"], 16)
            order_sp(sp, OD)
            sp.wait_ge(S["room"], 1)
            sp.dma_start(flat(0, 32), by_node(x_in)).then_inc(S["back"], 16)
            store_node(sp, "kv", TB["kv"], 2, 64)
            store_node(sp, "q", TB["q"], 3, 32)
            store_node(sp, "res0", TB["res0"], 0, 32)
            sp.wait_ge(S["scores_spread"], 16 * NT)
            load_sp(sp, "scores", [(XQ, 32, X)])
            store_node(sp, "m", TB["m"], 1, 4)
            sp.wait_ge(S["soft_spread"], 16 * NT)
            load_sp(sp, "soft", [(KV, 64, G), (XM, 4, X)])
            load_node(sp, "res0", TB["res0"], 3, 32, "res0_kept")
            store_node(sp, "res1", TB["res1"], 3, 32)
            for layer in range(1, 6):
                f = 32 if layer in (1, 5) else 64
                name = f"gcn{layer}"
                store_node(sp, "gcn", TB[name], 1, f, layer)
                load_node(sp, name, TB[name], 1, f, "gcn_kept", layer)
            load_node(sp, "res1", TB["res1"], 3, 32, "res1_kept")
            store_node(sp, "res2", TB["res2"], 3, 32)
            store_node(sp, "za", TB["za"], 4, 65)
            sp.dma_start(by_node(TB["ad"]), scalars(5)).then_inc(S["ad_kept"], 16)
            sp.wait_ge(S["attend_spread"], 16 * NT)
            load_sp(sp, "attend", [(XA, 1, X)])
            store_node(sp, "h", TB["h"], 1, 64)
            ka = TB["ka"].rearrange("(p t) f -> p t f", t=NT)
            sp.wait_ge(S["A1_made"], 1)
            sp.dma_start(ka[:, :, 64:128], nodes(3, 64)).then_inc(S["A1_kept"], 16)
            store_node(sp, "A2", TB["a2"], 4, 64)
            sp.wait_ge(S["k01_made"], 1)
            sp.dma_start(by_node(TB["k0"]), flat(2, 64)).then_inc(S["k0_kept"], 16)
            sp.dma_start(by_node(TB["k1"]), flat(3, 64)).then_inc(S["k1_kept"], 16)
            sp.wait_ge(S["KW_made"], 1)
            sp.dma_start(ka[:, :, 0:64], nodes(5, 64)).then_inc(S["KW_kept"], 16)
            sp.wait_ge(S["umlp_spread"], 16 * NT)
            load_sp(sp, "umlp", [(XA2, 64, X)])
            store_node(sp, "dpd", TB["dp"], 0, 64)
            load_node(sp, "k1", TB["k1"], 7, 64, "k1_kept")
            load_node(sp, "k0", TB["k0"], 5, 64, "k0_kept")
            store_node(sp, "dh1", TB["dh1"], 6, 64)
            load_node(sp, "dpd", TB["dp"], 4, 64, "dpd_kept")
            store_node(sp, "dhu", TB["w2"], 5, 64)
            load_node(sp, "dhu", TB["w2"], 2, 64, "dhu_kept")
            load_node(sp, "h", TB["h"], 3, 64, "h_kept")
            load_node(sp, "za", TB["za"], 6, 65, "za_kept")
            sp.wait_ge(S["grad_made"], 1)
            sp.dma_start(by_node(TB["dst"]), flat(4, 67)).then_inc(S["to_s_kept"], 16)
            sp.dma_start(by_node(TB["f"]), flat(5, 66)).then_inc(S["to_d_kept"], 16)
            sp.wait_ge(S["grad_spread"], 16 * NT)
            sp.wait_ge(S["back_spread"], 16 * NT)
            load_sp(sp, "grad", [(XS, 65, X)])
            store_node(sp, "gs", TB["gs"], 0, 65)
            load_sp(sp, "back", [(ZA, 65, G), (XF, 66, X)])
            load_node(sp, "gs", TB["gs"], 1, 65, "gs_kept")
            load_node(sp, "res2", TB["res2"], 6, 32, "res2_kept")
            store_node(sp, "res3", TB["res3"], 6, 32)
            store_node(sp, "hin", TB["hin"], 1, 32)
            load_node(sp, "hin", TB["hin"], 1, 32, "hin_kept")
            load_node(sp, "res3", TB["res3"], 5, 32, "res3_kept")
            sp.wait_ge(S["result"], 1)
            full, rest = N // NT, N % NT
            sp.dma_start(out[0:full * NT, :].rearrange("(p t) f -> p (t f)", t=NT),
                         NODE[4][0:full, 0:NT * 32]).then_inc(S["out"], 16)
            sp.dma_start(out[full * NT:N, :].rearrange("(p t) f -> p (t f)", t=rest),
                         NODE[4][full:full + 1, 0:rest * 32]).then_inc(S["out"], 16)
            sp.wait_ge(S["out"], 32)


def kernel(**inputs):
    import numpy as np
    import concourse.bacc as bacc
    from concourse.bass_utils import run_bass_kernel_spmd as run

    def edges(a, fill):
        padded = np.full((EP,), fill, a.dtype)
        padded[:E] = a
        return padded.reshape(P, J)

    x = np.zeros((NR, 32), np.float32)
    x[:N] = inputs["x"]
    places, width = weight_places()
    weights = np.zeros((P, width), np.float32)
    for name, source, transposed, rows, cols in weight_plan():
        parts = [np.asarray(inputs[s]) for s in (source if isinstance(source, tuple) else (source,))]
        w = np.concatenate([p.T if transposed else p for p in parts], axis=1)
        for i in range(P // rows):
            at = places[name][0] + i * cols
            weights[i * rows:(i + 1) * rows, at:at + cols] = w
    places, width = vector_places()
    vectors = np.zeros((1, width), np.float32)
    for name in VECTORS:
        at, size = places[name]
        for i in range(4 if name.startswith(FOUR) else 1):
            vectors[0, at + i * size:at + (i + 1) * size] = np.asarray(inputs[name]).reshape(-1)
    arrays = {"x": x, "src": edges(np.asarray(inputs["src"]), PAD), "dst": edges(np.asarray(inputs["dst"]), PAD),
              "w": edges(np.asarray(inputs["edge_weight"]), 0), "weights": weights, "vectors": vectors}
    nc = bacc.Bacc("TRN2", target_bir_lowering=False, num_devices=1)
    args = [nc.dram_tensor(f"in_{k}", a.shape, mybir.dt.from_np(a.dtype), kind="ExternalInput").ap()
            for k, a in arrays.items()]
    out = nc.dram_tensor("out_x", (N, 32), F32, kind="ExternalOutput").ap()
    build(nc, *args, out)
    r = run(nc, [{f"in_{k}": a for k, a in arrays.items()}], core_ids=[0])
    return r.results[0]["out_x"]
```

```python
from contextlib import ExitStack

import concourse.bass as bass
from concourse import mybir

F32, I32, BF16 = mybir.dt.float32, mybir.dt.int32, mybir.dt.bfloat16
ALU, ACT, AX = mybir.AluOpType, mybir.ActivationFunctionType, mybir.AxisListType

P = 128
N = 6250
NT = 52
NR = P * NT
E = 106250
J = 832
EP = P * J
PAD = NR - 1
CJ = 32
IT = J // CJ // 2
ER = EP + 1 + NR
ZERO_ROW, SPARE_ROW = EP, EP + 1
HEADS, DH = 4, 8
BIG = 1.0e30
LO, HI = 64, NR // 64
EPS = 1e-5


def weight_plan():
    two = [(f"L1_W{i}", f"L1_gnn_W{i}", False, 64, 64) for i in (2, 3, 4)]
    sq = [("encK_T", "L2_gnn_W_encK", True), ("p1_T", "L2_gnn_W_p1", True), ("p2_T", "L2_gnn_W_p2", True),
          ("K0_T", "L2_gnn_K_w0", True), ("K1_T", "L2_gnn_K_w1", True), ("K2_T", "L2_gnn_K_w2", True),
          ("U0_T", "L2_gnn_U_w0", True), ("U1_T", "L2_gnn_U_w1", True), ("U2_T", "L2_gnn_U_w2", True),
          ("encK", "L2_gnn_W_encK", False), ("p1", "L2_gnn_W_p1", False), ("p2", "L2_gnn_W_p2", False),
          ("K0", "L2_gnn_K_w0", False), ("K1", "L2_gnn_K_w1", False), ("K2", "L2_gnn_K_w2", False),
          ("U0", "L2_gnn_U_w0", False), ("U1", "L2_gnn_U_w1", False), ("U2", "L2_gnn_U_w2", False)]
    return ([("kvq", ("L0_gnn_Wk", "L0_gnn_Wv", "L0_gnn_Wq"), False, 32, 96),
             ("Wo", "L0_gnn_Wo", False, 32, 32), ("L1_W1", "L1_gnn_W1", False, 32, 64)] + two
            + [("L1_W5", "L1_gnn_W5", False, 64, 32), ("fc_T", "L2_gnn_W_fc", True, 32, 64),
               ("fc", "L2_gnn_W_fc", False, 64, 32), ("D_T", "L2_gnn_D", True, 32, 32),
               ("L3_W", "L3_gnn_W", False, 64, 32)]
            + [(n, i, t, 64, 64) for n, i, t in sq])


def weight_places():
    at, out = 0, {}
    for name, _, _, rows, cols in weight_plan():
        width = (P // rows) * cols
        out[name] = (at, width)
        at += width
    return out, at


VECTORS = ([f"L1_gnn_{v}{i}{w}" for i in range(1, 6) for v, w in (("b", ""), ("g", "w"), ("g", "b"), ("g", "a"))]
           + ["L2_gnn_W_attn", "L2_gnn_b_encK", "L2_gnn_b_p1", "L2_gnn_b_p2", "L2_gnn_K_b0", "L2_gnn_K_b1",
              "L2_gnn_K_b2", "L2_gnn_U_b0", "L2_gnn_U_b1", "L2_gnn_U_b2", "L3_gnn_b"])


def vector_places():
    at, out = 0, {}
    for name in VECTORS:
        size = 128 if name == "L2_gnn_W_attn" else 32 if (name.startswith("L1_gnn") and "5" in name) or name == "L3_gnn_b" else 64
        out[name] = (at, size)
        at += size
    return out, at


def build(nc, x_in, src_in, dst_in, w_in, weights_in, vectors_in, out):
    ctx = ExitStack()
    with ctx:
        WAT, WCOLS = weight_places()
        VAT, VCOLS = vector_places()

        class Semaphores(dict):
            def __missing__(self, name):
                self[name] = ctx.enter_context(nc.semaphore(name))
                return self[name]

        S = Semaphores()

        def sb(name, shape, dt=F32):
            return ctx.enter_context(nc.sbuf_tensor(name, shape, dt))

        def dram(name, shape, dt=F32):
            return nc.dram_tensor(name, shape, dt).ap()

        weights = sb("weights", [P, WCOLS])
        vectors = sb("vectors", [P, VCOLS])
        ident = sb("ident", [P, P])
        ones = sb("ones", [P, P])
        below = sb("below", [P, P])
        node_id = sb("node_id", [P, NT + 1])
        part_id = sb("part_id", [P, 1])
        valid = sb("valid", [P, NT])
        w_d = sb("w_d", [P, J])
        arena = sb("arena", [P, 2 * (4096 + 4096 + 67 * CJ) + 67 * CJ + 4096 + 5 * 2048])
        half = sb("half", [P, 1])
        digits = sb("digits", [P, P])

        at = [0]

        def take(n):
            at[0] += n
            return arena[:, at[0] - n:at[0]]

        G = [take(4096) for _ in range(2)]
        OUT = [take(4096) for _ in range(2)]
        X = [take(67 * CJ) for _ in range(2)]
        XP = take(67 * CJ)
        M = take(4096)
        MR = take(2048)
        T = take(2048)
        HB = take(2048)
        H = [take(2048) for _ in range(2)]
        score = arena[:, at[0] - 4096:at[0] - 4096 + J * HEADS]
        SLOT = NT * 67
        NODE = [arena[:, i * SLOT:(i + 1) * SLOT] for i in range(8)]
        key = HB[:, 0:J]
        WIDE = arena[:, at[0] - 4096:at[0]]

        class Order:
            def __init__(self, k, n):
                self.k, self.n = k, n
                self.key = key
                self.same = sb(f"same_{k}", [P, J], BF16)
                self.ends = sb(f"ends_{k}", [P, 8])
                self.equal = sb(f"equal_{k}", [P, P])
                self.all_equal = sb(f"all_equal_{k}", [P, P])
                self.last_row = sb(f"last_row_{k}", [P, P])
                self.join = sb(f"join_{k}", [P, 1], I32)
                self.first = sb(f"first_{k}", [P, 1], I32)
                self.last = sb(f"last_{k}", [P, 1], I32)
                self.end = sb(f"end_{k}", [P, NT], I32)
                self.start = sb(f"start_{k}", [P, NT], I32)
                self.count = sb(f"count_{k}", [P, NT])
                self.upto = sb(f"upto_{k}", [P, NT + 1])
                self.part = sb(f"part_{k}", [P, NT + 1])
                self.part_i = sb(f"part_i_{k}", [P, NT + 1], I32)
                self.keys = dram(f"keys_{k}", (P, J))
                self.upto_rows = dram(f"upto_rows_{k}", (NR, 1))

        OD, OS = Order("d", 0), Order("s", 1)
        idx = [sb(f"idx{b}", [P, CJ], I32) for b in range(2)]
        sidx = [sb(f"sidx{b}", [P, CJ], I32) for b in range(2)]
        moved = [sb(f"moved{b}", [P, 4 * CJ], I32) for b in range(2)]
        tally = sb("tally", [P, P])
        m0 = sb("m0", [P, 1])
        neg0 = sb("neg0", [P, 1])
        side = [sb(f"side{b}", [P, CJ * 4]) for b in range(2)]
        narrow = [sb(f"narrow{b}", [P, CJ * 2]) for b in range(2)]
        carry = sb("carry", [P, P])
        spread_carry = sb("spread_carry", [P, P])
        joined = sb("joined", [P, P])
        small = sb("small", [P, 16 * NT])
        spread_carry2 = sb("spread_carry2", [P, 67])
        sums = sb("sums", [P, 8 * 64])
        packT = [sb(f"packT{b}", [P, 512]) for b in range(2)]
        packB = [sb(f"packB{b}", [P, 512]) for b in range(2)]
        dis = sb("dis", [P, NT])
        rden = sb("rden", [P, NT])

        psT = [ctx.enter_context(nc.psum_tensor(f"psT{b}", [P, 512], F32)) for b in range(2)]
        psO = [ctx.enter_context(nc.psum_tensor(f"psO{b}", [P, 512], F32)) for b in range(2)]
        psB = [ctx.enter_context(nc.psum_tensor(f"psB{b}", [P, 512], F32)) for b in range(2)]
        psD = [ctx.enter_context(nc.psum_tensor(f"psD{b}", [P, 512], F32)) for b in range(2)]

        def rows(buf, f, n=CJ):
            return buf[:, 0:n * f].rearrange("p (j f) -> p j f", f=f)

        def nodes(i, f, off=0):
            return NODE[i][:, off:off + NT * f].rearrange("p (t f) -> p t f", f=f)

        def scalars(i):
            return small[:, i * NT:(i + 1) * NT]

        def over(col, f):
            return col.unsqueeze(2).broadcast_to([P, col.shape[1], f])

        def vec(name, n=NT, off=0, size=None):
            a, s = VAT[name]
            s = size or s
            return vectors[:, a + off:a + off + s].unsqueeze(1).broadcast_to([P, n, s])

        def edge_table(name, f):
            return dram(name, (ER, f))

        R = {f: dram(f"runs{f}", (EP + 1 + P, f)) for f in (1, 5, 32, 36, 64, 65, 128)}
        XQ, XM, XA, XA2, XF, XS = (edge_table(n, f) for n, f in
                                   (("xq", 32), ("xm", 4), ("xa", 1), ("xa2", 64), ("xf", 67), ("xs", 65)))
        KV, ZA, UD = dram("kv_rows", (EP, 64)), dram("za_rows", (EP, 65)), dram("ud_rows", (EP, 128))
        TB = {n: dram("t_" + n, (NR, f)) for n, f in
              (("kv", 64), ("q", 32), ("m", 4), ("za", 65), ("ad", 1), ("h", 64),
               ("ka", 128), ("a2", 64), ("k0", 64), ("k1", 64), ("dh1", 64), ("dp", 64), ("dst", 67),
               ("res0", 32), ("res1", 32), ("res2", 32), ("res3", 32), ("hin", 32), ("w2", 64), ("gs", 65),
               ("gcn1", 32), ("gcn2", 64), ("gcn3", 64), ("gcn4", 64), ("gcn5", 32))}
        SPREADS = [(XQ, 32), (XM, 4), (XA, 1), (XA2, 64), (XF, 67), (XS, 65)]
        FILLS = len(SPREADS) + 2 * len(R) - 6
        UG = CJ // 8
        SORT = [dram(f"sorted{i}", (EP, 4), I32) for i in range(3)]
        RANK, DST_S, POS_S = (dram(n, (P, J), I32) for n in ("rank_rows", "dst_s", "pos_s"))

        def by_edge(t, f):
            return t[0:EP, :].rearrange("(p j) f -> p j f", j=J)

        def by_node(t):
            return t.rearrange("(p t) f -> p (t f)", t=NT)

        def turned(buf, f, at=0):
            return buf[:, at * CJ:(at + f) * CJ].rearrange("p (f j) -> p j f", f=f)

        def by_feature(buf, f, at=0):
            return buf[:, at * CJ:(at + f) * CJ].rearrange("p (f j) -> p f j", f=f)

        def chunk(t, f, it, b):
            return by_edge(t, f)[:, bass.ds(it * (2 * CJ) + b * CJ, CJ), :]

        def cols(t, it, b, f=1):
            return t[:, bass.ds(it * (2 * CJ * f) + b * CJ * f, CJ * f)]

        PASSES = [("scores", 1, 1), ("soft", 2, 1), ("gcn1", 0, 1), ("gcn2", 0, 1), ("gcn3", 0, 1), ("gcn4", 0, 1),
                  ("gcn5", 0, 1), ("attend", 1, 1), ("hsum", 0, 1), ("umlp", 1, 2), ("upair", 0, 1), ("dh1", 0, 1),
                  ("grad", 1, 1), ("back", 2, 1), ("mean", 0, 1)]
        TURN = {n: k for k, (n, _, _) in enumerate(PASSES)}
        FREE = {n: TURN[n] * (IT + 1) for n in TURN}
        SCANNED = {n: TURN[n] * (2 * IT + 1) for n in TURN}
        PREPARED = {n: TURN[n] * 2 * IT for n in TURN}
        PASS_LOADS = {n: a for n, a, _ in PASSES}
        PASS_STORES = {n: a for n, _, a in PASSES}
        LOADED = {n: 16 * IT * sum(a for _, a, _ in PASSES[:TURN[n]]) for n in TURN}
        CREDIT = 16
        STORED = {n: CREDIT + 16 * IT * sum(a for _, _, a in PASSES[:TURN[n]]) for n in TURN}

        LOADS = ["x", "res0", "gcn1", "gcn2", "gcn3", "gcn4", "gcn5", "res1", "k1", "k0", "dpd", "dhu", "h", "za",
                 "gs", "res2", "hin", "res3"]
        GATHERS = ["scores", "gcn1", "gcn2", "gcn3", "gcn4", "gcn5", "attend", "hsum", "umlp", "upair", "dh1", "grad", "mean"]
        ROWS = {n: (k // 4, k % 4 * 16 * CJ * IT) for k, n in enumerate(GATHERS)}
        FED = {n: k * 16 * IT for k, n in enumerate(GATHERS)}

        PRODUCTS = [("kvq", 32), ("Wo", 32), ("L1_W1", 32), ("L1_W2", 64), ("L1_W3", 64), ("L1_W4", 64),
                    ("L1_W5", 64), ("fc_T", 32), ("h_p1", 64), ("A1", 64), ("h_p2", 64), ("A2", 64),
                    ("enc", 64), ("K_0", 64), ("K_1", 64), ("K_2", 64), ("KW", 64),
                    ("b_U2", 64), ("b_K2", 64), ("b_K1", 64), ("b_K0", 64), ("b_U0s", 64), ("b_p1", 64),
                    ("b_U0d", 64), ("b_p2", 64), ("b_enc", 64), ("b_fc", 64), ("b_D", 32), ("L3", 64)]
        ORDINAL = {n: k for k, (n, _) in enumerate(PRODUCTS)}
        WIDTH = {"kvq": 384, "L1_W1": 256, "fc_T": 256, "L1_W5": 64, "b_fc": 64, "L3": 64}

        def batches(name):
            n, per = NT // (P // dict(PRODUCTS)[name]), min(4, 512 // WIDTH.get(name, P))
            return [(g, min(per, n - g)) for g in range(0, n, per)]

        FIRST, total = {}, 0
        for name, _ in PRODUCTS:
            FIRST[name] = total
            total += len(batches(name))

        def product_pe(pe, name, weight, source, bias=None):
            k = FIRST[name]
            a, width = WAT[weight]
            todo = batches(name)
            pe.wait_ge(S["product_in"], ORDINAL[name] + 1)
            for i in range(len(todo) + 1):
                if i < len(todo):
                    if k + i >= 2:
                        pe.wait_ge(S["turned_copied"], k + i - 1)
                    for g in range(todo[i][1]):
                        at = (todo[i][0] + g) * P
                        last = pe.transpose(psT[(k + i) % 2][:, g * P:(g + 1) * P], source[:, at:at + P], ident[:])
                    last.then_inc(S["turned"], 1)
                if i >= 1:
                    h, n = k + i - 1, todo[i - 1][1]
                    pe.wait_ge(S["turned_copied"], h + 1)
                    if h >= 2:
                        pe.wait_ge(S["product_taken"], h - 1)
                    if bias is not None:
                        v, size = VAT[bias]
                        times = n * width // size
                        pe.matmul(psO[h % 2][:, 0:n * width].rearrange("p (t f) -> p t f", f=size), ones[0:1, :],
                                  vectors[0:1, v:v + size].unsqueeze(1).broadcast_to([1, times, size]),
                                  start=True, stop=False, skip_group_check=True)
                    for g in range(n):
                        last = pe.matmul(psO[h % 2][:, g * width:(g + 1) * width], packT[h % 2][:, g * P:(g + 1) * P],
                                         weights[:, a:a + width], start=bias is None, stop=True, skip_group_check=True)
                    last.then_inc(S["product"], 1)

        def product_act(act, name):
            k = FIRST[name]
            for i, (_, n) in enumerate(batches(name)):
                act.wait_ge(S["turned"], k + i + 1)
                if k + i >= 2:
                    act.wait_ge(S["product"], k + i - 1)
                act.copy(packT[(k + i) % 2][:, 0:n * P], psT[(k + i) % 2][:, 0:n * P]).then_inc(S["turned_copied"], 1)

        def product_dve(dve, name, take_out, cols_out):
            k, per = FIRST[name], P // dict(PRODUCTS)[name]
            for i, (g, n) in enumerate(batches(name)):
                dve.wait_ge(S["product"], k + i + 1)
                ps = psO[(k + i) % 2][:, 0:n * per * cols_out].rearrange("p (t f) -> p t f", f=cols_out)
                take_out(slice(g * per, (g + n) * per), ps).then_inc(S["product_taken"], 1)

        def plain(dst):
            return lambda t, ps: nc.vector.tensor_copy(dst[:, t, :], ps)

        def scaled(dst, col):
            return lambda t, ps: nc.vector.tensor_tensor(dst[:, t, :], ps, over(col[:, t], ps.shape[2]), ALU.mult)

        def relu_to(dst):
            return lambda t, ps: nc.vector.tensor_scalar(dst[:, t, :], ps, 0.0, None, ALU.max)

        def order_dve(dve, o):
            n = o.n
            dve.wait_ge(S["ends_read"], 16 * 3 * (n + 1))
            dve.tensor_tensor(o.same[:, 1:J], o.key[:, 1:J], o.key[:, 0:J - 1], ALU.is_equal)
            dve.tensor_tensor(o.same[:, 0:1], o.key[:, 0:1], o.ends[:, 0:1], ALU.is_equal)
            dve.tensor_copy(o.first[:], o.key[:, 0:1])
            dve.tensor_copy(o.last[:], o.key[:, J - 1:J])
            dve.tensor_tensor(o.ends[:, 3:4], o.key[:, J - 1:J], o.ends[:, 1:2], ALU.is_equal)
            dve.tensor_tensor(o.ends[:, 4:5], o.key[:, J - 1:J], o.ends[:, 2:3], ALU.not_equal)
            dve.tensor_scalar(joined[:], ident[:], o.key[:, J - 1:J], None, ALU.mult).then_inc(S["order_diag"], 1)
            dve.wait_ge(S["order_last_row"], n + 1)
            dve.tensor_copy(o.last_row[:], psB[0][:, 0:P])
            dve.drain()
            dve.tensor_scalar(o.all_equal[:], o.last_row[:], o.key[:, J - 1:J], None, ALU.is_equal)
            dve.tensor_scalar(o.equal[:], o.last_row[:], o.key[:, J - 1:J], o.ends[:, 3:4], ALU.is_equal, ALU.mult)
            dve.tensor_tensor(o.ends[:, 4:5], o.ends[:, 4:5], o.ends[:, 3:4], ALU.mult)
            for t in range(NT + 1):
                dve.tensor_scalar(carry[:], o.last_row[:], node_id[:, t:t + 1], 0.0, ALU.is_le, ALU.add,
                                  accum_out=o.part[:, t:t + 1])
                dve.drain()
            dve.tensor_scalar(o.part[:], o.part[:], float(P - 1), None, ALU.min)
            dve.drain()
            dve.tensor_copy(o.part_i[:], o.part[:]).then_inc(S["order_part"], 1)
            for t in range(NT + 1):
                dve.wait_ge(S[f"search{t % 4}"], 16 * (t // 4 + 1 + n * len(range(t % 4, NT + 1, 4))))
                dve.tensor_scalar(T[:, 0:J], WIDE[:, (t % 4) * J:(t % 4 + 1) * J], node_id[:, t:t + 1], 0.0,
                                  ALU.is_le, ALU.add, accum_out=o.upto[:, t:t + 1]).then_inc(S["searched"], 1)
                dve.drain()
            dve.scalar_tensor_tensor(o.upto[:], o.part[:], float(J), o.upto[:], ALU.mult, ALU.add)
            dve.drain()
            dve.tensor_tensor(o.count[:], o.upto[:, 1:], o.upto[:, 0:NT], ALU.subtract).then_inc(S["order_upto"], 1)
            dve.drain()
            has, a, b = scalars(0), scalars(1), scalars(2)
            spare, spares = scalars(3)[:, 0:1], scalars(4)
            dve.tensor_scalar(has, o.count[:], 0.0, None, ALU.is_gt)
            dve.tensor_scalar(spare, part_id[:], float(SPARE_ROW), None, ALU.add)
            dve.drain()
            dve.tensor_scalar(a, o.upto[:, 1:], float(-1 - ZERO_ROW), None, ALU.add)
            dve.tensor_scalar(spares, node_id[:, 1:], float(SPARE_ROW), None, ALU.add)
            dve.drain()
            dve.tensor_tensor(b, o.upto[:, 0:NT], spares, ALU.subtract)
            dve.drain()
            dve.tensor_tensor(a, a, has, ALU.mult)
            dve.tensor_tensor(b, b, has, ALU.mult)
            dve.drain()
            dve.tensor_scalar(o.end[:], a, float(ZERO_ROW), None, ALU.add)
            dve.tensor_tensor(o.start[:], b, spares, ALU.add)
            dve.wait_ge(S["order_join_end"], 16 * (n + 1))
            dve.tensor_scalar(o.ends[:, 5:6], o.ends[:, 6:7], -1.0, spare, ALU.add, ALU.subtract)
            dve.drain()
            dve.tensor_tensor(o.ends[:, 5:6], o.ends[:, 5:6], o.ends[:, 4:5], ALU.mult)
            dve.drain()
            dve.tensor_scalar(o.join[:], o.ends[:, 5:6], spare, None, ALU.add).then_inc(S["order_built"], 1)
            dve.drain()

        def keys_sp(sp, o):
            n = o.n
            sp.wait_ge(S["order_key"], n + 1)
            sp.dma_start(o.keys, o.key[:]).then_inc(S["order_keys"], 16)
            sp.wait_ge(S["order_keys"], 16 * (n + 1))
            sp.dma_start(o.ends[1:P, 0:1], o.keys[0:P - 1, J - 1:J], allow_slow_non_contiguous=True).then_inc(S["ends_read"], 16)
            sp.dma_start(o.ends[0:P - 1, 1:2], o.keys[1:P, 0:1], allow_slow_non_contiguous=True).then_inc(S["ends_read"], 16)
            sp.dma_start(o.ends[0:P - 1, 2:3], o.keys[1:P, J - 1:J], allow_slow_non_contiguous=True).then_inc(S["ends_read"], 16)

        def upto_sp(sp, o):
            n = o.n
            sp.wait_ge(S["order_upto"], n + 1)
            sp.dma_start(by_node(o.upto_rows), o.upto[:, 1:]).then_inc(S["order_upto_rows"], 16)

        def order_pe(pe, o):
            n = o.n
            pe.wait_ge(S["order_diag"], n + 1)
            pe.matmul(psB[0][:, 0:P], ones[:], joined[:], start=True, stop=True).then_inc(S["order_last_row"], 1)

        def order_pool(pool, o):
            n = o.n
            pool.wait_ge(S["order_keys"], 16 * (n + 1))
            pool.wait_ge(S["order_part"], n + 1)
            for t in range(NT + 1):
                if t >= 4:
                    pool.wait_ge(S["searched"], t - 3 + n * (NT + 1))
                fetch(pool, WIDE[:, (t % 4) * J:(t % 4 + 1) * J], o.keys, o.part_i[:, t:t + 1]).then_inc(S[f"search{t % 4}"], 16)
            pool.wait_ge(S["order_upto_rows"], 16 * (n + 1))
            fetch(pool, o.ends[:, 6:7], o.upto_rows, o.last[:]).then_inc(S["order_join_end"], 16)
            pool.wait_ge(S["order_built"], n + 1)

        def fetch(pool, dst, table, index):
            return pool.indirect_dma_start(dst, None, table, bass.IndirectOffsetOnAxis(ap=index, axis=0))

        def put(pool, table, index, source):
            return pool.indirect_dma_start(table, bass.IndirectOffsetOnAxis(ap=index, axis=0), source, None)

        def feed_sp(sp, name, index=None, loads=(), saved=False):
            with sp.Fori(0, IT) as it:
                for b in range(2):
                    sp.wait_ge(S[f"free{b}"], it + (FREE[name] + 1))
                    if saved:
                        sp.wait_ge(S[f"{name}_saved{b}"], it * 16 + CREDIT)
                    if index is not None:
                        sp.dma_start(idx[b][:], cols(index, it, b)).then_inc(S[f"fed{b}"], 16)
                    for table, f, buf in loads:
                        sp.dma_start(rows(buf[b], f), chunk(table, f, it, b)).then_inc(S[f"loaded{b}"], 16)

        def gather_pool(pool, name, table, f):
            with pool.Fori(0, IT) as it:
                for b in range(2):
                    pool.wait_ge(S[f"fed{b}"], it * 16 + (FED[name] + 16))
                    pool.sem_inc(S["gathering"], 1)
                    for j in range(CJ):
                        fetch(pool, G[b][:, j * f:(j + 1) * f], table, idx[b][:, j:j + 1]).then_inc(S[f"rows{ROWS[name][0]}{b}"], 16)

        def prepare_act(act, name, o, it, b, spread=0):
            c = it * 2 + (SCANNED[name] + b + 1)
            act.wait_ge(S["scanned"], c)
            same = cols(o.same, it, b)
            act.copy(by_feature(MR, 64)[:, :, 1:CJ], same[:, 1:CJ].unsqueeze(1).broadcast_to([P, 64, CJ - 1]))
            last = act.copy(m0[:], same[:, 0:1])
            if spread:
                k = PASS_LOADS[name]
                act.wait_ge(S[f"loaded{b}"], it * (16 * k) + (LOADED[name] + 16 * k))
                last = act.copy(by_feature(XP, spread), X[b][:, 0:CJ * spread].rearrange("p (j f) -> p f j", f=spread))
            last.then_inc(S["prepared"], 1)

        def finish_act(act, name, it, b, f, table, out=None):
            out = out or OUT
            act.wait_ge(S["scanned"], it * 2 + (SCANNED[name] + b + 2))
            act.wait_ge(S[f"stored{b}"], it * (16 * PASS_STORES[name]) + STORED[name])
            act.copy(rows(out[b], f), turned(M, f))
            act.drain()
            act.dma_start(chunk(table, f, it, b), rows(out[b], f)).then_inc(S[f"stored{b}"], 16)

        def plain_act(act, name, o, f, table):
            with act.Fori(0, IT) as it:
                for b in range(2):
                    prepare_act(act, name, o, it, b)
                    finish_act(act, name, it, b, f, table)

        def scan(dve, buf, f, kept, maxima=0, at=0):
            first = by_feature(buf, f, at)[:, :, 0]
            if maxima:
                dve.scalar_tensor_tensor(first[:, 0:maxima], kept[:, 0:maxima], neg0[:], first[:, 0:maxima], ALU.add, ALU.max)
            dve.scalar_tensor_tensor(first[:, maxima:f], kept[:, at + maxima:at + f], m0[:], first[:, maxima:f], ALU.mult, ALU.add)
            dve.drain()
            if maxima:
                run = buf[:, 0:maxima * CJ]
                dve.tensor_tensor_scan(run, T[:, 0:maxima * CJ], run, -BIG, ALU.add, ALU.max)
            for a in range(maxima, f, 64):
                n = min(f - a, 64)
                run = buf[:, (at + a) * CJ:(at + a + n) * CJ]
                dve.tensor_tensor_scan(run, MR[:, 0:n * CJ], run, 0.0, ALU.mult, ALU.add)
            dve.drain()
            return dve.tensor_copy(kept[:, at:at + f], by_feature(buf, f, at)[:, :, CJ - 1])

        def begin(dve, name, kept, maxima=0):
            dve.drain()
            dve.memset(by_feature(MR, 64)[:, :, 0], 0.0)
            dve.memset(kept, 0.0)
            if maxima:
                dve.drain()
                dve.memset(kept[:, 0:maxima], -BIG)
            dve.drain()
            dve.sem_inc(S["scanned"], 1)
            for b in range(2):
                dve.sem_inc(S[f"free{b}"], 1)

        def await_prepared(dve, name, it, b):
            dve.wait_ge(S["prepared"], it * 2 + (PREPARED[name] + b + 1))

        def plain_pass_dve(dve, name, f, weighted=False, beside=None, first=None):
            begin(dve, name, carry[:, 0:f])
            if first:
                first()
            with dve.Fori(0, IT) as it:
                for b in range(2):
                    g, m = rows(G[b], f), turned(M, f)
                    if weighted:
                        dve.tensor_copy(side[b][:, 0:CJ], cols(w_d, it, b))
                        dve.drain()
                    dve.wait_ge(S[f"rows{ROWS[name][0]}{b}"], it * (16 * CJ) + (ROWS[name][1] + 16 * CJ))
                    await_prepared(dve, name, it, b)
                    if weighted:
                        dve.tensor_tensor(m, g, over(side[b][:, 0:CJ], f), ALU.mult).then_inc(S[f"free{b}"], 1)
                    else:
                        dve.tensor_copy(m, g).then_inc(S[f"free{b}"], 1)
                    dve.drain()
                    scan(dve, M, f, carry).then_inc(S["scanned"], 1)
                    dve.drain()
                    if beside:
                        beside(dve, it, b)

        def ends_dve(dve, name, o, f, stores=1, maxima=0):
            for b in range(2):
                dve.wait_ge(S[f"stored{b}"], STORED[name] + 16 * IT * stores)
            if maxima:
                for h in range(maxima):
                    dve.tensor_scalar(T[:, h * P:(h + 1) * P], ident[:], carry[:, h:h + 1], None, ALU.mult)
                dve.tensor_scalar(HB[:, 0:P], o.all_equal[:], BIG, -BIG, ALU.mult, ALU.add)
                dve.drain()
            dve.sem_inc(S["carried"], 1)
            dve.wait_ge(S["crossed"], TURN[name] + 1)
            dve.wait_ge(S["join_read"], 16 * (TURN[name] + 1))
            if maxima:
                for h in range(maxima):
                    dve.tensor_tensor(T[:, h * P:(h + 1) * P], psB[0][:, h * P:(h + 1) * P], HB[:, 0:P], ALU.add)
                dve.drain()
                dve.tensor_reduce(sums[:, 0:maxima], T[:, 0:maxima * P].rearrange("p (h q) -> p h q", h=maxima),
                                  AX.X, ALU.max)
                dve.drain()
                dve.tensor_tensor(joined[:, 0:maxima], joined[:, 0:maxima], sums[:, 0:maxima], ALU.max)
            dve.tensor_tensor(joined[:, maxima:f], joined[:, maxima:f], psB[1][:, maxima:f], ALU.add)
            dve.drain()
            dve.sem_inc(S["join"], 1)
            dve.wait_ge(S["ends"], 16 * NT * (TURN[name] + 1))

        def ends_pe(pe, name, o, f, maxima=0):
            pe.wait_ge(S["carried"], TURN[name] + 1)
            if maxima:
                pe.matmul(psB[0][:, 0:maxima * P], ones[:], T[:, 0:maxima * P], start=True, stop=True)
            pe.matmul(psB[1][:, 0:f], o.equal[:], carry[:, 0:f], start=True, stop=True).then_inc(S["crossed"], 1)

        def ends_pool(pool, name, o, f, slot=0):
            pool.wait_ge(S["carried"], TURN[name] + 1)
            fetch(pool, joined[:, 0:f], R[f], o.join[:]).then_inc(S["join_read"], 16)
            pool.wait_ge(S["join"], TURN[name] + 1)
            put(pool, R[f], o.join[:], joined[:, 0:f]).then_inc(S["joined"], 16)
            pool.wait_ge(S["joined"], 16 * (TURN[name] + 1))
            for t in range(NT):
                fetch(pool, arena[:, slot * SLOT + t * f:slot * SLOT + (t + 1) * f], R[f], o.end[:, t:t + 1]).then_inc(S["ends"], 16)

        def spread_pool(pool, name, o, f, source, xtable):
            for t in range(NT):
                put(pool, xtable, o.start[:, t:t + 1], source[:, t * f:(t + 1) * f]).then_inc(S[f"{name}_spread"], 16)

        def spread_first_pool(pool, name, o, f, table, kept):
            fetch(pool, kept[:, 0:f], table, o.first[:]).then_inc(S[f"{name}_first"], 16)

        digit, running = T[:, 0:J], T[:, J:2 * J]
        rank, rank_i = HB[:, 0:J], HB[:, J:2 * J].bitcast(I32)
        hit_i = WIDE[:, 0:J].bitcast(I32)
        pay_i = WIDE[:, 0:4 * J].bitcast(I32)
        digit_i = HB[:, J:2 * J].bitcast(I32)
        VALUES = [LO, HI]

        def reload_digit(dve, n):
            dve.wait_ge(S["reloaded"], 16 * (n + 1))
            src = pay_i.rearrange("p (j f) -> p j f", f=4)[:, :, 0]
            if n == 0:
                dve.tensor_scalar(digit_i, src, LO - 1, None, ALU.bitwise_and)
            else:
                dve.tensor_scalar(digit_i, src, LO.bit_length() - 1, None, ALU.arith_shift_right)
            dve.drain()
            dve.tensor_copy(digit, digit_i)
            dve.drain()

        def count_step(dve, d):
            dve.tensor_scalar(running, digit, digits[:, bass.ds(d, 1)], 0.0, ALU.is_equal, ALU.add,
                              accum_out=tally[:, bass.ds(d, 1)])
            dve.drain()

        def count_steps(n):
            per = -(-VALUES[n] // (2 * IT))

            def beside(dve, it, b):
                for i in range(per):
                    count_step(dve, it * (2 * per) + (b * per + i))
            return beside

        def tallied_dve(dve, n):
            dve.drain()
            dve.sem_inc(S["counted"], 1)
            dve.wait_ge(S["summed"], n + 1)
            tot, run = joined[:, 0:VALUES[n]], tally[:, 0:VALUES[n]]
            dve.tensor_copy(tot, psD[1][:, 0:VALUES[n]])
            dve.drain()
            dve.tensor_tensor_scan(run, ones[:, 0:VALUES[n]], tot, 0.0, ALU.mult, ALU.add)
            dve.drain()
            dve.tensor_tensor(run, run, tot, ALU.subtract)
            dve.drain()
            dve.tensor_tensor(run, run, psD[1][:, P:P + VALUES[n]], ALU.add)
            dve.drain()

        def count_digit(dve, n):
            reload_digit(dve, n)
            with dve.Fori(0, VALUES[n]) as d:
                count_step(dve, d)
            tallied_dve(dve, n)

        def rank_digit(n):
            per = -(-VALUES[n] // (2 * IT))

            def beside(dve, it, b):
                for i in range(per):
                    d = bass.ds(it * (2 * per) + (b * per + i), 1)
                    dve.tensor_scalar(hit_i, digit, digits[:, d], None, ALU.is_equal)
                    dve.drain()
                    dve.tensor_tensor_scan(running, hit_i, hit_i, tally[:, d], ALU.add, ALU.max)
                    dve.drain()
                    dve.copy_predicated(rank, hit_i, running)
                    dve.drain()
            return beside

        def ranks_dve(dve, n):
            dve.tensor_scalar(rank_i, rank, -1.0, None, ALU.add)
            ready(dve, "ranked")

        def count_pe(pe, n):
            pe.wait_ge(S["counted"], n + 1)
            pe.matmul(psD[1][:, P:P + VALUES[n]], below[:], tally[:, 0:VALUES[n]], start=True, stop=True)
            pe.matmul(psD[1][:, 0:VALUES[n]], ones[:], tally[:, 0:VALUES[n]], start=True, stop=True).then_inc(S["summed"], 1)

        SLICES = {"gcn1": (0, 0, 6), "gcn2": (0, 6, IT - 6), "gcn4": (1, 0, 3), "gcn5": (1, 3, 5), "attend": (1, 8, IT - 8)}

        def scatter_sp(sp, n, first, count):
            if first == 0:
                sp.wait_ge(S["ranked"], n + 1)
                sp.dma_start(RANK, rank_i).then_inc(S["rank_rows"], 16)
                sp.wait_ge(S["rank_rows"], 16 * (n + 1))
            with sp.Fori(first, first + count) as it:
                for b in range(2):
                    sp.wait_ge(S[f"scatter_room{b}"], it + (n * (IT + 1) + 1))
                    sp.dma_start(sidx[b][:], cols(RANK, it, b)).then_inc(S[f"scatter_fed{b}"], 16)
                    sp.dma_start(moved[b][:].rearrange("p (j f) -> p j f", f=4), chunk(SORT[n], 4, it, b)).then_inc(S[f"scatter_fed{b}"], 16)

        def scatter_pool(pool, n, first, count):
            if first == 0:
                for b in range(2):
                    pool.sem_inc(S[f"scatter_room{b}"], 1)
            with pool.Fori(first, first + count) as it:
                for b in range(2):
                    pool.wait_ge(S[f"scatter_fed{b}"], it * 32 + (n * 32 * IT + 32))
                    pool.sem_inc(S["scattering"], 1)
                    for j in range(CJ):
                        put(pool, SORT[n + 1], sidx[b][:, j:j + 1], moved[b][:, 4 * j:4 * j + 4]).then_inc(S[f"scattered{b}"], 16)
                for b in range(2):
                    pool.wait_ge(S[f"scattered{b}"], it * (16 * CJ) + (n * 16 * CJ * IT + 16 * CJ))
                    pool.sem_inc(S[f"scatter_room{b}"], 1)

        def reload_sp(sp, n, rows_from):
            if n == 0:
                sp.wait_ge(S["unsorted"], 16)
            else:
                sp.wait_ge(S["ranked"], n)
                for b in range(2):
                    sp.wait_ge(S[f"scatter_room{b}"], n * (IT + 1))
            sp.dma_start(pay_i, rows_from.rearrange("(p j) f -> p (j f)", j=J)).then_inc(S["reloaded"], 16)

        def norm_relu(dve, n, dst, src, tmp):
            s0, s1, s2 = scalars(0), scalars(1), scalars(2)
            dve.tensor_reduce(s0, src, AX.X, ALU.add)
            dve.drain()
            dve.tensor_scalar(s0, s0, 1.0 / 32, None, ALU.mult)
            dve.drain()
            dve.tensor_tensor(dst, src, over(s0, 32), ALU.subtract)
            dve.drain()
            dve.tensor_tensor(tmp, dst, dst, ALU.mult)
            dve.drain()
            dve.tensor_reduce(s1, tmp, AX.X, ALU.add)
            dve.drain()
            dve.tensor_scalar(s1, s1, 1.0 / 32, EPS, ALU.mult, ALU.add).then_inc(S["variance"], 1)
            dve.wait_ge(S["deviation"], n)
            dve.reciprocal(s2, s2)
            dve.drain()
            dve.tensor_tensor(dst, dst, over(s2, 32), ALU.mult)
            dve.drain()
            dve.tensor_scalar(dst, dst, 0.0, None, ALU.max)
            dve.drain()

        def deviation_act(act, n):
            act.wait_ge(S["variance"], n)
            act.activation(scalars(2), scalars(1), ACT.Sqrt).then_inc(S["deviation"], 1)

        def graph_norm(dve, layer, v, f, tmp):
            i = f"{layer}"
            col = lambda k: sums[:, k * 64:k * 64 + f]
            row = lambda k: col(k).unsqueeze(1).broadcast_to([P, NT, f])
            by_feature = lambda a: a.rearrange("p t f -> p f t")
            dve.tensor_tensor(v, v, vec(f"L1_gnn_b{i}"), ALU.add)
            dve.drain()
            dve.tensor_tensor(tmp, v, over(valid[:], f), ALU.mult)
            dve.drain()
            dve.tensor_reduce(col(0), by_feature(tmp), AX.X, ALU.add).then_inc(S["part_sum"], 1)
            dve.wait_ge(S["node_sum"], 2 * layer - 1)
            a, _ = VAT[f"L1_gnn_g{i}a"]
            w, _ = VAT[f"L1_gnn_g{i}w"]
            dve.scalar_tensor_tensor(col(1), psD[0][:, 0:f], 1.0 / N, vectors[:, a:a + f], ALU.mult, ALU.mult)
            dve.drain()
            dve.tensor_tensor(v, v, row(1), ALU.subtract)
            dve.drain()
            dve.tensor_tensor(tmp, v, over(valid[:], f), ALU.mult)
            dve.drain()
            dve.tensor_tensor(tmp, tmp, tmp, ALU.mult)
            dve.drain()
            dve.tensor_reduce(col(0), by_feature(tmp), AX.X, ALU.add).then_inc(S["part_sum"], 1)
            dve.wait_ge(S["node_sum"], 2 * layer)
            dve.tensor_scalar(col(2), psD[0][:, 0:f], 1.0 / N, EPS, ALU.mult, ALU.add).then_inc(S["graph_var"], 1)
            dve.wait_ge(S["graph_std"], layer)
            dve.reciprocal(col(3), col(3))
            dve.drain()
            dve.tensor_tensor(col(3), col(3), vectors[:, w:w + f], ALU.mult)
            dve.drain()
            dve.tensor_tensor(v, v, row(3), ALU.mult)
            dve.drain()
            dve.tensor_tensor(v, v, vec(f"L1_gnn_g{i}b"), ALU.add)
            dve.drain()

        def graph_norm_pe(pe, layer, f):
            for k in (2 * layer - 1, 2 * layer):
                pe.wait_ge(S["part_sum"], k)
                pe.matmul(psD[0][:, 0:f], ones[:], sums[:, 0:f], start=True, stop=True).then_inc(S["node_sum"], 1)

        def graph_norm_act(act, layer, f):
            act.wait_ge(S["graph_var"], layer)
            act.activation(sums[:, 192:192 + f], sums[:, 128:128 + f], ACT.Sqrt).then_inc(S["graph_std"], 1)

        def ready(dve, name):
            dve.drain()
            dve.sem_inc(S[name], 1)

        def flat(i, f):
            return NODE[i][:, 0:NT * f]

        def store_node(sp, name, table, i, f, nth=1):
            sp.wait_ge(S[f"{name}_made"], nth)
            sp.dma_start(by_node(table), flat(i, f)).then_inc(S[f"{name}_kept"], 16)

        def load_node(sp, name, table, i, f, kept, nth=1):
            sp.wait_ge(S[kept], 16 * nth)
            sp.wait_ge(S["room"], LOADS.index(name) + 1)
            sp.dma_start(flat(i, f), by_node(table)).then_inc(S["back"], 16)

        def fetch_back(dve, name):
            ready(dve, "room")
            dve.wait_ge(S["back"], 16 * (LOADS.index(name) + 1))

        W_SRC = VAT["L2_gnn_W_attn"][0]

        block = ctx.enter_context(nc.Block())

        @block.vector
        def _(dve):
            dve.wait_ge(S["weights"], 32)
            dve.memset(ones[:], 1.0)
            dve.memset(G[0], 0.0)
            dve.memset(half[:], 0.5)
            dve.memset(tally[:], 0.0)
            for o in (OD, OS):
                dve.memset(o.ends[:], -1.0)
            dve.wait_ge(S["iotas"], 1)
            dve.tensor_scalar(valid[:], node_id[:, 1:], float(N), None, ALU.is_lt)
            dve.tensor_scalar(below[:], digits[:], part_id[:], None, ALU.is_gt)
            dve.tensor_scalar(ident[:], digits[:], part_id[:], None, ALU.is_equal)
            ready(dve, "zeros")
            dve.wait_ge(S["edges"], 16 * 3)
            pay = pay_i.rearrange("p (j f) -> p j f", f=4)
            for k, column in enumerate((T[:, 0:J], T[:, J:2 * J], HB[:, J:2 * J])):
                dve.tensor_copy(pay[:, :, k], column.bitcast(I32))
            dve.memset(pay[:, :, 3], 0)
            dve.tensor_copy(key, T[:, J:2 * J].bitcast(I32))
            ready(dve, "payload")
            dve.sem_inc(S["order_key"], 1)
            order_dve(dve, OD)

            fetch_back(dve, "x")
            x, h = nodes(0, 32), nodes(1, 32)
            norm_relu(dve, 1, h, x, nodes(2, 32))
            ready(dve, "product_in")
            kv, q = nodes(2, 64), nodes(3, 32)

            def split_kvq(t, ps):
                dve.tensor_copy(kv[:, t, :], ps[:, :, 0:64])
                return dve.tensor_copy(q[:, t, :], ps[:, :, 64:96])
            product_dve(dve, "kvq", split_kvq, 96)
            dve.tensor_tensor(x, x, h, ALU.add)
            ready(dve, "kv_made")
            ready(dve, "q_made")
            ready(dve, "res0_made")
            for name in ("kv_kept", "q_kept", "res0_kept"):
                dve.wait_ge(S[name], 16)
            dve.wait_ge(S["scores_spread"], 16 * NT)
            dve.wait_ge(S["scores_first"], 16)

            dve.wait_ge(S["filled"], 16 * FILLS)
            begin(dve, "scores", carry[:, 0:5], maxima=4)
            with dve.Fori(0, IT) as it:
                for b in range(2):
                    dve.wait_ge(S[f"rows{ROWS["scores"][0]}{b}"], it * (16 * CJ) + (ROWS["scores"][1] + 16 * CJ))
                    await_prepared(dve, "scores", it, b)
                    dve.tensor_scalar(T[:, 0:HEADS * CJ], MR[:, 0:HEADS * CJ], BIG, -BIG, ALU.mult, ALU.add)
                    dve.tensor_scalar(neg0[:], m0[:], BIG, -BIG, ALU.mult, ALU.add)
                    scan(dve, XP, 32, spread_carry)
                    dve.tensor_tensor(rows(HB, 32), turned(XP, 32), rows(G[b], 64)[:, :, 0:32], ALU.mult).then_inc(S[f"free{b}"], 1)
                    dve.drain()
                    dve.tensor_reduce(side[b][:, 0:CJ * HEADS],
                                      HB[:, 0:CJ * 32].rearrange("p (n d) -> p n d", d=DH), AX.X, ALU.add)
                    dve.drain()
                    dve.tensor_scalar(cols(score, it, b, HEADS), side[b][:, 0:CJ * HEADS], float(DH ** -0.5), None, ALU.mult)
                    dve.tensor_scalar(by_feature(M, HEADS), side[b][:, 0:CJ * HEADS].rearrange("p (j h) -> p h j", h=HEADS),
                                      float(DH ** -0.5), None, ALU.mult)
                    dve.tensor_copy(M[:, HEADS * CJ:(HEADS + 1) * CJ], cols(w_d, it, b))
                    dve.drain()
                    scan(dve, M, 5, carry, maxima=4).then_inc(S["scanned"], 1)
                    dve.drain()
            for b in range(2):
                dve.wait_ge(S[f"scores_saved{b}"], CREDIT + 16 * IT)
            ends_dve(dve, "scores", OD, 5, maxima=4)
            ends = nodes(0, 5)
            s0, s1 = scalars(0), scalars(1)
            dve.tensor_copy(nodes(1, 4), ends[:, :, 0:4])
            dve.tensor_scalar(s0, ends[:, :, 4], 1.0, None, ALU.add)
            ready(dve, "m_made")
            dve.tensor_scalar(s1, s0, 1e-12, None, ALU.max)
            dve.tensor_scalar(scalars(3), s0, 0.0, None, ALU.is_gt)
            ready(dve, "degree")
            dve.wait_ge(S["degree_root"], 1)
            dve.reciprocal(scalars(2), scalars(2))
            dve.drain()
            dve.tensor_tensor(dis[:], scalars(2), scalars(3), ALU.mult)
            dve.drain()
            dve.wait_ge(S["m_kept"], 16)
            dve.wait_ge(S["soft_spread"], 16 * NT)
            dve.wait_ge(S["soft_first"], 16)

            begin(dve, "soft", carry[:, 0:36])
            with dve.Fori(0, IT) as it:
                for b in range(2):
                    await_prepared(dve, "soft", it, b)
                    dve.wait_ge(S[f"loaded{b}"], it * 32 + (LOADED["soft"] + 32))
                    g = rows(G[b], 64)
                    scan(dve, XP, 4, spread_carry)
                    dve.tensor_tensor(side[b][:, 0:CJ * HEADS].rearrange("p (j h) -> p j h", h=HEADS),
                                      cols(score, it, b, HEADS).rearrange("p (j h) -> p j h", h=HEADS), turned(XP, HEADS),
                                      ALU.subtract).then_inc(S["soft_shifted"], 1)
                    dve.wait_ge(S["soft_exp"], it * 2 + (b + 1))
                    e = rows(side[b], HEADS)
                    dve.tensor_tensor(M[:, 0:32 * CJ].rearrange("p (h d j) -> p j h d", h=HEADS, d=DH),
                                      g[:, :, 32:64].rearrange("p j (h d) -> p j h d", d=DH),
                                      e.unsqueeze(3).broadcast_to([P, CJ, HEADS, DH]), ALU.mult)
                    dve.tensor_copy(turned(M, HEADS, 32), e).then_inc(S[f"free{b}"], 1)
                    dve.drain()
                    scan(dve, M, 36, carry).then_inc(S["scanned"], 1)
                    dve.drain()
            ends_dve(dve, "soft", OD, 36)
            ends, attn = nodes(0, 36), nodes(1, 32)
            den = nodes(2, 4)
            dve.tensor_scalar(den, ends[:, :, 32:36], 1e-16, None, ALU.max)
            dve.drain()
            dve.reciprocal(den, den)
            dve.drain()
            dve.tensor_tensor(attn.rearrange("p t (h d) -> p t h d", d=DH),
                              ends[:, :, 0:32].rearrange("p t (h d) -> p t h d", d=DH),
                              den.unsqueeze(3).broadcast_to([P, NT, HEADS, DH]), ALU.mult)
            ready(dve, "product_in")
            x1, h = nodes(3, 32), nodes(5, 32)
            product_dve(dve, "Wo", plain(nodes(2, 32)), 32)
            fetch_back(dve, "res0")
            dve.tensor_tensor(x1, x1, nodes(2, 32), ALU.add)
            dve.drain()
            dve.sem_inc(S["res1_made"], 1)
            norm_relu(dve, 2, h, x1, nodes(6, 32))

            dve.tensor_tensor(nodes(1, 32), h, over(dis[:], 32), ALU.mult)
            ready(dve, "gcn_made")
            dve.wait_ge(S["gcn_kept"], 16)
            dve.wait_ge(S["res1_kept"], 16)
            for layer in range(1, 6):
                f = 32 if layer in (1, 5) else 64
                name = f"gcn{layer}"
                if layer == 3:
                    reload_digit(dve, 1)
                plain_pass_dve(dve, name, f, weighted=True, first={1: lambda: count_digit(dve, 0)}.get(layer),
                               beside={1: rank_digit(0), 3: count_steps(1), 4: rank_digit(1)}.get(layer))
                if layer == 3:
                    tallied_dve(dve, 1)
                if layer in (1, 4):
                    ranks_dve(dve, layer // 4)
                ends_dve(dve, name, OD, f)
                fetch_back(dve, name)
                agg = nodes(2, f)
                dve.tensor_tensor(agg, nodes(0, f), nodes(1, f), ALU.add)
                dve.drain()
                dve.tensor_tensor(agg, agg, over(dis[:], f), ALU.mult)
                dve.drain()
                if layer == 1:
                    ready(dve, "product_in")
                    agg = nodes(3, 64)
                    product_dve(dve, "L1_W1", plain(agg), 64)
                    dve.drain()
                    f = 64
                graph_norm(dve, layer, agg, f, nodes(4, f))
                if layer < 5:
                    dve.tensor_scalar(nodes(5, 64), agg, 0.0, None, ALU.max)
                    nxt = layer + 1
                    fo = 32 if nxt == 5 else 64
                    ready(dve, "product_in")
                    product_dve(dve, f"L1_W{nxt}", scaled(nodes(1, fo), dis), fo)
                    ready(dve, "gcn_made")
                    dve.wait_ge(S["gcn_kept"], 16 * nxt)
            fetch_back(dve, "res1")
            x2, h = nodes(3, 32), nodes(1, 32)
            dve.tensor_tensor(x2, x2, nodes(2, 32), ALU.add)
            dve.drain()
            dve.sem_inc(S["res2_made"], 1)
            norm_relu(dve, 3, h, x2, nodes(4, 32))

            ready(dve, "product_in")
            z, za = nodes(2, 64), nodes(4, 65)
            product_dve(dve, "fc_T", plain(z), 64)
            dve.drain()
            a_s, a_d = scalars(4), scalars(5)
            for part, a in ((0, a_s), (64, a_d)):
                dve.tensor_tensor(nodes(5, 64), z, vec("L2_gnn_W_attn", off=part, size=64), ALU.mult)
                dve.drain()
                dve.tensor_reduce(a, nodes(5, 64), AX.X, ALU.add)
                dve.drain()
            dve.tensor_copy(za[:, :, 0:64], z)
            dve.tensor_copy(za[:, :, 64], a_s)
            ready(dve, "za_made")
            for name in ("za_kept", "ad_kept", "res2_kept", "attend_first"):
                dve.wait_ge(S[name], 16)
            dve.wait_ge(S["attend_spread"], 16 * NT)
            begin(dve, "attend", carry[:, 0:65])
            with dve.Fori(0, IT) as it:
                for b in range(2):
                    dve.wait_ge(S[f"rows{ROWS["attend"][0]}{b}"], it * (16 * CJ) + (ROWS["attend"][1] + 16 * CJ))
                    await_prepared(dve, "attend", it, b)
                    g = rows(G[b], 65)
                    scan(dve, XP, 1, spread_carry)
                    dve.tensor_tensor(side[b][:, 0:CJ], XP[:, 0:CJ], g[:, :, 64], ALU.add).then_inc(S["attend_sum"], 1)
                    dve.wait_ge(S["attend_exp"], it * 2 + (b + 1))
                    dve.tensor_copy(M[:, 64 * CJ:65 * CJ], narrow[b][:, CJ:2 * CJ])
                    dve.tensor_tensor(turned(M, 64), g[:, :, 0:64], over(narrow[b][:, CJ:2 * CJ], 64),
                                      ALU.mult).then_inc(S[f"free{b}"], 1)
                    dve.drain()
                    scan(dve, M, 65, carry).then_inc(S["scanned"], 1)
                    dve.drain()
            for b in range(2):
                dve.wait_ge(S[f"attend_saved{b}"], CREDIT + 16 * IT)
            ends_dve(dve, "attend", OD, 65)
            ends, h = nodes(0, 65), nodes(1, 64)
            dve.tensor_scalar(rden[:], ends[:, :, 64], 1e-30, None, ALU.max)
            dve.drain()
            dve.reciprocal(rden[:], rden[:])
            dve.drain()
            dve.tensor_tensor(h, ends[:, :, 0:64], over(rden[:], 64), ALU.mult)
            ready(dve, "h_made")
            dve.sem_inc(S["product_in"], 1)
            product_dve(dve, "h_p1", plain(nodes(2, 64)), 64)
            ready(dve, "product_in")
            product_dve(dve, "A1", plain(nodes(3, 64)), 64)
            ready(dve, "A1_made")
            dve.sem_inc(S["product_in"], 1)
            product_dve(dve, "h_p2", plain(nodes(2, 64)), 64)
            ready(dve, "product_in")
            product_dve(dve, "A2", plain(nodes(4, 64)), 64)
            ready(dve, "A2_made")
            for name in ("h_kept", "A1_kept", "A2_kept", "umlp_first"):
                dve.wait_ge(S[name], 16)
            dve.wait_ge(S["umlp_spread"], 16 * NT)
            dve.wait_ge(S["reloaded"], 16 * 3)
            pay = pay_i.rearrange("p (j f) -> p j f", f=4)
            dve.tensor_copy(T[:, 0:J].bitcast(I32), pay[:, :, 1])
            dve.tensor_copy(T[:, J:2 * J].bitcast(I32), pay[:, :, 2])
            dve.tensor_copy(key, pay[:, :, 0])
            ready(dve, "payload")
            dve.sem_inc(S["order_key"], 1)
            dve.wait_ge(S["s_rows"], 32)
            order_dve(dve, OS)
            plain_pass_dve(dve, "hsum", 64)
            ends_dve(dve, "hsum", OD, 64)
            ready(dve, "product_in")
            h1 = nodes(1, 64)
            product_dve(dve, "enc", plain(h1), 64)
            dve.tensor_tensor(nodes(2, 64), over(OD.count[:], 64), vec("L2_gnn_b_encK"), ALU.mult)
            dve.drain()
            dve.tensor_tensor(h1, h1, nodes(2, 64), ALU.add)
            ready(dve, "product_in")
            product_dve(dve, "K_0", plain(nodes(2, 64)), 64)
            ready(dve, "k0_raw")
            dve.wait_ge(S["product_in"], ORDINAL["K_1"] + 1)
            product_dve(dve, "K_1", relu_to(nodes(3, 64)), 64)
            ready(dve, "product_in")
            dve.sem_inc(S["k01_made"], 1)
            product_dve(dve, "K_2", plain(nodes(4, 64)), 64)
            ready(dve, "product_in")
            product_dve(dve, "KW", plain(nodes(5, 64)), 64)
            ready(dve, "KW_made")
            for name in ("k0_kept", "k1_kept", "KW_kept"):
                dve.wait_ge(S[name], 16)

            begin(dve, "umlp", carry[:, 0:64])
            with dve.Fori(0, IT) as it:
                for b in range(2):
                    dve.wait_ge(S[f"rows{ROWS["umlp"][0]}{b}"], it * (16 * CJ) + (ROWS["umlp"][1] + 16 * CJ))
                    await_prepared(dve, "umlp", it, b)
                    g, out_rows, tb, hb = rows(G[b], 128), rows(OUT[b], 128), rows(T, 64), rows(HB, 64)
                    scan(dve, XP, 64, spread_carry)
                    dve.tensor_tensor(tb, turned(XP, 64), g[:, :, 64:128], ALU.add).then_inc(S["umlp_pre"], 1)
                    dve.wait_ge(S["umlp_tanh"], it * 2 + (b + 1))
                    slope = rows(XP, 64)
                    dve.scalar_tensor_tensor(slope, tb, -1.0, tb, ALU.mult, ALU.mult)
                    for u in range(UG):
                        k = b * UG + u
                        t = slice(8 * u, 8 * u + 8)
                        dve.wait_ge(S["umlp_relu"], it * (2 * UG) + (k + 3))
                        dve.scalar_tensor_tensor(hb[:, t, :], out_rows[:, t, 0:64], 0.0, g[:, t, 0:64], ALU.is_gt,
                                                 ALU.mult).then_inc(S["umlp_slope"], 1)
                    for u in range(UG):
                        k = b * UG + u
                        t = slice(8 * u, 8 * u + 8)
                        dve.wait_ge(S["umlp_down"], it * (2 * UG) + (k + 1))
                        ps = psD[k % 2][:, 0:512].rearrange("p (j f) -> p j f", f=64)
                        dve.scalar_tensor_tensor(out_rows[:, t, 64:128], slope[:, t, :], 1.0, ps, ALU.add,
                                                 ALU.mult).then_inc(S["umlp_taken"], 1)
                    dve.drain()
                    dve.tensor_copy(turned(M, 64), out_rows[:, :, 64:128]).then_inc(S[f"free{b}"], 1)
                    dve.drain()
                    scan(dve, M, 64, carry).then_inc(S["scanned"], 1)
                    dve.drain()
            ends_dve(dve, "umlp", OD, 64, stores=2)
            ready(dve, "dpd_made")
            dve.wait_ge(S["dpd_kept"], 16)

            plain_pass_dve(dve, "upair", 128)
            ends_dve(dve, "upair", OS, 128)
            both = arena[:, 0:NT * 128].rearrange("p (t f) -> p t f", f=128)
            dve.tensor_copy(nodes(2, 64), both[:, :, 0:64])
            dve.tensor_copy(nodes(3, 64), both[:, :, 64:128])
            ready(dve, "product_in")
            product_dve(dve, "b_U2", plain(nodes(5, 64)), 64)
            dve.tensor_tensor(nodes(6, 64), over(OS.count[:], 64), vec("L2_gnn_U_b2"), ALU.mult)
            dve.drain()
            dve.tensor_tensor(nodes(5, 64), nodes(5, 64), nodes(6, 64), ALU.add)
            ready(dve, "product_in")
            product_dve(dve, "b_K2", plain(nodes(6, 64)), 64)
            fetch_back(dve, "k1")
            dve.scalar_tensor_tensor(nodes(6, 64), nodes(7, 64), 0.0, nodes(6, 64), ALU.is_gt, ALU.mult)
            ready(dve, "product_in")
            product_dve(dve, "b_K1", plain(nodes(2, 64)), 64)
            fetch_back(dve, "k0")
            dve.tensor_tensor(nodes(5, 64), nodes(5, 64), nodes(5, 64), ALU.mult)
            dve.drain()
            dve.tensor_scalar(nodes(5, 64), nodes(5, 64), -1.0, 1.0, ALU.mult, ALU.add)
            dve.drain()
            dve.tensor_tensor(nodes(2, 64), nodes(2, 64), nodes(5, 64), ALU.mult)
            ready(dve, "product_in")
            product_dve(dve, "b_K0", plain(nodes(6, 64)), 64)
            ready(dve, "dh1_made")
            dve.sem_inc(S["product_in"], 1)
            product_dve(dve, "b_U0s", plain(nodes(2, 64)), 64)
            ready(dve, "product_in")
            product_dve(dve, "b_p1", plain(nodes(5, 64)), 64)
            fetch_back(dve, "dpd")
            dve.sem_inc(S["product_in"], 1)
            product_dve(dve, "b_U0d", plain(nodes(2, 64)), 64)
            ready(dve, "product_in")
            product_dve(dve, "b_p2", plain(nodes(7, 64)), 64)
            dve.drain()
            dve.tensor_tensor(nodes(5, 64), nodes(5, 64), nodes(7, 64), ALU.add)
            ready(dve, "dhu_made")
            for name in ("dh1_kept", "dhu_kept"):
                dve.wait_ge(S[name], 16)
            plain_pass_dve(dve, "dh1", 64)
            ends_dve(dve, "dh1", OS, 64)
            ready(dve, "product_in")
            dh = nodes(1, 64)
            product_dve(dve, "b_enc", plain(dh), 64)
            fetch_back(dve, "dhu")
            fetch_back(dve, "h")
            fetch_back(dve, "za")
            dve.tensor_tensor(dh, dh, nodes(2, 64), ALU.add)
            dve.drain()
            dve.tensor_tensor(nodes(3, 64), nodes(3, 64), dh, ALU.mult)
            dve.drain()
            c = scalars(6)
            dve.tensor_reduce(c, nodes(3, 64), AX.X, ALU.add)
            dve.drain()
            back = nodes(4, 67)
            dve.tensor_copy(back[:, :, 0:64], dh)
            dve.tensor_copy(back[:, :, 64], a_d)
            dve.tensor_copy(back[:, :, 65], c)
            dve.tensor_copy(back[:, :, 66], rden[:])
            ready(dve, "grad_made")
            for name in ("grad_kept", "grad_first", "back_first"):
                dve.wait_ge(S[name], 16)
            for name in ("grad_spread", "back_spread"):
                dve.wait_ge(S[name], 16 * NT)

            def softmax_back(name, kept, f, sums_of):
                by_src = name == "grad"
                begin(dve, name, carry[:, 0:sums_of])
                with dve.Fori(0, IT) as it:
                    for b in range(2):
                        if by_src:
                            dve.wait_ge(S[f"rows{ROWS["grad"][0]}{b}"], it * (16 * CJ) + (ROWS["grad"][1] + 16 * CJ))
                        else:
                            dve.wait_ge(S[f"loaded{b}"], it * 32 + (LOADED["back"] + 32))
                        await_prepared(dve, name, it, b)
                        scan(dve, XP, f, kept)
                        dve.drain()
                        zr, dr = (turned(XP, 65), rows(G[b], 67)) if by_src else (rows(G[b], 65), turned(XP, 67))
                        u, w, t = side[b], narrow[b][:, CJ:2 * CJ], narrow[b][:, 0:CJ]
                        dalpha, alpha, slope = u[:, CJ:2 * CJ], u[:, 2 * CJ:3 * CJ], u[:, 3 * CJ:4 * CJ]
                        dve.tensor_tensor(u[:, 0:CJ], zr[:, :, 64], dr[:, :, 64], ALU.add).then_inc(S[f"{name}_sum"], 1)
                        dve.tensor_tensor(rows(T, 64), zr[:, :, 0:64], dr[:, :, 0:64], ALU.mult)
                        dve.drain()
                        dve.tensor_reduce(dalpha, rows(T, 64), AX.X, ALU.add)
                        dve.drain()
                        dve.wait_ge(S[f"{name}_exp"], it * 2 + (b + 1))
                        dve.tensor_tensor(alpha, w, dr[:, :, 66], ALU.mult)
                        dve.tensor_tensor(dalpha, dalpha, dr[:, :, 65], ALU.subtract)
                        dve.tensor_tensor(slope, t, t, ALU.mult)
                        dve.drain()
                        dve.tensor_tensor(dalpha, dalpha, alpha, ALU.mult)
                        dve.tensor_scalar(slope, slope, -0.25, 0.25, ALU.mult, ALU.add)
                        if by_src:
                            dve.tensor_tensor(turned(M, 64), dr[:, :, 0:64], over(alpha, 64), ALU.mult)
                        dve.drain()
                        at = (sums_of - 1) * CJ
                        dve.tensor_tensor(M[:, at:at + CJ], dalpha, slope, ALU.mult).then_inc(S[f"free{b}"], 1)
                        dve.drain()
                        scan(dve, M, sums_of, carry).then_inc(S["scanned"], 1)
                        dve.drain()

            softmax_back("grad", spread_carry, 65, 65)
            ends_dve(dve, "grad", OS, 65)
            ready(dve, "gs_made")
            dve.wait_ge(S["gs_kept"], 16)

            softmax_back("back", spread_carry2, 67, 1)
            ends_dve(dve, "back", OD, 1)
            fetch_back(dve, "gs")
            gs, dz = nodes(1, 65), nodes(2, 64)
            dve.tensor_copy(scalars(7), gs[:, :, 64])
            dve.drain()
            dve.tensor_tensor(nodes(3, 64), over(scalars(7), 64), vec("L2_gnn_W_attn", off=0, size=64), ALU.mult)
            dve.tensor_tensor(nodes(4, 64), over(NODE[0][:, 0:NT], 64), vec("L2_gnn_W_attn", off=64, size=64), ALU.mult)
            dve.drain()
            dve.tensor_tensor(dz, gs[:, :, 0:64], nodes(3, 64), ALU.add)
            dve.drain()
            dve.tensor_tensor(dz, dz, nodes(4, 64), ALU.add)
            ready(dve, "product_in")
            y, yd, t2 = nodes(3, 32), nodes(4, 32), nodes(5, 32)
            product_dve(dve, "b_fc", plain(y), 32)
            ready(dve, "product_in")
            product_dve(dve, "b_D", plain(yd), 32)
            dve.drain()
            dve.tensor_tensor(t2[:, :, 0:16], y[:, :, 16:32], yd[:, :, 0:16], ALU.subtract)
            dve.scalar_tensor_tensor(t2[:, :, 16:32], y[:, :, 0:16], -1.0, yd[:, :, 16:32], ALU.mult, ALU.subtract)
            fetch_back(dve, "res2")
            x3, h = nodes(6, 32), nodes(1, 32)
            dve.tensor_tensor(x3, x3, t2, ALU.add)
            dve.drain()
            dve.sem_inc(S["res3_made"], 1)
            norm_relu(dve, 4, h, x3, nodes(2, 32))

            ready(dve, "hin_made")
            dve.wait_ge(S["hin_kept"], 16)
            dve.wait_ge(S["res3_kept"], 16)
            plain_pass_dve(dve, "mean", 32)
            ends_dve(dve, "mean", OD, 32)
            fetch_back(dve, "hin")
            cat = nodes(2, 64)
            dve.tensor_scalar(scalars(0), OD.count[:], 1.0, None, ALU.max)
            dve.drain()
            dve.reciprocal(scalars(0), scalars(0))
            dve.drain()
            dve.tensor_tensor(cat[:, :, 32:64], nodes(0, 32), over(scalars(0), 32), ALU.mult)
            dve.tensor_copy(cat[:, :, 0:32], nodes(1, 32))
            ready(dve, "product_in")
            product_dve(dve, "L3", plain(nodes(4, 32)), 32)
            dve.drain()
            dve.tensor_tensor(nodes(4, 32), nodes(4, 32), vec("L3_gnn_b"), ALU.add)
            fetch_back(dve, "res3")
            dve.scalar_tensor_tensor(nodes(4, 32), nodes(4, 32), 0.0, nodes(5, 32), ALU.max, ALU.add)
            ready(dve, "result")

        @block.scalar
        def _(act):
            def save_chunks(name, table, f, it, b):
                act.wait_ge(S[f"rows{ROWS[name][0]}{b}"], it * (16 * CJ) + (ROWS[name][1] + 16 * CJ))
                act.dma_start(chunk(table, f, it, b), rows(G[b], f)).then_inc(S[f"{name}_saved{b}"], 16)

            def sigmoid_exp(name, it, b):
                act.wait_ge(S[f"{name}_sum"], it * 2 + (b + 1))
                act.activation(narrow[b][:, 0:CJ], side[b][:, 0:CJ], ACT.Tanh, scale=0.5)
                act.drain()
                act.activation(narrow[b][:, CJ:2 * CJ], narrow[b][:, 0:CJ], ACT.Exp, scale=0.5,
                               bias=half[:]).then_inc(S[f"{name}_exp"], 1)

            deviation_act(act, 1)
            product_act(act, "kvq")
            with act.Fori(0, IT) as it:
                for b in range(2):
                    prepare_act(act, "scores", OD, it, b, spread=32)
                    save_chunks("scores", KV, 64, it, b)
                    finish_act(act, "scores", it, b, 5, R[5])
            act.wait_ge(S["degree"], 1)
            act.activation(scalars(2), scalars(1), ACT.Sqrt).then_inc(S["degree_root"], 1)
            with act.Fori(0, IT) as it:
                for b in range(2):
                    prepare_act(act, "soft", OD, it, b, spread=4)
                    act.wait_ge(S["soft_shifted"], it * 2 + (b + 1))
                    act.activation(side[b][:, 0:CJ * HEADS], side[b][:, 0:CJ * HEADS], ACT.Exp).then_inc(S["soft_exp"], 1)
                    finish_act(act, "soft", it, b, 36, R[36])
            product_act(act, "Wo")
            deviation_act(act, 2)
            for layer in range(1, 6):
                f = 32 if layer in (1, 5) else 64
                plain_act(act, f"gcn{layer}", OD, f, R[f])
                if layer == 1:
                    product_act(act, "L1_W1")
                graph_norm_act(act, layer, 32 if layer == 5 else 64)
                if layer < 5:
                    product_act(act, f"L1_W{layer + 1}")
            deviation_act(act, 3)
            product_act(act, "fc_T")
            with act.Fori(0, IT) as it:
                for b in range(2):
                    prepare_act(act, "attend", OD, it, b, spread=1)
                    save_chunks("attend", ZA, 65, it, b)
                    sigmoid_exp("attend", it, b)
                    finish_act(act, "attend", it, b, 65, R[65])
            for name in ("h_p1", "A1", "h_p2", "A2"):
                product_act(act, name)
            plain_act(act, "hsum", OD, 64, R[64])
            product_act(act, "enc")
            product_act(act, "K_0")
            act.wait_ge(S["k0_raw"], 1)
            act.activation(flat(2, 64), flat(2, 64), ACT.Tanh).then_inc(S["product_in"], 1)
            for name in ("K_1", "K_2", "KW"):
                product_act(act, name)
            with act.Fori(0, IT) as it:
                for b in range(2):
                    prepare_act(act, "umlp", OD, it, b, spread=64)
                    act.wait_ge(S["umlp_pre"], it * 2 + (b + 1))
                    act.activation(T, T, ACT.Tanh).then_inc(S["umlp_tanh"], 1)
                    act.wait_ge(S[f"stored{b}"], it * 32 + STORED["umlp"])
                    for u in range(UG):
                        k = b * UG + u
                        act.wait_ge(S["umlp_turned"], it * (2 * UG) + (k + 1))
                        act.copy(packT[k % 2][:], psT[k % 2][:]).then_inc(S["umlp_turned_copied"], 1)
                        act.wait_ge(S["umlp_up"], it * (2 * UG) + (k + 1))
                        act.activation(rows(OUT[b], 128)[:, 8 * u:8 * u + 8, 0:64],
                                       psO[k % 2][:].rearrange("p (j f) -> p j f", f=64), ACT.Relu).then_inc(S["umlp_relu"], 1)
                    for u in range(UG):
                        k = b * UG + u
                        act.wait_ge(S["umlp_turned_down"], it * (2 * UG) + (k + 1))
                        act.copy(packB[k % 2][:], psB[k % 2][:]).then_inc(S["umlp_down_copied"], 1)
                    finish_act(act, "umlp", it, b, 64, R[64], out=H)
                    act.dma_start(chunk(UD, 128, it, b), rows(OUT[b], 128)).then_inc(S[f"stored{b}"], 16)
            plain_act(act, "upair", OS, 128, R[128])
            for name in ("b_U2", "b_K2", "b_K1", "b_K0", "b_U0s", "b_p1", "b_U0d", "b_p2"):
                product_act(act, name)
            plain_act(act, "dh1", OS, 64, R[64])
            product_act(act, "b_enc")
            for name, o, f, sums_of in (("grad", OS, 65, 65), ("back", OD, 67, 1)):
                with act.Fori(0, IT) as it:
                    for b in range(2):
                        prepare_act(act, name, o, it, b, spread=f)
                        sigmoid_exp(name, it, b)
                        finish_act(act, name, it, b, sums_of, R[sums_of])
            product_act(act, "b_fc")
            product_act(act, "b_D")
            deviation_act(act, 4)
            plain_act(act, "mean", OD, 32, R[32])
            product_act(act, "L3")

        @block.tensor
        def _(pe):
            pe.wait_ge(S["weights"], 32)
            pe.wait_ge(S["zeros"], 1)
            order_pe(pe, OD)
            product_pe(pe, "kvq", "kvq", NODE[1])
            ends_pe(pe, "scores", OD, 5, maxima=4)
            ends_pe(pe, "soft", OD, 36)
            product_pe(pe, "Wo", "Wo", NODE[1])
            for layer in range(1, 6):
                f = 32 if layer in (1, 5) else 64
                if layer in (1, 3):
                    count_pe(pe, layer // 3)
                ends_pe(pe, f"gcn{layer}", OD, f)
                if layer == 1:
                    product_pe(pe, "L1_W1", "L1_W1", NODE[2])
                graph_norm_pe(pe, layer, 32 if layer == 5 else 64)
                if layer < 5:
                    product_pe(pe, f"L1_W{layer + 1}", f"L1_W{layer + 1}", NODE[5])
            product_pe(pe, "fc_T", "fc_T", NODE[1])
            ends_pe(pe, "attend", OD, 65)
            product_pe(pe, "h_p1", "p1_T", NODE[1], "L2_gnn_b_p1")
            product_pe(pe, "A1", "U0_T", NODE[2], "L2_gnn_U_b0")
            product_pe(pe, "h_p2", "p2_T", NODE[1], "L2_gnn_b_p2")
            product_pe(pe, "A2", "U0_T", NODE[2])
            order_pe(pe, OS)
            ends_pe(pe, "hsum", OD, 64)
            product_pe(pe, "enc", "encK_T", NODE[0])
            product_pe(pe, "K_0", "K0_T", NODE[1], "L2_gnn_K_b0")
            product_pe(pe, "K_1", "K1_T", NODE[2], "L2_gnn_K_b1")
            product_pe(pe, "K_2", "K2_T", NODE[3], "L2_gnn_K_b2")
            product_pe(pe, "KW", "U2", NODE[4])
            for name in ("umlp_turned_copied", "umlp_relu", "umlp_down_copied", "umlp_taken"):
                pe.sem_inc(S[name], 2)
            up, down, bias = WAT["U1_T"][0], WAT["U1"][0], VAT["L2_gnn_U_b1"][0]
            with pe.Fori(0, IT) as it:
                for b in range(2):
                    n = 2 * UG
                    pe.wait_ge(S["umlp_tanh"], it * 2 + (b + 1))
                    for u in range(UG):
                        k = b * UG + u
                        pe.wait_ge(S["umlp_turned_copied"], it * n + (k + 1))
                        for i in range(4):
                            last = pe.transpose(psT[k % 2][:, i * P:(i + 1) * P], T[:, (4 * u + i) * P:(4 * u + i + 1) * P], ident[:])
                        last.then_inc(S["umlp_turned"], 1)
                        pe.wait_ge(S["umlp_turned_copied"], it * n + (k + 3))
                        pe.wait_ge(S["umlp_relu"], it * n + (k + 1))
                        pe.matmul(psO[k % 2][:].rearrange("p (j f) -> p j f", f=64), ones[0:1, :],
                                  vectors[0:1, bias:bias + 64].unsqueeze(1).broadcast_to([1, 8, 64]),
                                  start=True, stop=False, skip_group_check=True)
                        for i in range(4):
                            last = pe.matmul(psO[k % 2][:, i * P:(i + 1) * P], packT[k % 2][:, i * P:(i + 1) * P],
                                             weights[:, up:up + P], start=False, stop=True, skip_group_check=True)
                        last.then_inc(S["umlp_up"], 1)
                    for u in range(UG):
                        k = b * UG + u
                        pe.wait_ge(S["umlp_slope"], it * n + (k + 1))
                        pe.wait_ge(S["umlp_down_copied"], it * n + (k + 1))
                        for i in range(4):
                            last = pe.transpose(psB[k % 2][:, i * P:(i + 1) * P], HB[:, (4 * u + i) * P:(4 * u + i + 1) * P], ident[:])
                        last.then_inc(S["umlp_turned_down"], 1)
                        pe.wait_ge(S["umlp_down_copied"], it * n + (k + 3))
                        pe.wait_ge(S["umlp_taken"], it * n + (k + 1))
                        for i in range(4):
                            last = pe.matmul(psD[k % 2][:, i * P:(i + 1) * P], packB[k % 2][:, i * P:(i + 1) * P],
                                             weights[:, down:down + P], start=True, stop=True)
                        last.then_inc(S["umlp_down"], 1)
            ends_pe(pe, "umlp", OD, 64)
            ends_pe(pe, "upair", OS, 128)
            product_pe(pe, "b_U2", "U2_T", NODE[2])
            product_pe(pe, "b_K2", "K2", NODE[5])
            product_pe(pe, "b_K1", "K1", NODE[6])
            product_pe(pe, "b_K0", "K0", NODE[2])
            product_pe(pe, "b_U0s", "U0", NODE[3])
            product_pe(pe, "b_p1", "p1", NODE[2])
            product_pe(pe, "b_U0d", "U0", NODE[4])
            product_pe(pe, "b_p2", "p2", NODE[2])
            ends_pe(pe, "dh1", OS, 64)
            product_pe(pe, "b_enc", "encK", NODE[0])
            ends_pe(pe, "grad", OS, 65)
            ends_pe(pe, "back", OD, 1)
            product_pe(pe, "b_fc", "fc", NODE[2])
            product_pe(pe, "b_D", "D_T", NODE[3])
            ends_pe(pe, "mean", OD, 32)
            product_pe(pe, "L3", "L3_W", NODE[2])

        @block.gpsimd
        def _(pool):
            pool.iota(digits[:], [[1, P]], base=0, channel_multiplier=0, allow_small_or_imprecise_dtypes=True)
            pool.iota(part_id[:], [[0, 1]], base=0, channel_multiplier=1, allow_small_or_imprecise_dtypes=True)
            pool.iota(node_id[:], [[1, NT + 1]], base=-1, channel_multiplier=NT, allow_small_or_imprecise_dtypes=True)
            pool.iota(HB[:, J:2 * J].bitcast(I32), [[1, J]], base=0, channel_multiplier=J)
            pool.drain()
            pool.sem_inc(S["iotas"], 1)
            pool.wait_ge(S["unsorted"], 16)
            order_pool(pool, OD)
            pool.wait_ge(S["filled"], 16 * FILLS)
            pool.wait_ge(S["q_made"], 1)
            spread_pool(pool, "scores", OD, 32, NODE[3], XQ)
            pool.wait_ge(S["q_kept"], 16)
            spread_first_pool(pool, "scores", OD, 32, TB["q"], spread_carry)
            pool.wait_ge(S["kv_kept"], 16)
            gather_pool(pool, "scores", TB["kv"], 64)
            ends_pool(pool, "scores", OD, 5)
            pool.wait_ge(S["m_made"], 1)
            spread_pool(pool, "soft", OD, 4, NODE[1], XM)
            pool.wait_ge(S["m_kept"], 16)
            spread_first_pool(pool, "soft", OD, 4, TB["m"], spread_carry)
            ends_pool(pool, "soft", OD, 36)
            for layer in range(1, 6):
                f = 32 if layer in (1, 5) else 64
                pool.wait_ge(S["gcn_kept"], 16 * layer)
                gather_pool(pool, f"gcn{layer}", TB[f"gcn{layer}"], f)
                ends_pool(pool, f"gcn{layer}", OD, f)
                if f"gcn{layer}" in SLICES:
                    scatter_pool(pool, *SLICES[f"gcn{layer}"])
            pool.wait_ge(S["za_made"], 1)
            spread_pool(pool, "attend", OD, 1, scalars(5), XA)
            pool.wait_ge(S["ad_kept"], 16)
            spread_first_pool(pool, "attend", OD, 1, TB["ad"], spread_carry)
            pool.wait_ge(S["za_kept"], 16)
            gather_pool(pool, "attend", TB["za"], 65)
            ends_pool(pool, "attend", OD, 65)
            scatter_pool(pool, *SLICES["attend"])
            pool.wait_ge(S["A2_made"], 1)
            spread_pool(pool, "umlp", OD, 64, NODE[4], XA2)
            pool.wait_ge(S["A2_kept"], 16)
            spread_first_pool(pool, "umlp", OD, 64, TB["a2"], spread_carry)
            order_pool(pool, OS)
            pool.wait_ge(S["h_kept"], 16)
            gather_pool(pool, "hsum", TB["h"], 64)
            ends_pool(pool, "hsum", OD, 64)
            pool.wait_ge(S["A1_kept"], 16)
            pool.wait_ge(S["KW_kept"], 16)
            gather_pool(pool, "umlp", TB["ka"], 128)
            ends_pool(pool, "umlp", OD, 64)
            gather_pool(pool, "upair", UD, 128)
            ends_pool(pool, "upair", OS, 128)
            pool.wait_ge(S["dh1_kept"], 16)
            gather_pool(pool, "dh1", TB["dh1"], 64)
            ends_pool(pool, "dh1", OS, 64)
            pool.wait_ge(S["grad_made"], 1)
            spread_pool(pool, "grad", OS, 65, NODE[6], XS)
            spread_pool(pool, "back", OD, 67, NODE[4], XF)
            spread_first_pool(pool, "grad", OS, 65, TB["za"], spread_carry)
            pool.wait_ge(S["grad_kept"], 16)
            spread_first_pool(pool, "back", OD, 67, TB["dst"], spread_carry2)
            gather_pool(pool, "grad", TB["dst"], 67)
            ends_pool(pool, "grad", OS, 65)
            ends_pool(pool, "back", OD, 1)
            pool.wait_ge(S["hin_kept"], 16)
            gather_pool(pool, "mean", TB["hin"], 32)
            ends_pool(pool, "mean", OD, 32)

        @block.sync
        def _(sp):
            sp.dma_start(weights[:], weights_in).then_inc(S["weights"], 16)
            sp.dma_start(vectors[:], vectors_in.broadcast_to([P, VCOLS])).then_inc(S["weights"], 16)
            sp.dma_start(T[:, 0:J].bitcast(I32), src_in).then_inc(S["edges"], 16)
            sp.dma_start(T[:, J:2 * J].bitcast(I32), dst_in).then_inc(S["edges"], 16)
            sp.dma_start(w_d[:], w_in).then_inc(S["edges"], 16)
            sp.wait_ge(S["zeros"], 1)
            sp.wait_ge(S["payload"], 1)
            sp.dma_start(SORT[0].rearrange("(p j) f -> p (j f)", j=J), pay_i).then_inc(S["unsorted"], 16)
            keys_sp(sp, OD)
            for t, f in SPREADS:
                sp.dma_start(t[0:EP, :].rearrange("(p j) f -> p (j f)", j=J).rearrange("p (f j) -> p f j", j=J),
                             G[0][:, 0:J].unsqueeze(1).broadcast_to([P, f, J])).then_inc(S["filled"], 16)
            firsts = ["stored0", "stored1", "scores_saved0", "scores_saved1", "attend_saved0", "attend_saved1"]
            for f in R:
                name = firsts.pop(0) if firsts else "filled"
                sp.dma_start(R[f][EP:EP + P, :], G[0][:, 0:f]).then_inc(S[name], CREDIT)
                sp.dma_start(R[f][EP + P:EP + P + 1, :], G[0][0:1, 0:f]).then_inc(S["filled"], 16)
            upto_sp(sp, OD)
            sp.wait_ge(S["room"], 1)
            sp.dma_start(flat(0, 32), by_node(x_in)).then_inc(S["back"], 16)
            store_node(sp, "kv", TB["kv"], 2, 64)
            store_node(sp, "q", TB["q"], 3, 32)
            store_node(sp, "res0", TB["res0"], 0, 32)
            sp.wait_ge(S["scores_spread"], 16 * NT)
            feed_sp(sp, "scores", src_in, [(XQ, 32, X)], saved=True)
            store_node(sp, "m", TB["m"], 1, 4)
            sp.wait_ge(S["soft_spread"], 16 * NT)
            feed_sp(sp, "soft", None, [(KV, 64, G), (XM, 4, X)])
            load_node(sp, "res0", TB["res0"], 3, 32, "res0_kept")
            reload_sp(sp, 0, SORT[0])
            store_node(sp, "res1", TB["res1"], 3, 32)
            for layer in range(1, 6):
                f = 32 if layer in (1, 5) else 64
                name = f"gcn{layer}"
                store_node(sp, "gcn", TB[name], 1, f, layer)
                feed_sp(sp, name, src_in)
                load_node(sp, name, TB[name], 1, f, "gcn_kept", layer)
                if name in SLICES:
                    scatter_sp(sp, *SLICES[name])
                if layer == 2:
                    reload_sp(sp, 1, SORT[1])
            load_node(sp, "res1", TB["res1"], 3, 32, "res1_kept")
            store_node(sp, "res2", TB["res2"], 3, 32)
            store_node(sp, "za", TB["za"], 4, 65)
            sp.dma_start(by_node(TB["ad"]), scalars(5)).then_inc(S["ad_kept"], 16)
            sp.wait_ge(S["attend_spread"], 16 * NT)
            feed_sp(sp, "attend", src_in, [(XA, 1, X)], saved=True)
            scatter_sp(sp, *SLICES["attend"])
            reload_sp(sp, 2, SORT[2])
            store_node(sp, "h", TB["h"], 1, 64)
            ka = TB["ka"].rearrange("(p t) f -> p t f", t=NT)
            sp.wait_ge(S["A1_made"], 1)
            sp.dma_start(ka[:, :, 64:128], nodes(3, 64)).then_inc(S["A1_kept"], 16)
            store_node(sp, "A2", TB["a2"], 4, 64)
            sp.wait_ge(S["payload"], 2)
            sp.dma_start(DST_S, T[:, 0:J].bitcast(I32)).then_inc(S["s_rows"], 16)
            sp.dma_start(POS_S, T[:, J:2 * J].bitcast(I32)).then_inc(S["s_rows"], 16)
            sp.wait_ge(S["s_rows"], 32)
            keys_sp(sp, OS)
            upto_sp(sp, OS)
            feed_sp(sp, "hsum", src_in)
            sp.wait_ge(S["k01_made"], 1)
            sp.dma_start(by_node(TB["k0"]), flat(2, 64)).then_inc(S["k0_kept"], 16)
            sp.dma_start(by_node(TB["k1"]), flat(3, 64)).then_inc(S["k1_kept"], 16)
            sp.wait_ge(S["KW_made"], 1)
            sp.dma_start(ka[:, :, 0:64], nodes(5, 64)).then_inc(S["KW_kept"], 16)
            sp.wait_ge(S["umlp_spread"], 16 * NT)
            feed_sp(sp, "umlp", src_in, [(XA2, 64, X)])
            store_node(sp, "dpd", TB["dp"], 0, 64)
            feed_sp(sp, "upair", POS_S)
            load_node(sp, "k1", TB["k1"], 7, 64, "k1_kept")
            load_node(sp, "k0", TB["k0"], 5, 64, "k0_kept")
            store_node(sp, "dh1", TB["dh1"], 6, 64)
            load_node(sp, "dpd", TB["dp"], 4, 64, "dpd_kept")
            store_node(sp, "dhu", TB["w2"], 5, 64)
            feed_sp(sp, "dh1", DST_S)
            load_node(sp, "dhu", TB["w2"], 2, 64, "dhu_kept")
            load_node(sp, "h", TB["h"], 3, 64, "h_kept")
            load_node(sp, "za", TB["za"], 6, 65, "za_kept")
            sp.wait_ge(S["grad_made"], 1)
            sp.dma_start(by_node(TB["dst"]), flat(4, 67)).then_inc(S["grad_kept"], 16)
            sp.wait_ge(S["grad_spread"], 16 * NT)
            sp.wait_ge(S["back_spread"], 16 * NT)
            feed_sp(sp, "grad", DST_S, [(XS, 65, X)])
            store_node(sp, "gs", TB["gs"], 0, 65)
            feed_sp(sp, "back", None, [(ZA, 65, G), (XF, 67, X)])
            load_node(sp, "gs", TB["gs"], 1, 65, "gs_kept")
            load_node(sp, "res2", TB["res2"], 6, 32, "res2_kept")
            store_node(sp, "res3", TB["res3"], 6, 32)
            store_node(sp, "hin", TB["hin"], 1, 32)
            feed_sp(sp, "mean", src_in)
            load_node(sp, "hin", TB["hin"], 1, 32, "hin_kept")
            load_node(sp, "res3", TB["res3"], 5, 32, "res3_kept")
            sp.wait_ge(S["result"], 1)
            full, rest = N // NT, N % NT
            sp.dma_start(out[0:full * NT, :].rearrange("(p t) f -> p (t f)", t=NT),
                         NODE[4][0:full, 0:NT * 32]).then_inc(S["out"], 16)
            sp.dma_start(out[full * NT:N, :].rearrange("(p t) f -> p (t f)", t=rest),
                         NODE[4][full:full + 1, 0:rest * 32]).then_inc(S["out"], 16)
            sp.wait_ge(S["out"], 32)


def kernel(**inputs):
    import numpy as np
    import concourse.bacc as bacc
    from concourse.bass_utils import run_bass_kernel_spmd as run

    def edges(a, fill):
        padded = np.full((EP,), fill, a.dtype)
        padded[:E] = a
        return padded.reshape(P, J)

    x = np.zeros((NR, 32), np.float32)
    x[:N] = inputs["x"]
    places, width = weight_places()
    weights = np.zeros((P, width), np.float32)
    for name, source, transposed, rows, cols in weight_plan():
        parts = [np.asarray(inputs[s]) for s in (source if isinstance(source, tuple) else (source,))]
        w = np.concatenate([p.T if transposed else p for p in parts], axis=1)
        for i in range(P // rows):
            at = places[name][0] + i * cols
            weights[i * rows:(i + 1) * rows, at:at + cols] = w
    places, width = vector_places()
    vectors = np.zeros((1, width), np.float32)
    for name in VECTORS:
        at, size = places[name]
        vectors[0, at:at + size] = np.asarray(inputs[name]).reshape(-1)
    arrays = {"x": x, "src": edges(np.asarray(inputs["src"]), PAD), "dst": edges(np.asarray(inputs["dst"]), PAD),
              "w": edges(np.asarray(inputs["edge_weight"]), 0), "weights": weights, "vectors": vectors}
    nc = bacc.Bacc("TRN2", target_bir_lowering=False, num_devices=1)
    args = [nc.dram_tensor(f"in_{k}", a.shape, mybir.dt.from_np(a.dtype), kind="ExternalInput").ap()
            for k, a in arrays.items()]
    out = nc.dram_tensor("out_x", (N, 32), F32, kind="ExternalOutput").ap()
    build(nc, *args, out)
    r = run(nc, [{f"in_{k}": a for k, a in arrays.items()}], core_ids=[0])
    return r.results[0]["out_x"]
```

```python
from contextlib import ExitStack

import concourse.bass as bass
from concourse import mybir

F32, I32, BF16 = mybir.dt.float32, mybir.dt.int32, mybir.dt.bfloat16
ALU, ACT, AX = mybir.AluOpType, mybir.ActivationFunctionType, mybir.AxisListType

P = 128
N = 6250
NT = 50
NR = P * NT
E = 106250
J = 832
EP = P * J
PAD = NR - 1
CJ = 32
IT = J // CJ // 2
ER = EP + 1 + NR
ZERO_ROW, SPARE_ROW = EP, EP + 1
HEADS, DH = 4, 8
BIG = 1.0e30
LO = 64
TABLES = 4
GROUP = 4
EPS = 1e-5


def weight_plan():
    two = [(f"L1_W{i}", f"L1_gnn_W{i}", False, 64, 64) for i in (2, 3, 4)]
    sq = [("encK_T", "L2_gnn_W_encK", True), ("p1_T", "L2_gnn_W_p1", True), ("p2_T", "L2_gnn_W_p2", True),
          ("K0_T", "L2_gnn_K_w0", True), ("K1_T", "L2_gnn_K_w1", True), ("K2_T", "L2_gnn_K_w2", True),
          ("U0_T", "L2_gnn_U_w0", True), ("U1_T", "L2_gnn_U_w1", True), ("U2_T", "L2_gnn_U_w2", True),
          ("encK", "L2_gnn_W_encK", False), ("p1", "L2_gnn_W_p1", False), ("p2", "L2_gnn_W_p2", False),
          ("K0", "L2_gnn_K_w0", False), ("K1", "L2_gnn_K_w1", False), ("K2", "L2_gnn_K_w2", False),
          ("U0", "L2_gnn_U_w0", False), ("U1", "L2_gnn_U_w1", False), ("U2", "L2_gnn_U_w2", False)]
    return ([("kvq", ("L0_gnn_Wk", "L0_gnn_Wv", "L0_gnn_Wq"), False, 32, 96),
             ("Wo", "L0_gnn_Wo", False, 32, 32), ("L1_W1", "L1_gnn_W1", False, 32, 64)] + two
            + [("L1_W5", "L1_gnn_W5", False, 64, 32), ("fc_T", "L2_gnn_W_fc", True, 32, 64),
               ("fc", "L2_gnn_W_fc", False, 64, 32), ("D_T", "L2_gnn_D", True, 32, 32),
               ("L3_W", "L3_gnn_W", False, 64, 32)]
            + [(n, i, t, 64, 64) for n, i, t in sq])


def weight_places():
    at, out = 0, {}
    for name, _, _, rows, cols in weight_plan():
        width = (P // rows) * cols
        out[name] = (at, width)
        at += width
    return out, at


VECTORS = ([f"L1_gnn_{v}{i}{w}" for i in range(1, 6) for v, w in (("b", ""), ("g", "w"), ("g", "b"), ("g", "a"))]
           + ["L2_gnn_W_attn", "L2_gnn_b_encK", "L2_gnn_b_p1", "L2_gnn_b_p2", "L2_gnn_K_b0", "L2_gnn_K_b1",
              "L2_gnn_K_b2", "L2_gnn_U_b0", "L2_gnn_U_b1", "L2_gnn_U_b2", "L3_gnn_b"])


def vector_places():
    at, out = 0, {}
    for name in VECTORS:
        size = 128 if name == "L2_gnn_W_attn" else 32 if (name.startswith("L1_gnn") and "5" in name) or name == "L3_gnn_b" else 64
        out[name] = (at, size)
        at += size
    return out, at


def build(nc, x_in, src_in, dst_in, src_t_in, w_in, weights_in, vectors_in, out):
    ctx = ExitStack()
    with ctx:
        WAT, WCOLS = weight_places()
        VAT, VCOLS = vector_places()

        class Semaphores(dict):
            def __missing__(self, name):
                self[name] = ctx.enter_context(nc.semaphore(name))
                return self[name]

        S = Semaphores()

        def sb(name, shape, dt=F32):
            return ctx.enter_context(nc.sbuf_tensor(name, shape, dt))

        def dram(name, shape, dt=F32):
            return nc.dram_tensor(name, shape, dt).ap()

        weights = sb("weights", [P, WCOLS])
        vectors = sb("vectors", [P, VCOLS])
        ident = sb("ident", [P, P])
        ones = sb("ones", [P, P])
        before = sb("before", [P, P])
        src_t = sb("src_t", [P, IT * P], BF16)
        digit_ident = sb("digit_ident", [P, 2 * CJ], BF16)
        src_keys = sb("src_keys", [P, J])
        key_cols = sb("key_cols", [P, CJ])
        zeros = sb("zeros", [P, 129])
        spare_rows = sb("spare_rows", [P, 1], I32)
        node_id = sb("node_id", [P, NT + 1])
        part_id = sb("part_id", [P, 1])
        real = sb("real", [P, P])
        norm_cols = sb("norm_cols", [P, 2])
        ones_bf = sb("ones_bf", [P, P], BF16)
        bias_parts = sb("bias_parts", [P, 64], BF16)
        w_d = sb("w_d", [P, J])
        arena = sb("arena", [P, 2 * (129 * CJ + 129 * CJ + 67 * CJ) + 67 * CJ + 4096 + 5 * 2048])
        half = sb("half", [P, 1])
        digits = sb("digits", [P, P])

        at = [0]

        def take(n):
            at[0] += n
            return arena[:, at[0] - n:at[0]]

        G = [take(129 * CJ) for _ in range(2)]
        OUT = [take(129 * CJ) for _ in range(2)]
        X = [take(67 * CJ) for _ in range(2)]
        XP = take(67 * CJ)
        M = take(4096)
        MR = take(2048)
        T = take(2048)
        HB = take(2048)
        H = [take(2048) for _ in range(2)]
        SLOT = NT * 67
        NODE = [arena[:, i * SLOT:(i + 1) * SLOT] for i in range(8)]
        key = HB[:, 0:J]
        BESIDE = arena[:, at[0] - 8192:at[0] - 4096]
        WIDE = arena[:, at[0] - 4096:at[0]]

        def own(layer):
            f, start = (32, at[0] - 4096) if layer == 1 else (32 if layer == 5 else 64, at[0] - 8192)
            return arena[:, start:start + NT * f].rearrange("p (t f) -> p t f", f=f)

        class Order:
            def __init__(self, k, n):
                self.k, self.n = k, n
                self.key = key
                self.same = sb(f"same_{k}", [P, J], BF16)
                self.ends = sb(f"ends_{k}", [P, 8])
                self.equal = sb(f"equal_{k}", [P, P])
                self.all_equal = sb(f"all_equal_{k}", [P, P])
                self.last_row = sb(f"last_row_{k}", [P, P])
                self.join = sb(f"join_{k}", [P, 1], I32)
                self.first = sb(f"first_{k}", [P, 1], I32)
                self.last = sb(f"last_{k}", [P, 1], I32)
                self.end = sb(f"end_{k}", [P, NT], I32)
                self.start = sb(f"start_{k}", [P, NT], I32)
                self.count = sb(f"count_{k}", [P, NT])
                self.upto = sb(f"upto_{k}", [P, NT + 1])
                self.part = sb(f"part_{k}", [P, NT + 1])
                self.part_i = sb(f"part_i_{k}", [P, NT + 1], I32)
                self.keys = dram(f"keys_{k}", (P, J))
                self.upto_rows = dram(f"upto_rows_{k}", (NR, 1))

        OD = Order("d", 0)
        idx = [sb(f"idx{b}", [P, CJ], I32) for b in range(2)]
        add_idx = [sb(f"add_idx{b}", [P, CJ], I32) for b in range(2)]
        m0 = sb("m0", [P, 1])
        neg0 = sb("neg0", [P, 1])
        side = [sb(f"side{b}", [P, CJ * 4]) for b in range(2)]
        narrow = [sb(f"narrow{b}", [P, CJ * 2]) for b in range(2)]
        carry = sb("carry", [P, P])
        spread_carry = sb("spread_carry", [P, P])
        joined = sb("joined", [P, P])
        small = sb("small", [P, 16 * NT])
        sums = sb("sums", [P, 8 * 64])
        packT = [sb(f"packT{b}", [P, 512]) for b in range(2)]
        packB = [sb(f"packB{b}", [P, 512]) for b in range(2)]
        dis = sb("dis", [P, NT])
        rden = sb("rden", [P, NT])

        psT = [ctx.enter_context(nc.psum_tensor(f"psT{b}", [P, 512], F32)) for b in range(2)]
        psO = [ctx.enter_context(nc.psum_tensor(f"psO{b}", [P, 512], F32)) for b in range(2)]
        psB = [ctx.enter_context(nc.psum_tensor(f"psB{b}", [P, 512], F32)) for b in range(2)]
        psD = [ctx.enter_context(nc.psum_tensor(f"psD{b}", [P, 512], F32)) for b in range(2)]

        def rows(buf, f, n=CJ):
            return buf[:, 0:n * f].rearrange("p (j f) -> p j f", f=f)

        def nodes(i, f, off=0):
            return NODE[i][:, off:off + NT * f].rearrange("p (t f) -> p t f", f=f)

        def scalars(i):
            return small[:, i * NT:(i + 1) * NT]

        def over(col, f):
            return col.unsqueeze(2).broadcast_to([P, col.shape[1], f])

        def vec(name, n=NT, off=0, size=None):
            a, s = VAT[name]
            s = size or s
            return vectors[:, a + off:a + off + s].unsqueeze(1).broadcast_to([P, n, s])

        def edge_table(name, f):
            return dram(name, (ER, f))

        R = {f: dram(f"runs{f}", (EP + 1 + P, f)) for f in (1, 32, 41, 64, 65)}
        XQ, XA, X64, XF = (edge_table(n, f) for n, f in (("xq", 32), ("xa", 1), ("x64", 64), ("xf", 67)))
        ZA, UD = dram("za_rows", (EP, 65)), dram("ud_rows", (EP, 129))
        TB = {n: dram("t_" + n, (NR, f)) for n, f in
              (("kv", 64), ("q", 32), ("za", 65), ("ad", 1), ("h", 64),
               ("ka", 128), ("a2", 64), ("k0", 64), ("k1", 64), ("dh1", 64), ("dst", 67),
               ("res0", 32), ("res1", 32), ("res2", 32), ("res3", 32), ("hin", 32), ("w2", 64), 
               ("gcn1", 32), ("gcn2", 64), ("gcn3", 64), ("gcn4", 64), ("gcn5", 32))}
        FIRSTS = ["stored0", "stored1", "attend_saved0", "attend_saved1"]
        FILLS = 2 + 2 * len(R) - len(FIRSTS)
        UG = CJ // 8
        ADD = {f: [dram(f"added{f}_{k}", (NR + P, f)) for k in range(TABLES)] for f in (129, 64, 65)}
        ADD_ROWS = dram("add_rows", (P, J), I32)

        def by_edge(t, f):
            return t[0:EP, :].rearrange("(p j) f -> p j f", j=J)

        def by_node(t):
            return t.rearrange("(p t) f -> p (t f)", t=NT)

        def turned(buf, f, at=0):
            return buf[:, at * CJ:(at + f) * CJ].rearrange("p (f j) -> p j f", f=f)

        def by_feature(buf, f, at=0):
            return buf[:, at * CJ:(at + f) * CJ].rearrange("p (f j) -> p f j", f=f)

        def chunk(t, f, it, b):
            return by_edge(t, f)[:, bass.ds(it * (2 * CJ) + b * CJ, CJ), :]

        def cols(t, it, b, f=1):
            return t[:, bass.ds(it * (2 * CJ * f) + b * CJ * f, CJ * f)]

        PASSES = [("scores", 1, 1), ("gcn1", 0, 1), ("gcn2", 0, 1), ("gcn3", 0, 1), ("gcn4", 0, 1),
                  ("gcn5", 0, 1), ("attend", 1, 1), ("hsum", 0, 1), ("umlp", 1, 2), ("upair", 1, 0), ("dh1", 1, 0),
                  ("back", 2, 1), ("mean", 0, 1)]
        TURN = {n: k for k, (n, _, _) in enumerate(PASSES)}
        FREE = {n: TURN[n] * (IT + 1) for n in TURN}
        SCANS = {n: sum(m != "upair" for m in list(TURN)[:TURN[n]]) for n in TURN}
        ENDED = {n: sum(m not in ("upair", "dh1") for m in list(TURN)[:TURN[n]]) for n in TURN}
        SCANNED = {n: SCANS[n] * (2 * IT + 1) for n in TURN}
        PREPARED = {n: SCANS[n] * 2 * IT for n in TURN}
        PASS_LOADS = {n: a for n, a, _ in PASSES}
        PASS_STORES = {n: a for n, _, a in PASSES}
        LOADED = {n: 16 * IT * sum(a for _, a, _ in PASSES[:TURN[n]]) for n in TURN}
        CREDIT = 16
        STORED = {n: CREDIT + 16 * IT * sum(a for _, _, a in PASSES[:TURN[n]]) for n in TURN}

        LOADS = ["x", "res0", "res1", "k1", "k0", "dhu", "h",
                 "res2", "hin", "res3"]
        GATHERS = ["scores", "gcn1", "gcn2", "gcn3", "gcn4", "gcn5", "attend", "hsum", "umlp", "mean"]
        ROWS = {n: (k // 4, k % 4 * 16 * CJ * IT) for k, n in enumerate(GATHERS)}
        FED = {n: k * 16 * IT for k, n in enumerate(GATHERS)}

        MATCHES = ["gcn1", "upair", "dh1", "back"]
        ADDS = {"upair": (0, 129), "dh1": (1, 64), "back": (2, 65)}
        GROUPS = CJ // GROUP
        BANKS = 2

        PRODUCTS = [("kvq", 32), ("Wo", 32), ("L1_W1", 32), ("L1_W2", 64), ("L1_W3", 64), ("L1_W4", 64),
                    ("L1_W5", 64), ("fc_T", 32), ("h_p1", 64), ("A1", 64), ("h_p2", 64), ("A2", 64),
                    ("enc", 64), ("K_0", 64), ("K_1", 64), ("K_2", 64), ("KW", 64),
                    ("b_U2", 64), ("b_K2", 64), ("b_K1", 64), ("b_K0", 64), ("b_U0s", 64), ("b_p1", 64),
                    ("b_U0d", 64), ("b_p2", 64), ("b_enc", 64), ("b_fc", 64), ("b_D", 32), ("L3", 64)]
        ORDINAL = {n: k for k, (n, _) in enumerate(PRODUCTS)}
        WIDTH = {"kvq": 384, "L1_W1": 256, "fc_T": 256, "L1_W5": 64, "b_fc": 64, "L3": 64}

        def batches(name):
            n, per = -(-NT // (P // dict(PRODUCTS)[name])), min(4, 512 // WIDTH.get(name, P))
            return [(g, min(per, n - g)) for g in range(0, n, per)]

        FIRST, total = {}, 0
        for name, _ in PRODUCTS:
            FIRST[name] = total
            total += len(batches(name))

        def product_pe(pe, name, weight, source, bias=None):
            k = FIRST[name]
            a, width = WAT[weight]
            todo = batches(name)
            pe.wait_ge(S["product_in"], ORDINAL[name] + 1)
            for i in range(len(todo) + 1):
                if i < len(todo):
                    if k + i >= 2:
                        pe.wait_ge(S["turned_copied"], k + i - 1)
                    for g in range(todo[i][1]):
                        at = (todo[i][0] + g) * P
                        last = pe.transpose(psT[(k + i) % 2][:, g * P:(g + 1) * P], source[:, at:at + P], ident[:])
                    last.then_inc(S["turned"], 1)
                if i >= 1:
                    h, n = k + i - 1, todo[i - 1][1]
                    pe.wait_ge(S["turned_copied"], h + 1)
                    if h >= 2:
                        pe.wait_ge(S["product_taken"], h - 1)
                    if bias is not None:
                        v, size = VAT[bias]
                        times = n * width // size
                        pe.matmul(psO[h % 2][:, 0:n * width].rearrange("p (t f) -> p t f", f=size), ones[0:1, :],
                                  vectors[0:1, v:v + size].unsqueeze(1).broadcast_to([1, times, size]),
                                  start=True, stop=False, skip_group_check=True)
                    for g in range(n):
                        last = pe.matmul(psO[h % 2][:, g * width:(g + 1) * width], packT[h % 2][:, g * P:(g + 1) * P],
                                         weights[:, a:a + width], start=bias is None, stop=True, skip_group_check=True)
                    last.then_inc(S["product"], 1)

        def product_act(act, name, scale=None, shift=None):
            k = FIRST[name]
            for i, (_, n) in enumerate(batches(name)):
                act.wait_ge(S["turned"], k + i + 1)
                if k + i >= 2:
                    act.wait_ge(S["product"], k + i - 1)
                to, turned_rows = packT[(k + i) % 2][:, 0:n * P], psT[(k + i) % 2][:, 0:n * P]
                if scale is None:
                    act.copy(to, turned_rows).then_inc(S["turned_copied"], 1)
                else:
                    act.activation(to, turned_rows, ACT.Relu, scale=scale, bias=shift).then_inc(S["turned_copied"], 1)

        def product_dve(dve, name, take_out, cols_out):
            k, per = FIRST[name], P // dict(PRODUCTS)[name]
            for i, (g, n) in enumerate(batches(name)):
                dve.wait_ge(S["product"], k + i + 1)
                ps = psO[(k + i) % 2][:, 0:n * per * cols_out].rearrange("p (t f) -> p t f", f=cols_out)
                end = min((g + n) * per, NT)
                take_out(slice(g * per, end), ps[:, 0:end - g * per, :]).then_inc(S["product_taken"], 1)

        def pad(dve, i):
            dve.memset(NODE[i][:, NT * 32:-(-NT // 4) * 4 * 32], 0.0)

        def plain(dst):
            return lambda t, ps: nc.vector.tensor_copy(dst[:, t, :], ps)

        def scaled(dst, col):
            return lambda t, ps: nc.vector.tensor_tensor(dst[:, t, :], ps, over(col[:, t], ps.shape[2]), ALU.mult)

        def relu_to(dst):
            return lambda t, ps: nc.vector.tensor_scalar(dst[:, t, :], ps, 0.0, None, ALU.max)

        def order_dve(dve, o):
            n = o.n
            dve.wait_ge(S["ends_read"], 16 * 3 * (n + 1))
            dve.tensor_tensor(o.same[:, 1:J], o.key[:, 1:J], o.key[:, 0:J - 1], ALU.is_equal)
            dve.tensor_tensor(o.same[:, 0:1], o.key[:, 0:1], o.ends[:, 0:1], ALU.is_equal)
            dve.tensor_copy(o.first[:], o.key[:, 0:1])
            dve.tensor_copy(o.last[:], o.key[:, J - 1:J])
            dve.tensor_tensor(o.ends[:, 3:4], o.key[:, J - 1:J], o.ends[:, 1:2], ALU.is_equal)
            dve.tensor_tensor(o.ends[:, 4:5], o.key[:, J - 1:J], o.ends[:, 2:3], ALU.not_equal)
            dve.tensor_tensor(o.ends[:, 7:8], o.key[:, J - 1:J], o.ends[:, 0:1], ALU.is_equal)
            dve.tensor_scalar(joined[:], ident[:], o.key[:, J - 1:J], None, ALU.mult).then_inc(S["order_diag"], 1)
            dve.wait_ge(S["order_last_row"], n + 1)
            dve.tensor_copy(o.last_row[:], psB[0][:, 0:P])
            dve.drain()
            dve.tensor_scalar(o.all_equal[:], o.last_row[:], o.key[:, J - 1:J], None, ALU.is_equal)
            dve.tensor_scalar(o.equal[:], o.last_row[:], o.key[:, J - 1:J], o.ends[:, 3:4], ALU.is_equal, ALU.mult)
            dve.tensor_tensor(o.ends[:, 4:5], o.ends[:, 4:5], o.ends[:, 3:4], ALU.mult)
            dve.tensor_tensor(o.ends[:, 7:8], o.ends[:, 7:8], o.ends[:, 3:4], ALU.is_gt)
            dve.drain()
            dve.tensor_tensor(o.ends[:, 4:5], o.ends[:, 4:5], o.ends[:, 7:8], ALU.add)
            for t in range(NT + 1):
                dve.tensor_scalar(carry[:], o.last_row[:], node_id[:, t:t + 1], 0.0, ALU.is_le, ALU.add,
                                  accum_out=o.part[:, t:t + 1])
                dve.drain()
            dve.tensor_scalar(o.part[:], o.part[:], float(P - 1), None, ALU.min)
            dve.drain()
            dve.tensor_copy(o.part_i[:], o.part[:]).then_inc(S["order_part"], 1)
            for t in range(NT + 1):
                dve.wait_ge(S[f"search{t % 4}"], 16 * (t // 4 + 1 + n * len(range(t % 4, NT + 1, 4))))
                dve.tensor_scalar(T[:, 0:J], WIDE[:, (t % 4) * J:(t % 4 + 1) * J], node_id[:, t:t + 1], 0.0,
                                  ALU.is_le, ALU.add, accum_out=o.upto[:, t:t + 1]).then_inc(S["searched"], 1)
                dve.drain()
            dve.scalar_tensor_tensor(o.upto[:], o.part[:], float(J), o.upto[:], ALU.mult, ALU.add)
            dve.drain()
            dve.tensor_tensor(o.count[:], o.upto[:, 1:], o.upto[:, 0:NT], ALU.subtract).then_inc(S["order_upto"], 1)
            dve.drain()
            has, a, b = scalars(0), scalars(1), scalars(2)
            spare, spares = scalars(3)[:, 0:1], scalars(4)
            dve.tensor_scalar(has, o.count[:], 0.0, None, ALU.is_gt)
            dve.tensor_scalar(spare, part_id[:], float(SPARE_ROW), None, ALU.add)
            dve.drain()
            dve.tensor_scalar(a, o.upto[:, 1:], float(-1 - ZERO_ROW), None, ALU.add)
            dve.tensor_scalar(spares, node_id[:, 1:], float(SPARE_ROW), None, ALU.add)
            dve.drain()
            dve.tensor_tensor(b, o.upto[:, 0:NT], spares, ALU.subtract)
            dve.drain()
            dve.tensor_tensor(a, a, has, ALU.mult)
            dve.tensor_tensor(b, b, has, ALU.mult)
            dve.drain()
            dve.tensor_scalar(o.end[:], a, float(ZERO_ROW), None, ALU.add)
            dve.tensor_tensor(o.start[:], b, spares, ALU.add)
            dve.wait_ge(S["order_join_end"], 16 * (n + 1))
            dve.tensor_scalar(o.ends[:, 5:6], o.ends[:, 6:7], -1.0, spare, ALU.add, ALU.subtract)
            dve.drain()
            dve.tensor_tensor(o.ends[:, 5:6], o.ends[:, 5:6], o.ends[:, 4:5], ALU.mult)
            dve.drain()
            dve.tensor_scalar(o.join[:], o.ends[:, 5:6], spare, None, ALU.add).then_inc(S["order_built"], 1)
            dve.drain()

        def keys_sp(sp, o):
            n = o.n
            sp.wait_ge(S["order_key"], n + 1)
            sp.dma_start(o.keys, o.key[:]).then_inc(S["order_keys"], 16)
            sp.wait_ge(S["order_keys"], 16 * (n + 1))
            sp.dma_start(o.ends[1:P, 0:1], o.keys[0:P - 1, J - 1:J], allow_slow_non_contiguous=True).then_inc(S["ends_read"], 16)
            sp.dma_start(o.ends[0:P - 1, 1:2], o.keys[1:P, 0:1], allow_slow_non_contiguous=True).then_inc(S["ends_read"], 16)
            sp.dma_start(o.ends[0:P - 1, 2:3], o.keys[1:P, J - 1:J], allow_slow_non_contiguous=True).then_inc(S["ends_read"], 16)

        def upto_sp(sp, o):
            n = o.n
            sp.wait_ge(S["order_upto"], n + 1)
            sp.dma_start(by_node(o.upto_rows), o.upto[:, 1:]).then_inc(S["order_upto_rows"], 16)

        def order_pe(pe, o):
            n = o.n
            pe.wait_ge(S["order_diag"], n + 1)
            pe.matmul(psB[0][:, 0:P], ones[:], joined[:], start=True, stop=True).then_inc(S["order_last_row"], 1)

        def order_pool(pool, o):
            n = o.n
            pool.wait_ge(S["order_keys"], 16 * (n + 1))
            pool.wait_ge(S["order_part"], n + 1)
            for t in range(NT + 1):
                if t >= 4:
                    pool.wait_ge(S["searched"], t - 3 + n * (NT + 1))
                fetch(pool, WIDE[:, (t % 4) * J:(t % 4 + 1) * J], o.keys, o.part_i[:, t:t + 1]).then_inc(S[f"search{t % 4}"], 16)
            pool.wait_ge(S["order_upto_rows"], 16 * (n + 1))
            fetch(pool, o.ends[:, 6:7], o.upto_rows, o.last[:]).then_inc(S["order_join_end"], 16)
            pool.wait_ge(S["order_built"], n + 1)

        def fetch(pool, dst, table, index):
            return pool.indirect_dma_start(dst, None, table, bass.IndirectOffsetOnAxis(ap=index, axis=0))

        def put(pool, table, index, source):
            return pool.indirect_dma_start(table, bass.IndirectOffsetOnAxis(ap=index, axis=0), source, None)

        def feed_sp(sp, name, index=None, loads=(), saved=False, clear=None):
            with sp.Fori(0, IT) as it:
                for b in range(2):
                    sp.wait_ge(S[f"free{b}"], it + (FREE[name] + 1))
                    if saved:
                        sp.wait_ge(S[f"{name}_saved{b}"], it * 16 + CREDIT)
                    if index is not None:
                        sp.dma_start(idx[b][:], cols(index, it, b)).then_inc(S[f"fed{b}"], 16)
                    for table, f, buf in loads:
                        sp.dma_start(rows(buf[b], f), chunk(table, f, it, b)).then_inc(S[f"loaded{b}"], 16)
                    if clear is not None:
                        part = J // (2 * IT) * clear.shape[1]
                        sp.dma_start(clear[0:EP, :].rearrange("(p j) f -> p (j f)", j=J)[:, bass.ds(it * (2 * part) + b * part, part)],
                                     WIDE[:, 0:part]).then_inc(S["add_filled"], 16)

        def gather_pool(pool, name, table, f):
            with pool.Fori(0, IT) as it:
                for b in range(2):
                    pool.wait_ge(S[f"fed{b}"], it * 16 + (FED[name] + 16))
                    pool.sem_inc(S["paced"], 1)
                    for j in range(CJ):
                        fetch(pool, G[b][:, j * f:(j + 1) * f], table, idx[b][:, j:j + 1]).then_inc(S[f"rows{ROWS[name][0]}{b}"], 16)

        def prepare_act(act, name, o, it, b, spread=0):
            act.wait_ge(S["scanned"], it * 2 + (SCANNED[name] + b + 1))
            same = cols(o.same, it, b)
            act.copy(by_feature(MR, 64)[:, :, 1:CJ], same[:, 1:CJ].unsqueeze(1).broadcast_to([P, 64, CJ - 1]))
            last = act.copy(m0[:], same[:, 0:1])
            if spread:
                k = PASS_LOADS[name]
                act.wait_ge(S[f"loaded{b % 2}"], it * (16 * k) + (LOADED[name] + 16 * k * (1 + b // 2)))
                last = act.copy(by_feature(XP, spread), X[b % 2][:, 0:CJ * spread].rearrange("p (j f) -> p f j", f=spread))
            last.then_inc(S["prepared"], 1)

        def prepared_ahead_act(act, name, o, spread, first, last):
            prepare_act(act, name, o, 0, 0, spread)

            def step(it, more):
                for b in range(2):
                    first(it, b)
                    if more or b == 0:
                        prepare_act(act, name, o, it, b + 1, spread)
                    last(it, b)

            with act.Fori(0, IT - 1) as it:
                step(it, True)
            step(IT - 1, False)

        def finish_act(act, name, it, b, f, table, out=None):
            out = out or OUT
            act.wait_ge(S["scanned"], it * 2 + (SCANNED[name] + b + 2))
            act.wait_ge(S[f"stored{b}"], it * (16 * PASS_STORES[name]) + STORED[name])
            act.copy(rows(out[b], f), turned(M, f))
            act.drain()
            act.dma_start(chunk(table, f, it, b), rows(out[b], f)).then_inc(S[f"stored{b}"], 16)

        def plain_act(act, name, o, f, table):
            with act.Fori(0, IT) as it:
                for b in range(2):
                    prepare_act(act, name, o, it, b)
                    finish_act(act, name, it, b, f, table)

        def scan(dve, buf, f, kept, at=0):
            first = by_feature(buf, f, at)[:, :, 0]
            dve.scalar_tensor_tensor(first, kept[:, at:at + f], m0[:], first, ALU.mult, ALU.add)
            dve.drain()
            for a in range(0, f, 64):
                n = min(f - a, 64)
                run = buf[:, (at + a) * CJ:(at + a + n) * CJ]
                dve.tensor_tensor_scan(run, MR[:, 0:n * CJ], run, 0.0, ALU.mult, ALU.add)
            dve.drain()
            return dve.tensor_copy(kept[:, at:at + f], by_feature(buf, f, at)[:, :, CJ - 1])

        def begin(dve, name, kept):
            if name in MATCHES:
                ready(dve, "match_begun")
            dve.drain()
            dve.memset(by_feature(MR, 64)[:, :, 0], 0.0)
            dve.memset(kept, 0.0)
            dve.drain()
            dve.sem_inc(S["scanned"], 1)
            for b in range(2):
                dve.sem_inc(S[f"free{b}"], 1)

        def await_prepared(dve, name, it, b):
            dve.wait_ge(S["prepared"], it * 2 + (PREPARED[name] + b + 1))

        def plain_pass_dve(dve, name, f, weighted=False, beside=None):
            begin(dve, name, carry[:, 0:f])
            with dve.Fori(0, IT) as it:
                for b in range(2):
                    g, m = rows(G[b], f), turned(M, f)
                    if weighted:
                        dve.tensor_copy(side[b][:, 0:CJ], cols(w_d, it, b))
                        dve.drain()
                    dve.wait_ge(S[f"rows{ROWS[name][0]}{b}"], it * (16 * CJ) + (ROWS[name][1] + 16 * CJ))
                    await_prepared(dve, name, it, b)
                    if weighted:
                        dve.tensor_tensor(m, g, over(side[b][:, 0:CJ], f), ALU.mult).then_inc(S[f"free{b}"], 1)
                    else:
                        dve.tensor_copy(m, g).then_inc(S[f"free{b}"], 1)
                    dve.drain()
                    scan(dve, M, f, carry).then_inc(S["scanned"], 1)
                    dve.drain()
                    if beside:
                        beside(dve, it, b)

        def ends_dve(dve, name, f, stores=1, wait=True):
            for b in range(2):
                dve.wait_ge(S[f"stored{b}"], STORED[name] + 16 * IT * stores)
            dve.sem_inc(S["carried"], 1)
            dve.wait_ge(S["crossed"], ENDED[name] + 1)
            dve.wait_ge(S["join_read"], 16 * (ENDED[name] + 1))
            dve.tensor_tensor(joined[:, 0:f], joined[:, 0:f], psB[1][:, 0:f], ALU.add)
            dve.drain()
            dve.sem_inc(S["join"], 1)
            if wait:
                dve.wait_ge(S["ends"], 16 * NT * (ENDED[name] + 1))

        def ends_pe(pe, name, o, f):
            pe.wait_ge(S["carried"], ENDED[name] + 1)
            pe.matmul(psB[1][:, 0:f], o.equal[:], carry[:, 0:f], start=True, stop=True).then_inc(S["crossed"], 1)

        HK = HEADS * (DH + 1)
        LEFT, SUM_W = slice(HEADS, HEADS + HK), slice(HEADS + HK, HEADS + HK + 1)

        def scores_ends_dve(dve):
            top, both, shifts = sums[:, 0:4], sums[:, 4:8], sums[:, 8:20]
            scale = lambda i: over(sums[:, 20 + 4 * i:24 + 4 * i], DH + 1)
            heads = lambda a: a.rearrange("p (h k) -> p h k", h=HEADS)
            for b in range(2):
                dve.wait_ge(S[f"stored{b}"], STORED["scores"] + 16 * IT)
            for h in range(HEADS):
                dve.tensor_scalar(T[:, h * P:(h + 1) * P], ident[:], carry[:, h:h + 1], None, ALU.mult)
            dve.tensor_scalar(HB[:, 0:P], OD.all_equal[:], BIG, -BIG, ALU.mult, ALU.add)
            dve.drain()
            dve.sem_inc(S["carried"], 1)
            dve.wait_ge(S["maxima_crossed"], 1)
            for h in range(HEADS):
                dve.tensor_tensor(T[:, h * P:(h + 1) * P], psB[0][:, h * P:(h + 1) * P], HB[:, 0:P], ALU.add)
            dve.drain()
            dve.tensor_reduce(top, T[:, 0:HEADS * P].rearrange("p (h q) -> p h q", h=HEADS), AX.X, ALU.max)
            dve.wait_ge(S["join_read"], 16)
            dve.drain()
            dve.tensor_tensor(both, joined[:, 0:HEADS], top, ALU.max)
            dve.drain()
            dve.tensor_tensor(shifts[:, 0:4], carry[:, 0:HEADS], top, ALU.subtract)
            dve.tensor_tensor(shifts[:, 4:8], joined[:, 0:HEADS], both, ALU.subtract)
            dve.tensor_tensor(shifts[:, 8:12], top, both, ALU.subtract)
            ready(dve, "join_shifts")
            dve.wait_ge(S["join_scales"], 1)
            dve.tensor_tensor(heads(carry[:, LEFT]), heads(carry[:, LEFT]), scale(0), ALU.mult)
            ready(dve, "carry_scaled")
            dve.wait_ge(S["crossed"], 1)
            dve.tensor_tensor(heads(joined[:, LEFT]), heads(joined[:, LEFT]), scale(1), ALU.mult)
            dve.tensor_tensor(heads(T[:, 0:HK]), heads(psB[1][:, LEFT]), scale(2), ALU.mult)
            dve.drain()
            dve.tensor_tensor(joined[:, LEFT], joined[:, LEFT], T[:, 0:HK], ALU.add)
            dve.tensor_tensor(joined[:, SUM_W], joined[:, SUM_W], psB[1][:, SUM_W], ALU.add)
            dve.tensor_copy(joined[:, 0:HEADS], both)
            dve.drain()
            dve.sem_inc(S["join"], 1)
            dve.wait_ge(S["ends"], 16 * NT)

        def scores_ends_pe(pe):
            pe.wait_ge(S["carried"], 1)
            pe.matmul(psB[0][:, 0:HEADS * P], ones[:], T[:, 0:HEADS * P], start=True, stop=True).then_inc(S["maxima_crossed"], 1)
            pe.wait_ge(S["carry_scaled"], 1)
            pe.matmul(psB[1][:, 0:41], OD.equal[:], carry[:, 0:41], start=True, stop=True).then_inc(S["crossed"], 1)

        def ends_pool(pool, name, o, f, to=NODE[0]):
            pool.wait_ge(S["carried"], ENDED[name] + 1)
            fetch(pool, joined[:, 0:f], R[f], o.join[:]).then_inc(S["join_read"], 16)
            pool.wait_ge(S["join"], ENDED[name] + 1)
            put(pool, R[f], o.join[:], joined[:, 0:f]).then_inc(S["joined"], 16)
            pool.wait_ge(S["joined"], 16 * (ENDED[name] + 1))
            for t in range(NT):
                fetch(pool, to[:, t * f:(t + 1) * f], R[f], o.end[:, t:t + 1]).then_inc(S["ends"], 16)

        def spread_pool(pool, name, o, f, source, xtable):
            for t in range(NT):
                put(pool, xtable, o.start[:, t:t + 1], source[:, t * f:(t + 1) * f]).then_inc(S[f"{name}_spread"], 16)

        def spread_first_pool(pool, name, o, f, table, kept):
            fetch(pool, kept[:, 0:f], table, o.first[:]).then_inc(S[f"{name}_first"], 16)

        def match_pe(pe, name):
            n = MATCHES.index(name)
            turn, width = ADDS.get(name, (0, 0))

            def broadcast(it, k):
                pe.wait_ge(S["matched"], it * (2 * GROUPS) + (n * 2 * GROUPS * IT + k - 1 + BANKS))
                pe.sem_inc(S["paced"], 1)
                for i in range(GROUP):
                    col = GROUP * k + i
                    last = pe.matmul(psB[k % 2][:, i * P:(i + 1) * P], digit_ident[:, col:col + 1].broadcast_to([P, P]),
                                     src_t[:, bass.ds(it * P, P)], start=True, stop=True)
                last.then_inc(S["broadcast"], 1)

            def add_up(it, b, u):
                k = b * GROUPS + u
                pe.wait_ge(S["matched"], it * (2 * GROUPS) + (n * 2 * GROUPS * IT + k + 1 + BANKS))
                pe.wait_ge(S["sums_copied"], it * (2 * GROUPS) + (turn * 2 * GROUPS * IT + k - 1 + BANKS))
                for i in range(GROUP):
                    ps, at, j = (psO, psD)[i // 2][k % 2], i % 2 * width, GROUP * u + i
                    equal = packT[k % 2][:, i * P:(i + 1) * P]
                    last = pe.matmul(ps[:, at:at + width], equal, G[b][:, j * width:(j + 1) * width], start=True, stop=True)
                last.then_inc(S["added_up"], 1)

            pe.wait_ge(S["match_begun"], n + 1)
            with pe.Fori(0, IT) as it:
                for b in range(2):
                    broadcast(it, b * GROUPS)
                    for u in range(GROUPS):
                        if u + 1 < GROUPS:
                            broadcast(it, b * GROUPS + u + 1)
                        if width:
                            add_up(it, b, u)

        def match_dve(dve, name, it, b, each=None):
            n = MATCHES.index(name)
            dve.tensor_copy(key_cols[:], cols(src_keys, it, b))
            dve.drain()
            for u in range(GROUPS):
                k = b * GROUPS + u
                dve.wait_ge(S["broadcast"], it * (2 * GROUPS) + (n * 2 * GROUPS * IT + k + 1))
                if name in ADDS:
                    dve.wait_ge(S["added_up"], it * (2 * GROUPS) + (ADDS[name][0] * 2 * GROUPS * IT + k - 1 + BANKS))
                by_col = lambda a: a[:].rearrange("p (j q) -> p j q", q=P)
                dve.tensor_tensor(by_col(packT[k % 2]), by_col(psB[k % 2]), over(key_cols[:, GROUP * u:GROUP * (u + 1)], P),
                                  ALU.is_equal).then_inc(S["matched"], 1)
                if each:
                    each(by_col(packT[k % 2]), bass.ds(it * (2 * CJ) + GROUP * k, GROUP))
            dve.drain()

        repeated = HB[:, 0:J]

        def find_repeated(dve, it, b):
            def each(equal, at):
                dve.drain()
                dve.tensor_tensor(equal, equal, before[:].unsqueeze(1).broadcast_to([P, GROUP, P]), ALU.mult)
                dve.drain()
                dve.tensor_reduce(repeated[:, at], equal, AX.X, ALU.max)
                dve.drain()
            match_dve(dve, "gcn1", it, b, each)

        def add_rows_dve(dve):
            spare, rel = sums[:, 0:1], T[:, 0:J]
            dve.tensor_scalar(spare, part_id[:], float(NR), None, ALU.add)
            dve.drain()
            dve.tensor_scalar(repeated, repeated, -1.0, 1.0, ALU.mult, ALU.add)
            dve.tensor_scalar(rel, src_keys[:], spare, None, ALU.subtract)
            dve.drain()
            dve.tensor_tensor(rel, rel, repeated, ALU.mult)
            dve.drain()
            dve.tensor_scalar(HB[:, J:2 * J].bitcast(I32), rel, spare, None, ALU.add)
            ready(dve, "add_rows_made")

        def sums_act(act, name, it, b):
            turn, width = ADDS[name]
            act.wait_ge(S[f"rows_left{b}"], it + (turn * IT + 1))
            act.sem_inc(S["paced"], 1)
            act.dma_start(add_idx[b][:], cols(ADD_ROWS, it, b)).then_inc(S[f"add_fed{b}"], 16)
            for u in range(GROUPS):
                k = b * GROUPS + u
                act.wait_ge(S["added_up"], it * (2 * GROUPS) + (turn * 2 * GROUPS * IT + k + 1 + BANKS))
                for i, ps in enumerate((psO, psD)):
                    at = (GROUP * u + 2 * i) * width
                    last = act.copy(OUT[b][:, at:at + 2 * width], ps[k % 2][:, 0:2 * width])
                last.then_inc(S["sums_copied"], 1)
            act.drain()
            act.sem_inc(S["sums_out"], 1)
            act.sem_inc(S[f"free{b}"], 1)

        def add_pool(pool, name):
            turn, width = ADDS[name]
            if turn == 0:
                for k in range(TABLES):
                    put(pool, ADD[width][k], spare_rows[:], zeros[:]).then_inc(S[f"added{k}"], 16)
                pool.sem_inc(S["rows_left0"], 1)
            per = CJ // TABLES
            with pool.Fori(0, IT) as it:
                for b in range(2):
                    pool.wait_ge(S[f"add_fed{b}"], it * 16 + (turn * 16 * IT + 16))
                    pool.sem_inc(S["paced"], 1)
                    pool.wait_ge(S["sums_out"], it * 2 + (turn * 2 * IT + b + 1))
                    pool.sem_inc(S["paced"], 1)
                    for j in range(CJ):
                        k = j % TABLES
                        pool.wait_ge(S[f"added{k}"], it * (2 * per * 16) + 16 * (turn * 2 * per * IT + b * per + j // TABLES + 1))
                        pool.sem_inc(S["paced"], 1)
                        pool.indirect_dma_start(ADD[width][k], bass.IndirectOffsetOnAxis(ap=add_idx[b][:, j:j + 1], axis=0),
                                                OUT[b][:, j * width:(j + 1) * width], None, compute_op=ALU.add).then_inc(S[f"added{k}"], 16)
                        if j == TABLES - 1:
                            pool.sem_inc(S[f"rows_left{1 - b}"], 1)
            for k in range(TABLES):
                pool.wait_ge(S[f"added{k}"], 16 * ((turn + 1) * 2 * per * IT + 1))
            pool.sem_inc(S["all_added"], 1)

        ADD_SLOT = {"upair": [0, 2, 4, 6], "dh1": [0, 1, 2, 3], "back": [1, 2, 3, 4]}

        def add_place(name, k):
            at = ADD_SLOT[name][k] * SLOT
            return arena[:, at:at + NT * ADDS[name][1]]

        def load_sums_sp(sp, name):
            turn, width = ADDS[name]
            sp.wait_ge(S["all_added"], turn + 1)
            for k in range(TABLES):
                sp.dma_start(add_place(name, k), by_node(ADD[width][k][0:NR, :])).then_inc(S[f"sums_back{k % 2}"], 16)

        def sums_dve(dve, name):
            turn, _ = ADDS[name]
            a = [add_place(name, k) for k in range(TABLES)]
            for b in range(2):
                dve.wait_ge(S[f"sums_back{b}"], 32 * (turn + 1))
            dve.tensor_tensor(a[0], a[0], a[1], ALU.add)
            dve.tensor_tensor(a[2], a[2], a[3], ALU.add)
            dve.drain()
            dve.tensor_tensor(a[0], a[0], a[2], ALU.add)
            dve.drain()

        CLEAR = [t[:].rearrange("(p t) f -> p (t f)", p=P) for f in ADD for t in ADD[f]]
        CLEAR = [c for t in CLEAR for c in ([t] if t.shape[1] <= 4096 else [t[:, 0:t.shape[1] // 2], t[:, t.shape[1] // 2:]])]
        ADD_FILLS = len(CLEAR) + 2 * 2 * IT

        def clear_sp(sp, part):
            for c in CLEAR[part * len(CLEAR) // 4:(part + 1) * len(CLEAR) // 4]:
                sp.dma_start(c, WIDE[:, 0:c.shape[1]]).then_inc(S["add_filled"], 16)

        def norm_relu(dve, n, dst, src, tmp):
            s0, s1, s2 = scalars(0), scalars(1), scalars(2)
            dve.tensor_reduce(s0, src, AX.X, ALU.add)
            dve.drain()
            dve.tensor_scalar(s0, s0, 1.0 / 32, None, ALU.mult)
            dve.drain()
            dve.tensor_tensor(dst, src, over(s0, 32), ALU.subtract)
            dve.drain()
            dve.tensor_tensor(tmp, dst, dst, ALU.mult)
            dve.drain()
            dve.tensor_reduce(s1, tmp, AX.X, ALU.add)
            dve.drain()
            dve.tensor_scalar(s1, s1, 1.0 / 32, EPS, ALU.mult, ALU.add).then_inc(S["variance"], 1)
            dve.wait_ge(S["deviation"], n)
            dve.reciprocal(s2, s2)
            dve.drain()
            dve.tensor_tensor(dst, dst, over(s2, 32), ALU.mult)
            dve.drain()
            dve.tensor_scalar(dst, dst, 0.0, None, ALU.max)
            dve.drain()

        def deviation_act(act, n):
            act.wait_ge(S["variance"], n)
            act.activation(scalars(2), scalars(1), ACT.Sqrt).then_inc(S["deviation"], 1)

        def graph_norm(dve, layer, v, f, tmp):
            i = f"{layer}"
            col = lambda k: sums[:, k * 64:k * 64 + f]
            row = lambda k: col(k).unsqueeze(1).broadcast_to([P, NT, f])
            by_feature = lambda a: a.rearrange("p t f -> p f t")
            b, ga, gw, gb = (vectors[:, VAT[f"L1_gnn_{n}"][0]:VAT[f"L1_gnn_{n}"][0] + f]
                             for n in (f"b{i}", f"g{i}a", f"g{i}w", f"g{i}b"))
            dve.tensor_reduce(col(0), by_feature(v), AX.X, ALU.add).then_inc(S["part_sum"], 1)
            dve.wait_ge(S["node_sum"], 2 * layer - 1)
            dve.scalar_tensor_tensor(col(1), psD[0][:, 0:f], 1.0 / N, b, ALU.mult, ALU.add)
            dve.drain()
            dve.tensor_tensor(col(1), col(1), ga, ALU.mult)
            dve.drain()
            dve.tensor_tensor(col(1), col(1), b, ALU.subtract)
            dve.drain()
            dve.tensor_tensor(tmp, v, row(1), ALU.subtract)
            dve.drain()
            dve.tensor_tensor(tmp, tmp, tmp, ALU.mult)
            dve.drain()
            dve.tensor_reduce(col(0), by_feature(tmp), AX.X, ALU.add).then_inc(S["part_sum"], 1)
            dve.wait_ge(S["node_sum"], 2 * layer)
            dve.tensor_scalar(col(2), psD[0][:, 0:f], 1.0 / N, EPS, ALU.mult, ALU.add).then_inc(S["graph_var"], 1)
            dve.wait_ge(S["graph_std"], layer)
            dve.reciprocal(col(3), col(3))
            dve.drain()
            dve.tensor_tensor(col(4), col(3), gw, ALU.mult)
            dve.tensor_tensor(col(5), col(3), gw, ALU.mult)
            dve.drain()
            dve.tensor_tensor(col(1), col(1), col(4), ALU.mult)
            dve.drain()
            dve.tensor_tensor(col(6), gb, col(1), ALU.subtract)
            dve.tensor_tensor(col(7), gb, col(1), ALU.subtract)
            dve.drain()

        def graph_norm_pe(pe, layer, f):
            for k in (2 * layer - 1, 2 * layer):
                pe.wait_ge(S["part_sum"], k)
                pe.matmul(psD[0][:, 0:f], real[:], sums[:, 0:f], start=True, stop=True).then_inc(S["node_sum"], 1)

        def graph_norm_turn_pe(pe, layer):
            pe.wait_ge(S["norm_rows"], layer)
            for k in range(2):
                last = pe.transpose(psD[1][:, k * P:(k + 1) * P], sums[:, 256 + k * P:256 + (k + 1) * P], ident[:])
            last.then_inc(S["norm_turned"], 1)

        def normed_product_act(act, name, layer):
            act.wait_ge(S["norm_turned"], layer)
            act.copy(norm_cols[:], psD[1][:, 0:2 * P].rearrange("p (k q) -> p k q", k=2)[:, :, 0])
            act.drain()
            product_act(act, name, norm_cols[:, 0:1], norm_cols[:, 1:2])

        def graph_norm_act(act, layer, f):
            act.wait_ge(S["graph_var"], layer)
            act.activation(sums[:, 192:192 + f], sums[:, 128:128 + f], ACT.Sqrt).then_inc(S["graph_std"], 1)

        def ready(dve, name):
            dve.drain()
            dve.sem_inc(S[name], 1)

        def flat(i, f):
            return NODE[i][:, 0:NT * f]

        def store_node(sp, name, table, i, f, nth=1):
            sp.wait_ge(S[f"{name}_made"], nth)
            sp.dma_start(by_node(table), flat(i, f)).then_inc(S[f"{name}_kept"], 16)

        def load_node(sp, name, table, i, f, kept, nth=1):
            sp.wait_ge(S[kept], 16 * nth)
            sp.wait_ge(S["room"], LOADS.index(name) + 1)
            sp.dma_start(flat(i, f), by_node(table)).then_inc(S["back"], 16)

        def fetch_back(dve, name):
            ready(dve, "room")
            dve.wait_ge(S["back"], 16 * (LOADS.index(name) + 1))

        W_SRC = VAT["L2_gnn_W_attn"][0]

        block = ctx.enter_context(nc.Block())

        @block.vector
        def _(dve):
            dve.wait_ge(S["weights"], 32)
            dve.memset(ones[:], 1.0)
            dve.memset(G[0], 0.0)
            dve.memset(half[:], 0.5)
            dve.memset(zeros[:], 0.0)
            dve.memset(OD.ends[:], -1.0)
            dve.wait_ge(S["iotas"], 1)
            dve.tensor_scalar(real[:, 0:1], part_id[:], float(N // NT), None, ALU.is_lt)
            dve.drain()
            dve.tensor_scalar(real[:], ones[:], real[:, 0:1], None, ALU.mult)
            dve.tensor_scalar(before[:], digits[:], part_id[:], None, ALU.is_lt)
            dve.tensor_scalar(ident[:], digits[:], part_id[:], None, ALU.is_equal)
            ready(dve, "zeros")
            dve.wait_ge(S["edges"], 16 * 4)
            dve.tensor_copy(key, T[:, J:2 * J].bitcast(I32))
            ready(dve, "order_key")
            dve.tensor_copy(src_keys[:], T[:, 0:J].bitcast(I32))
            whole, digit = (a[:, 0:IT * P].bitcast(I32) for a in (M, MR))
            for d, (op, by) in enumerate(((ALU.bitwise_and, LO - 1), (ALU.arith_shift_right, LO.bit_length() - 1))):
                part = slice(d * 2 * CJ, (d + 1) * 2 * CJ)
                dve.tensor_scalar(digit[part], whole[part], by, None, op)
                dve.tensor_scalar(digit_ident[part], ident[part, part], float(LO ** d), None, ALU.mult)
            dve.drain()
            dve.tensor_copy(src_t[:], digit)
            dve.drain()
            order_dve(dve, OD)

            fetch_back(dve, "x")
            x, h = nodes(0, 32), nodes(1, 32)
            norm_relu(dve, 1, h, x, nodes(2, 32))
            pad(dve, 1)
            ready(dve, "product_in")
            kv, q = nodes(2, 64), nodes(3, 32)

            def split_kvq(t, ps):
                dve.tensor_copy(kv[:, t, :], ps[:, :, 0:64])
                return dve.tensor_copy(q[:, t, :], ps[:, :, 64:96])
            product_dve(dve, "kvq", split_kvq, 96)
            dve.tensor_tensor(x, x, h, ALU.add)
            ready(dve, "kv_made")
            ready(dve, "q_made")
            ready(dve, "res0_made")
            for name in ("kv_kept", "q_kept", "res0_kept"):
                dve.wait_ge(S[name], 16)
            dve.wait_ge(S["scores_spread"], 16 * NT)
            dve.wait_ge(S["scores_first"], 16)

            dve.wait_ge(S["filled"], 16 * FILLS)
            begin(dve, "scores", carry[:, 0:41])
            dve.memset(carry[:, 0:HEADS], -BIG)
            dve.drain()
            with dve.Fori(0, IT) as it:
                for b in range(2):
                    W4 = HEADS * CJ
                    tie, raw, step, shift = (T[:, i * W4:(i + 1) * W4] for i in range(4))
                    top, left = M[:, 0:W4], M[:, W4:W4 + HK * CJ]
                    shrink, carried = HB[:, 0:HK * CJ], T[:, 4 * W4:4 * W4 + HK]
                    heads = lambda a: a.rearrange("p (h j) -> p h j", h=HEADS)
                    parts = lambda a: a.rearrange("p (h k j) -> p h k j", h=HEADS, k=DH + 1)
                    dve.wait_ge(S[f"rows{ROWS["scores"][0]}{b}"], it * (16 * CJ) + (ROWS["scores"][1] + 16 * CJ))
                    await_prepared(dve, "scores", it, b)
                    dve.tensor_scalar(tie, MR[:, 0:W4], BIG, -BIG, ALU.mult, ALU.add)
                    dve.tensor_scalar(neg0[:], m0[:], BIG, -BIG, ALU.mult, ALU.add)
                    scan(dve, XP, 32, spread_carry)
                    dve.tensor_tensor(rows(HB, 32), turned(XP, 32), rows(G[b], 64)[:, :, 0:32], ALU.mult)
                    dve.drain()
                    dve.tensor_reduce(side[b][:, 0:W4], HB[:, 0:CJ * 32].rearrange("p (n d) -> p n d", d=DH), AX.X, ALU.add)
                    dve.drain()
                    dve.tensor_scalar(heads(raw), side[b][:, 0:W4].rearrange("p (j h) -> p h j", h=HEADS),
                                      float(DH ** -0.5), None, ALU.mult)
                    dve.drain()
                    dve.tensor_copy(top, raw)
                    dve.drain()
                    first = heads(top)[:, :, 0]
                    dve.scalar_tensor_tensor(first, carry[:, 0:HEADS], neg0[:], first, ALU.add, ALU.max)
                    dve.drain()
                    dve.tensor_tensor_scan(top, tie, top, -BIG, ALU.add, ALU.max)
                    dve.drain()
                    dve.tensor_tensor(heads(step)[:, :, 1:CJ], heads(top)[:, :, 0:CJ - 1], heads(top)[:, :, 1:CJ], ALU.subtract)
                    dve.tensor_tensor(heads(step)[:, :, 0], carry[:, 0:HEADS], heads(top)[:, :, 0], ALU.subtract)
                    dve.tensor_tensor(shift, raw, top, ALU.subtract)
                    dve.drain()
                    dve.tensor_scalar(step, step, 0.0, None, ALU.min)
                    dve.tensor_copy(carry[:, 0:HEADS], heads(top)[:, :, CJ - 1])
                    dve.drain()
                    dve.sem_inc(S["soft_shifted"], 1)
                    dve.tensor_copy(M[:, 40 * CJ:41 * CJ], cols(w_d, it, b))
                    dve.drain()
                    scan(dve, M, 1, carry, at=40)
                    dve.wait_ge(S["soft_exp"], it * 2 + (b + 1))
                    dve.tensor_tensor(parts(shrink), parts(MR[:, 0:HK * CJ]),
                                      heads(step).unsqueeze(2).broadcast_to([P, HEADS, DH + 1, CJ]), ALU.mult)
                    dve.tensor_scalar(side[b][:, 0:HEADS], heads(step)[:, :, 0], m0[:], None, ALU.mult)
                    dve.tensor_copy(parts(left)[:, :, DH, :], heads(shift))
                    dve.tensor_tensor(left.rearrange("p (h k j) -> p j h k", h=HEADS, k=DH + 1)[:, :, :, 0:DH],
                                      rows(G[b], 64)[:, :, 32:64].rearrange("p j (h d) -> p j h d", d=DH),
                                      shift.rearrange("p (h j) -> p j h", h=HEADS).unsqueeze(3).broadcast_to([P, CJ, HEADS, DH]),
                                      ALU.mult).then_inc(S[f"free{b}"], 1)
                    dve.drain()
                    dve.tensor_tensor(carried.rearrange("p (h k) -> p h k", h=HEADS), carry[:, LEFT].rearrange("p (h k) -> p h k", h=HEADS),
                                      over(side[b][:, 0:HEADS], DH + 1), ALU.mult)
                    dve.drain()
                    first = by_feature(left, HK)[:, :, 0]
                    dve.tensor_tensor(first, first, carried, ALU.add)
                    dve.drain()
                    dve.tensor_tensor_scan(left, shrink, left, 0.0, ALU.mult, ALU.add)
                    dve.drain()
                    dve.tensor_copy(carry[:, LEFT], by_feature(left, HK)[:, :, CJ - 1]).then_inc(S["scanned"], 1)
                    dve.drain()
            scores_ends_dve(dve)
            ends = nodes(0, 41)
            s0, s1 = scalars(0), scalars(1)
            dve.tensor_scalar(s0, ends[:, :, 40], 1.0, None, ALU.add)
            dve.drain()
            dve.tensor_scalar(s1, s0, 1e-12, None, ALU.max)
            dve.tensor_scalar(scalars(3), s0, 0.0, None, ALU.is_gt)
            ready(dve, "degree")
            attn = nodes(1, 32)
            sums_of = ends[:, :, HEADS:40].rearrange("p t (h k) -> p t h k", h=HEADS)
            den = nodes(2, 4)
            dve.tensor_scalar(den, sums_of[:, :, :, DH], 1e-16, None, ALU.max)
            dve.drain()
            dve.reciprocal(den, den)
            dve.drain()
            dve.tensor_tensor(attn.rearrange("p t (h d) -> p t h d", d=DH),
                              sums_of[:, :, :, 0:DH],
                              den.unsqueeze(3).broadcast_to([P, NT, HEADS, DH]), ALU.mult)
            pad(dve, 1)
            ready(dve, "product_in")
            dve.wait_ge(S["degree_root"], 1)
            dve.reciprocal(scalars(2), scalars(2))
            dve.drain()
            dve.tensor_tensor(dis[:], scalars(2), scalars(3), ALU.mult)
            dve.drain()
            x1, h = nodes(3, 32), nodes(5, 32)
            product_dve(dve, "Wo", plain(nodes(2, 32)), 32)
            fetch_back(dve, "res0")
            dve.tensor_tensor(x1, x1, nodes(2, 32), ALU.add)
            dve.drain()
            dve.sem_inc(S["res1_made"], 1)
            norm_relu(dve, 2, h, x1, nodes(6, 32))

            dve.tensor_tensor(own(1), h, over(dis[:], 32), ALU.mult)
            ready(dve, "gcn_made")
            dve.wait_ge(S["res1_kept"], 16)
            for layer in range(1, 6):
                f = 32 if layer in (1, 5) else 64
                name = f"gcn{layer}"
                plain_pass_dve(dve, name, f, weighted=True, beside=find_repeated if layer == 1 else None)
                if layer == 1:
                    add_rows_dve(dve)
                ends_dve(dve, name, f)
                agg = nodes(2, f)
                dve.tensor_tensor(agg, nodes(0, f), own(layer), ALU.add)
                dve.drain()
                dve.tensor_tensor(agg, agg, over(dis[:], f), ALU.mult)
                if layer == 1:
                    pad(dve, 2)
                    ready(dve, "product_in")
                    agg = nodes(3, 64)
                    product_dve(dve, "L1_W1", plain(agg), 64)
                    f = 64
                dve.drain()
                if layer < 5:
                    dve.sem_inc(S["product_in"], 1)
                graph_norm(dve, layer, agg, f, nodes(4, f))
                if layer < 5:
                    dve.sem_inc(S["norm_rows"], 1)
                    if layer == 1:
                        dve.wait_ge(S["add_rows_kept"], 16)
                    product_dve(dve, f"L1_W{layer + 1}", scaled(own(layer + 1), dis), 32 if layer == 4 else 64)
                    ready(dve, "gcn_made")
                if layer == 1:
                    dve.memset(WIDE, 0.0)
                    ready(dve, "clear_zeros")
            row = lambda k: sums[:, k * 64:k * 64 + 32].unsqueeze(1).broadcast_to([P, NT, 32])
            dve.tensor_tensor(nodes(2, 32), nodes(2, 32), row(4), ALU.mult)
            dve.drain()
            dve.tensor_tensor(nodes(2, 32), nodes(2, 32), row(6), ALU.add)
            dve.drain()
            fetch_back(dve, "res1")
            x2, h = nodes(3, 32), nodes(1, 32)
            dve.tensor_tensor(x2, x2, nodes(2, 32), ALU.add)
            dve.drain()
            dve.sem_inc(S["res2_made"], 1)
            norm_relu(dve, 3, h, x2, nodes(4, 32))
            pad(dve, 1)

            ready(dve, "product_in")
            z, za = nodes(2, 64), nodes(4, 65)
            product_dve(dve, "fc_T", plain(z), 64)
            dve.drain()
            a_s, a_d = scalars(4), scalars(5)
            for part, a in ((0, a_s), (64, a_d)):
                dve.tensor_tensor(nodes(5, 64), z, vec("L2_gnn_W_attn", off=part, size=64), ALU.mult)
                dve.drain()
                dve.tensor_reduce(a, nodes(5, 64), AX.X, ALU.add)
                dve.drain()
            dve.tensor_copy(za[:, :, 0:64], z)
            dve.tensor_copy(za[:, :, 64], a_s)
            ready(dve, "za_made")
            for name in ("za_kept", "ad_kept", "res2_kept", "attend_first"):
                dve.wait_ge(S[name], 16)
            dve.wait_ge(S["attend_spread"], 16 * NT)
            begin(dve, "attend", carry[:, 0:65])
            with dve.Fori(0, IT) as it:
                for b in range(2):
                    dve.wait_ge(S[f"rows{ROWS["attend"][0]}{b}"], it * (16 * CJ) + (ROWS["attend"][1] + 16 * CJ))
                    await_prepared(dve, "attend", it, b)
                    g = rows(G[b], 65)
                    scan(dve, XP, 1, spread_carry)
                    dve.tensor_tensor(side[b][:, 0:CJ], XP[:, 0:CJ], g[:, :, 64], ALU.add).then_inc(S["attend_sum"], 1)
                    dve.wait_ge(S["attend_exp"], it * 2 + (b + 1))
                    dve.tensor_copy(M[:, 64 * CJ:65 * CJ], narrow[b][:, CJ:2 * CJ])
                    dve.tensor_tensor(turned(M, 64), g[:, :, 0:64], over(narrow[b][:, CJ:2 * CJ], 64),
                                      ALU.mult).then_inc(S[f"free{b}"], 1)
                    dve.drain()
                    scan(dve, M, 65, carry).then_inc(S["scanned"], 1)
                    dve.drain()
            for b in range(2):
                dve.wait_ge(S[f"attend_saved{b}"], CREDIT + 16 * IT)
            ends_dve(dve, "attend", 65)
            ends, h = nodes(0, 65), nodes(1, 64)
            dve.tensor_scalar(rden[:], ends[:, :, 64], 1e-30, None, ALU.max)
            dve.drain()
            dve.reciprocal(rden[:], rden[:])
            dve.drain()
            dve.tensor_tensor(h, ends[:, :, 0:64], over(rden[:], 64), ALU.mult)
            ready(dve, "h_made")
            dve.sem_inc(S["product_in"], 1)
            product_dve(dve, "h_p1", plain(nodes(2, 64)), 64)
            ready(dve, "product_in")
            product_dve(dve, "A1", plain(nodes(3, 64)), 64)
            ready(dve, "A1_made")
            dve.sem_inc(S["product_in"], 1)
            product_dve(dve, "h_p2", plain(nodes(2, 64)), 64)
            ready(dve, "product_in")
            product_dve(dve, "A2", plain(BESIDE[:, 0:NT * 64].rearrange("p (t f) -> p t f", f=64)), 64)
            ready(dve, "A2_made")
            for name in ("h_kept", "A1_kept"):
                dve.wait_ge(S[name], 16)
            dve.wait_ge(S["add_filled"], 16 * ADD_FILLS)
            plain_pass_dve(dve, "hsum", 64)
            ends_dve(dve, "hsum", 64)
            ready(dve, "product_in")
            h1 = nodes(1, 64)
            product_dve(dve, "enc", plain(h1), 64)
            dve.tensor_tensor(nodes(2, 64), over(OD.count[:], 64), vec("L2_gnn_b_encK"), ALU.mult)
            dve.drain()
            dve.tensor_tensor(h1, h1, nodes(2, 64), ALU.add)
            ready(dve, "product_in")
            product_dve(dve, "K_0", plain(nodes(2, 64)), 64)
            ready(dve, "k0_raw")
            dve.wait_ge(S["product_in"], ORDINAL["K_1"] + 1)
            product_dve(dve, "K_1", relu_to(nodes(3, 64)), 64)
            ready(dve, "product_in")
            dve.sem_inc(S["k01_made"], 1)
            product_dve(dve, "K_2", plain(nodes(4, 64)), 64)
            ready(dve, "product_in")
            product_dve(dve, "KW", plain(nodes(5, 64)), 64)
            ready(dve, "KW_made")
            for name in ("k0_kept", "k1_kept", "KW_kept", "A2_kept", "umlp_first"):
                dve.wait_ge(S[name], 16)
            dve.wait_ge(S["umlp_spread"], 16 * NT)

            rest, part, part_bf = sums[:, 0:64], sums[:, 64:128], bias_parts[:]
            dve.tensor_copy(ones_bf[:], ones[:])
            dve.tensor_copy(rest, vectors[:, VAT["L2_gnn_U_b1"][0]:VAT["L2_gnn_U_b1"][0] + 64])
            dve.memset(sums[:, 128:192], 0.0)
            for k in range(3):
                dve.drain()
                dve.tensor_copy(part_bf, rest)
                dve.drain()
                dve.tensor_copy(part, part_bf)
                dve.drain()
                dve.tensor_tensor(rest, rest, part, ALU.subtract)
                dve.scalar_tensor_tensor(sums[:, 128:192], part, ident[:, k:k + 1], sums[:, 128:192], ALU.mult, ALU.add)
            dve.drain()
            dve.tensor_copy(part_bf, sums[:, 128:192])
            dve.drain()

            for b in range(2):
                dve.memset(rows(OUT[b], 129)[:, :, 128], 1.0)
            begin(dve, "umlp", carry[:, 0:64])
            with dve.Fori(0, IT) as it:
                for b in range(2):
                    dve.wait_ge(S[f"rows{ROWS["umlp"][0]}{b}"], it * (16 * CJ) + (ROWS["umlp"][1] + 16 * CJ))
                    await_prepared(dve, "umlp", it, b)
                    g, out_rows, tb, hb = rows(G[b], 128), rows(OUT[b], 129), rows(T, 64), rows(HB, 64)
                    scan(dve, XP, 64, spread_carry)
                    for u in range(UG):
                        t = slice(8 * u, 8 * u + 8)
                        dve.tensor_tensor(tb[:, t, :], turned(XP, 64)[:, t, :], g[:, t, 64:128], ALU.add).then_inc(S["umlp_pre"], 1)
                    dve.wait_ge(S["umlp_tanh"], it * (2 * UG) + (b * UG + UG))
                    slope = rows(XP, 64)
                    dve.scalar_tensor_tensor(slope, tb, -1.0, tb, ALU.mult, ALU.mult)
                    for u in range(UG):
                        k = b * UG + u
                        t = slice(8 * u, 8 * u + 8)
                        dve.wait_ge(S["umlp_relu"], it * (2 * UG) + (k + 3))
                        dve.scalar_tensor_tensor(hb[:, t, :], out_rows[:, t, 0:64], 0.0, g[:, t, 0:64], ALU.is_gt,
                                                 ALU.mult).then_inc(S["umlp_slope"], 1)
                    for u in range(UG):
                        k = b * UG + u
                        t = slice(8 * u, 8 * u + 8)
                        dve.wait_ge(S["umlp_down"], it * (2 * UG) + (k + 1))
                        ps = psD[k % 2][:, 0:512].rearrange("p (j f) -> p j f", f=64)
                        dve.scalar_tensor_tensor(out_rows[:, t, 64:128], slope[:, t, :], 1.0, ps, ALU.add,
                                                 ALU.mult).then_inc(S["umlp_taken"], 1)
                        dve.drain()
                        last = dve.tensor_copy(turned(M, 64)[:, t, :], out_rows[:, t, 64:128])
                    last.then_inc(S[f"free{b}"], 1)
                    dve.drain()
                    scan(dve, M, 64, carry).then_inc(S["scanned"], 1)
                    dve.drain()
            ready(dve, "match_begun")
            for b in range(2):
                dve.sem_inc(S[f"free{b}"], 1)
            with dve.Fori(0, IT) as it:
                for b in range(2):
                    dve.wait_ge(S[f"loaded{b}"], it * 16 + (LOADED["upair"] + 16))
                    match_dve(dve, "upair", it, b)
            ends_dve(dve, "umlp", 64, stores=2, wait=False)
            sums_dve(dve, "upair")
            for name in ("k1", "k0"):
                ready(dve, "room")
            both = arena[:, 0:NT * 129].rearrange("p (t f) -> p t f", f=129)
            src_count = scalars(8)
            dve.tensor_copy(src_count, both[:, :, 128])
            dve.tensor_copy(nodes(2, 64), both[:, :, 0:64])
            dve.tensor_copy(nodes(3, 64), both[:, :, 64:128])
            ready(dve, "product_in")
            product_dve(dve, "b_U2", plain(nodes(5, 64)), 64)
            dve.tensor_tensor(nodes(6, 64), over(src_count, 64), vec("L2_gnn_U_b2"), ALU.mult)
            dve.drain()
            dve.tensor_tensor(nodes(5, 64), nodes(5, 64), nodes(6, 64), ALU.add)
            ready(dve, "product_in")
            product_dve(dve, "b_K2", plain(nodes(6, 64)), 64)
            dve.drain()
            dve.wait_ge(S["back"], 16 * (LOADS.index("k0") + 1))
            dve.scalar_tensor_tensor(nodes(6, 64), nodes(7, 64), 0.0, nodes(6, 64), ALU.is_gt, ALU.mult)
            ready(dve, "product_in")
            product_dve(dve, "b_K1", plain(nodes(2, 64)), 64)
            dve.tensor_tensor(nodes(4, 64), nodes(4, 64), nodes(4, 64), ALU.mult)
            dve.drain()
            dve.tensor_scalar(nodes(4, 64), nodes(4, 64), -1.0, 1.0, ALU.mult, ALU.add)
            dve.drain()
            dve.tensor_tensor(nodes(2, 64), nodes(2, 64), nodes(4, 64), ALU.mult)
            ready(dve, "product_in")
            product_dve(dve, "b_K0", plain(nodes(6, 64)), 64)
            ready(dve, "dh1_made")
            dve.sem_inc(S["product_in"], 1)
            product_dve(dve, "b_U0s", plain(nodes(2, 64)), 64)
            ready(dve, "product_in")
            product_dve(dve, "b_p1", plain(nodes(5, 64)), 64)
            dve.wait_ge(S["ends"], 16 * NT * (ENDED["umlp"] + 1))
            dve.sem_inc(S["product_in"], 1)
            product_dve(dve, "b_U0d", plain(nodes(2, 64)), 64)
            ready(dve, "product_in")
            product_dve(dve, "b_p2", plain(nodes(7, 64)), 64)
            dve.drain()
            dve.tensor_tensor(nodes(5, 64), nodes(5, 64), nodes(7, 64), ALU.add)
            ready(dve, "dhu_made")
            for name in ("dh1_kept", "dhu_kept", "dh1_first"):
                dve.wait_ge(S[name], 16)
            dve.wait_ge(S["dh1_spread"], 16 * NT)

            begin(dve, "dh1", carry[:, 0:64])
            with dve.Fori(0, IT) as it:
                for b in range(2):
                    await_prepared(dve, "dh1", it, b)
                    scan(dve, XP, 64, spread_carry)
                    dve.tensor_copy(rows(G[b], 64), turned(XP, 64)).then_inc(S["scanned"], 1)
                    dve.drain()
                    match_dve(dve, "dh1", it, b)
            sums_dve(dve, "dh1")
            ready(dve, "product_in")
            dh = nodes(1, 64)
            product_dve(dve, "b_enc", plain(dh), 64)
            fetch_back(dve, "dhu")
            fetch_back(dve, "h")
            dve.tensor_tensor(dh, dh, nodes(2, 64), ALU.add)
            dve.drain()
            dve.tensor_tensor(nodes(3, 64), nodes(3, 64), dh, ALU.mult)
            dve.drain()
            c = scalars(6)
            dve.tensor_reduce(c, nodes(3, 64), AX.X, ALU.add)
            dve.drain()
            back = nodes(4, 67)
            dve.tensor_copy(back[:, :, 0:64], dh)
            dve.tensor_copy(back[:, :, 64], a_d)
            dve.tensor_copy(back[:, :, 65], c)
            dve.tensor_copy(back[:, :, 66], rden[:])
            ready(dve, "back_made")
            for name in ("back_kept", "back_first"):
                dve.wait_ge(S[name], 16)
            dve.wait_ge(S["back_spread"], 16 * NT)

            begin(dve, "back", carry[:, 0:1])
            with dve.Fori(0, IT) as it:
                for b in range(2):
                    dve.wait_ge(S[f"loaded{b}"], it * 32 + (LOADED["back"] + 32))
                    await_prepared(dve, "back", it, b)
                    scan(dve, XP, 67, spread_carry)
                    dve.drain()
                    zr, dr = rows(G[b], 65), turned(XP, 67)
                    u, w, t = side[b], narrow[b][:, CJ:2 * CJ], narrow[b][:, 0:CJ]
                    dalpha, alpha, slope = u[:, CJ:2 * CJ], u[:, 2 * CJ:3 * CJ], u[:, 3 * CJ:4 * CJ]
                    dve.tensor_tensor(u[:, 0:CJ], zr[:, :, 64], dr[:, :, 64], ALU.add).then_inc(S["back_sum"], 1)
                    dve.tensor_tensor(rows(T, 64), zr[:, :, 0:64], dr[:, :, 0:64], ALU.mult)
                    dve.drain()
                    dve.tensor_reduce(dalpha, rows(T, 64), AX.X, ALU.add)
                    dve.drain()
                    dve.wait_ge(S["back_exp"], it * 2 + (b + 1))
                    dve.tensor_tensor(alpha, w, dr[:, :, 66], ALU.mult)
                    dve.tensor_tensor(dalpha, dalpha, dr[:, :, 65], ALU.subtract)
                    dve.tensor_tensor(slope, t, t, ALU.mult)
                    dve.drain()
                    dve.tensor_tensor(dalpha, dalpha, alpha, ALU.mult)
                    dve.tensor_scalar(slope, slope, -0.25, 0.25, ALU.mult, ALU.add)
                    dve.tensor_tensor(zr[:, :, 0:64], dr[:, :, 0:64], over(alpha, 64), ALU.mult)
                    dve.drain()
                    dve.tensor_tensor(M[:, 0:CJ], dalpha, slope, ALU.mult)
                    dve.drain()
                    dve.tensor_copy(zr[:, :, 64], M[:, 0:CJ])
                    dve.drain()
                    scan(dve, M, 1, carry).then_inc(S["scanned"], 1)
                    dve.drain()
                    match_dve(dve, "back", it, b)
            ends_dve(dve, "back", 1)
            sums_dve(dve, "back")
            gs, dz = nodes(1, 65), nodes(2, 64)
            dve.tensor_copy(scalars(7), gs[:, :, 64])
            dve.drain()
            dve.tensor_tensor(nodes(3, 64), over(scalars(7), 64), vec("L2_gnn_W_attn", off=0, size=64), ALU.mult)
            dve.tensor_tensor(nodes(4, 64), over(NODE[0][:, 0:NT], 64), vec("L2_gnn_W_attn", off=64, size=64), ALU.mult)
            dve.drain()
            dve.tensor_tensor(dz, gs[:, :, 0:64], nodes(3, 64), ALU.add)
            dve.drain()
            dve.tensor_tensor(dz, dz, nodes(4, 64), ALU.add)
            ready(dve, "product_in")
            y, yd, t2 = nodes(3, 32), nodes(4, 32), nodes(5, 32)
            product_dve(dve, "b_fc", plain(y), 32)
            pad(dve, 3)
            ready(dve, "product_in")
            product_dve(dve, "b_D", plain(yd), 32)
            dve.drain()
            dve.tensor_tensor(t2[:, :, 0:16], y[:, :, 16:32], yd[:, :, 0:16], ALU.subtract)
            dve.scalar_tensor_tensor(t2[:, :, 16:32], y[:, :, 0:16], -1.0, yd[:, :, 16:32], ALU.mult, ALU.subtract)
            fetch_back(dve, "res2")
            x3, h = nodes(6, 32), nodes(1, 32)
            dve.tensor_tensor(x3, x3, t2, ALU.add)
            dve.drain()
            dve.sem_inc(S["res3_made"], 1)
            norm_relu(dve, 4, h, x3, nodes(2, 32))

            ready(dve, "hin_made")
            dve.wait_ge(S["hin_kept"], 16)
            dve.wait_ge(S["res3_kept"], 16)
            plain_pass_dve(dve, "mean", 32)
            ends_dve(dve, "mean", 32)
            fetch_back(dve, "hin")
            cat = nodes(2, 64)
            dve.tensor_scalar(scalars(0), OD.count[:], 1.0, None, ALU.max)
            dve.drain()
            dve.reciprocal(scalars(0), scalars(0))
            dve.drain()
            dve.tensor_tensor(cat[:, :, 32:64], nodes(0, 32), over(scalars(0), 32), ALU.mult)
            dve.tensor_copy(cat[:, :, 0:32], nodes(1, 32))
            ready(dve, "product_in")
            product_dve(dve, "L3", plain(nodes(4, 32)), 32)
            dve.drain()
            dve.tensor_tensor(nodes(4, 32), nodes(4, 32), vec("L3_gnn_b"), ALU.add)
            fetch_back(dve, "res3")
            dve.scalar_tensor_tensor(nodes(4, 32), nodes(4, 32), 0.0, nodes(5, 32), ALU.max, ALU.add)
            ready(dve, "result")

        @block.scalar
        def _(act):
            def save_chunks(name, table, f, it, b):
                act.wait_ge(S[f"rows{ROWS[name][0]}{b}"], it * (16 * CJ) + (ROWS[name][1] + 16 * CJ))
                act.dma_start(chunk(table, f, it, b), rows(G[b], f)).then_inc(S[f"{name}_saved{b}"], 16)

            def sigmoid_exp(name, it, b):
                act.wait_ge(S[f"{name}_sum"], it * 2 + (b + 1))
                act.activation(narrow[b][:, 0:CJ], side[b][:, 0:CJ], ACT.Tanh, scale=0.5)
                act.drain()
                act.activation(narrow[b][:, CJ:2 * CJ], narrow[b][:, 0:CJ], ACT.Exp, scale=0.5,
                               bias=half[:]).then_inc(S[f"{name}_exp"], 1)

            deviation_act(act, 1)
            product_act(act, "kvq")
            with act.Fori(0, IT) as it:
                for b in range(2):
                    prepare_act(act, "scores", OD, it, b, spread=32)
                    act.wait_ge(S["soft_shifted"], it * 2 + (b + 1))
                    shifts = T[:, 2 * HEADS * CJ:4 * HEADS * CJ]
                    act.activation(shifts, shifts, ACT.Exp).then_inc(S["soft_exp"], 1)
                    finish_act(act, "scores", it, b, 41, R[41])
            act.wait_ge(S["join_shifts"], 1)
            act.activation(sums[:, 20:32], sums[:, 8:20], ACT.Exp).then_inc(S["join_scales"], 1)
            act.wait_ge(S["degree"], 1)
            act.activation(scalars(2), scalars(1), ACT.Sqrt).then_inc(S["degree_root"], 1)
            product_act(act, "Wo")
            deviation_act(act, 2)
            for layer in range(1, 6):
                f = 32 if layer in (1, 5) else 64
                plain_act(act, f"gcn{layer}", OD, f, R[f])
                if layer == 1:
                    product_act(act, "L1_W1")
                graph_norm_act(act, layer, 32 if layer == 5 else 64)
                if layer < 5:
                    normed_product_act(act, f"L1_W{layer + 1}", layer)
            deviation_act(act, 3)
            product_act(act, "fc_T")
            with act.Fori(0, IT) as it:
                for b in range(2):
                    prepare_act(act, "attend", OD, it, b, spread=1)
                    save_chunks("attend", ZA, 65, it, b)
                    sigmoid_exp("attend", it, b)
                    finish_act(act, "attend", it, b, 65, R[65])
            for name in ("h_p1", "A1", "h_p2", "A2"):
                product_act(act, name)
            plain_act(act, "hsum", OD, 64, R[64])
            product_act(act, "enc")
            product_act(act, "K_0")
            act.wait_ge(S["k0_raw"], 1)
            act.activation(flat(2, 64), flat(2, 64), ACT.Tanh).then_inc(S["product_in"], 1)
            for name in ("K_1", "K_2", "KW"):
                product_act(act, name)
            with act.Fori(0, IT) as it:
                for b in range(2):
                    prepare_act(act, "umlp", OD, it, b, spread=64)
                    for u in range(UG):
                        act.wait_ge(S["umlp_pre"], it * (2 * UG) + (b * UG + u + 1))
                        part = T[:, 512 * u:512 * (u + 1)]
                        act.activation(part, part, ACT.Tanh).then_inc(S["umlp_tanh"], 1)
                    act.wait_ge(S[f"stored{b}"], it * 32 + STORED["umlp"])
                    for u in range(UG):
                        k = b * UG + u
                        act.wait_ge(S["umlp_turned"], it * (2 * UG) + (k + 1))
                        act.copy(packT[k % 2][:], psT[k % 2][:]).then_inc(S["umlp_turned_copied"], 1)
                        act.wait_ge(S["umlp_up"], it * (2 * UG) + (k + 1))
                        act.activation(rows(OUT[b], 129)[:, 8 * u:8 * u + 8, 0:64],
                                       psO[k % 2][:].rearrange("p (j f) -> p j f", f=64), ACT.Relu).then_inc(S["umlp_relu"], 1)
                    for u in range(UG):
                        k = b * UG + u
                        act.wait_ge(S["umlp_turned_down"], it * (2 * UG) + (k + 1))
                        act.copy(packB[k % 2][:], psB[k % 2][:]).then_inc(S["umlp_down_copied"], 1)
                    finish_act(act, "umlp", it, b, 64, R[64], out=H)
                    act.dma_start(chunk(UD, 129, it, b), rows(OUT[b], 129)).then_inc(S[f"stored{b}"], 16)
            act.wait_ge(S["add_rows_kept"], 16)
            for b in range(2):
                act.wait_ge(S[f"stored{b}"], STORED["upair"])
            with act.Fori(0, IT) as it:
                for b in range(2):
                    sums_act(act, "upair", it, b)
            for name in ("b_U2", "b_K2", "b_K1", "b_K0", "b_U0s", "b_p1", "b_U0d", "b_p2"):
                product_act(act, name)
            prepared_ahead_act(act, "dh1", OD, 64, lambda it, b: None, lambda it, b: sums_act(act, "dh1", it, b))
            product_act(act, "b_enc")

            def back_dpre(it, b):
                sigmoid_exp("back", it, b)
                finish_act(act, "back", it, b, 1, R[1], out=H)

            prepared_ahead_act(act, "back", OD, 67, back_dpre, lambda it, b: sums_act(act, "back", it, b))
            product_act(act, "b_fc")
            product_act(act, "b_D")
            deviation_act(act, 4)
            plain_act(act, "mean", OD, 32, R[32])
            product_act(act, "L3")

        @block.tensor
        def _(pe):
            pe.wait_ge(S["weights"], 32)
            pe.wait_ge(S["zeros"], 1)
            for name in ("matched", "added_up", "sums_copied"):
                pe.sem_inc(S[name], BANKS)
            order_pe(pe, OD)
            product_pe(pe, "kvq", "kvq", NODE[1])
            scores_ends_pe(pe)
            product_pe(pe, "Wo", "Wo", NODE[1])
            for layer in range(1, 6):
                f = 32 if layer in (1, 5) else 64
                if layer == 1:
                    match_pe(pe, "gcn1")
                ends_pe(pe, f"gcn{layer}", OD, f)
                if layer == 1:
                    product_pe(pe, "L1_W1", "L1_W1", NODE[2])
                graph_norm_pe(pe, layer, 32 if layer == 5 else 64)
                if layer < 5:
                    graph_norm_turn_pe(pe, layer)
                    product_pe(pe, f"L1_W{layer + 1}", f"L1_W{layer + 1}", NODE[3 if layer == 1 else 2])
            product_pe(pe, "fc_T", "fc_T", NODE[1])
            ends_pe(pe, "attend", OD, 65)
            product_pe(pe, "h_p1", "p1_T", NODE[1], "L2_gnn_b_p1")
            product_pe(pe, "A1", "U0_T", NODE[2], "L2_gnn_U_b0")
            product_pe(pe, "h_p2", "p2_T", NODE[1], "L2_gnn_b_p2")
            product_pe(pe, "A2", "U0_T", NODE[2])
            ends_pe(pe, "hsum", OD, 64)
            product_pe(pe, "enc", "encK_T", NODE[0])
            product_pe(pe, "K_0", "K0_T", NODE[1], "L2_gnn_K_b0")
            product_pe(pe, "K_1", "K1_T", NODE[2], "L2_gnn_K_b1")
            product_pe(pe, "K_2", "K2_T", NODE[3], "L2_gnn_K_b2")
            product_pe(pe, "KW", "U2", NODE[4])
            for name in ("umlp_turned_copied", "umlp_relu", "umlp_down_copied", "umlp_taken"):
                pe.sem_inc(S[name], 2)
            up, down = WAT["U1_T"][0], WAT["U1"][0]
            with pe.Fori(0, IT) as it:
                for b in range(2):
                    n = 2 * UG
                    for u in range(UG):
                        k = b * UG + u
                        pe.wait_ge(S["umlp_tanh"], it * n + (k + 1))
                        pe.wait_ge(S["umlp_turned_copied"], it * n + (k + 1))
                        for i in range(4):
                            last = pe.transpose(psT[k % 2][:, i * P:(i + 1) * P], T[:, (4 * u + i) * P:(4 * u + i + 1) * P], ident[:])
                        last.then_inc(S["umlp_turned"], 1)
                        pe.wait_ge(S["umlp_turned_copied"], it * n + (k + 3))
                        pe.wait_ge(S["umlp_relu"], it * n + (k + 1))
                        pe.matmul(psO[k % 2][:].rearrange("p (j f) -> p j f", f=64), ones_bf[:],
                                  bias_parts[:].unsqueeze(1).broadcast_to([P, 8, 64]),
                                  start=True, stop=False, skip_group_check=True)
                        for i in range(4):
                            last = pe.matmul(psO[k % 2][:, i * P:(i + 1) * P], packT[k % 2][:, i * P:(i + 1) * P],
                                             weights[:, up:up + P], start=False, stop=True, skip_group_check=True)
                        last.then_inc(S["umlp_up"], 1)
                    for u in range(UG):
                        k = b * UG + u
                        pe.wait_ge(S["umlp_slope"], it * n + (k + 1))
                        pe.wait_ge(S["umlp_down_copied"], it * n + (k + 1))
                        for i in range(4):
                            last = pe.transpose(psB[k % 2][:, i * P:(i + 1) * P], HB[:, (4 * u + i) * P:(4 * u + i + 1) * P], ident[:])
                        last.then_inc(S["umlp_turned_down"], 1)
                        pe.wait_ge(S["umlp_down_copied"], it * n + (k + 3))
                        pe.wait_ge(S["umlp_taken"], it * n + (k + 1))
                        for i in range(4):
                            last = pe.matmul(psD[k % 2][:, i * P:(i + 1) * P], packB[k % 2][:, i * P:(i + 1) * P],
                                             weights[:, down:down + P], start=True, stop=True)
                        last.then_inc(S["umlp_down"], 1)
            match_pe(pe, "upair")
            ends_pe(pe, "umlp", OD, 64)
            product_pe(pe, "b_U2", "U2_T", NODE[2])
            product_pe(pe, "b_K2", "K2", NODE[5])
            product_pe(pe, "b_K1", "K1", NODE[6])
            product_pe(pe, "b_K0", "K0", NODE[2])
            product_pe(pe, "b_U0s", "U0", NODE[3])
            product_pe(pe, "b_p1", "p1", NODE[2])
            product_pe(pe, "b_U0d", "U0", BESIDE)
            product_pe(pe, "b_p2", "p2", NODE[2])
            match_pe(pe, "dh1")
            product_pe(pe, "b_enc", "encK", NODE[0])
            match_pe(pe, "back")
            ends_pe(pe, "back", OD, 1)
            product_pe(pe, "b_fc", "fc", NODE[2])
            product_pe(pe, "b_D", "D_T", NODE[3])
            ends_pe(pe, "mean", OD, 32)
            product_pe(pe, "L3", "L3_W", NODE[2])

        @block.gpsimd
        def _(pool):
            pool.iota(digits[:], [[1, P]], base=0, channel_multiplier=0, allow_small_or_imprecise_dtypes=True)
            pool.iota(part_id[:], [[0, 1]], base=0, channel_multiplier=1, allow_small_or_imprecise_dtypes=True)
            pool.iota(node_id[:], [[1, NT + 1]], base=-1, channel_multiplier=NT, allow_small_or_imprecise_dtypes=True)
            pool.iota(spare_rows[:], [[0, 1]], base=NR, channel_multiplier=1)
            pool.drain()
            pool.sem_inc(S["iotas"], 1)
            order_pool(pool, OD)
            pool.wait_ge(S["filled"], 16 * FILLS)
            pool.wait_ge(S["q_made"], 1)
            spread_pool(pool, "scores", OD, 32, NODE[3], XQ)
            pool.wait_ge(S["q_kept"], 16)
            spread_first_pool(pool, "scores", OD, 32, TB["q"], spread_carry)
            pool.wait_ge(S["kv_kept"], 16)
            gather_pool(pool, "scores", TB["kv"], 64)
            ends_pool(pool, "scores", OD, 41)
            for layer in range(1, 6):
                f = 32 if layer in (1, 5) else 64
                pool.wait_ge(S["gcn_kept"], 16 * layer)
                gather_pool(pool, f"gcn{layer}", TB[f"gcn{layer}"], f)
                ends_pool(pool, f"gcn{layer}", OD, f)
            pool.wait_ge(S["add_filled"], 16 * ADD_FILLS)
            pool.wait_ge(S["za_made"], 1)
            spread_pool(pool, "attend", OD, 1, scalars(5), XA)
            pool.wait_ge(S["ad_kept"], 16)
            spread_first_pool(pool, "attend", OD, 1, TB["ad"], spread_carry)
            pool.wait_ge(S["za_kept"], 16)
            gather_pool(pool, "attend", TB["za"], 65)
            ends_pool(pool, "attend", OD, 65)
            pool.wait_ge(S["h_kept"], 16)
            gather_pool(pool, "hsum", TB["h"], 64)
            ends_pool(pool, "hsum", OD, 64)
            pool.wait_ge(S["A2_made"], 1)
            spread_pool(pool, "umlp", OD, 64, BESIDE, X64)
            pool.wait_ge(S["A2_kept"], 16)
            spread_first_pool(pool, "umlp", OD, 64, TB["a2"], spread_carry)
            pool.wait_ge(S["A1_kept"], 16)
            pool.wait_ge(S["KW_kept"], 16)
            gather_pool(pool, "umlp", TB["ka"], 128)
            add_pool(pool, "upair")
            ends_pool(pool, "umlp", OD, 64, to=BESIDE)
            pool.wait_ge(S["dh1_made"], 1)
            spread_pool(pool, "dh1", OD, 64, NODE[6], X64)
            pool.wait_ge(S["dh1_kept"], 16)
            spread_first_pool(pool, "dh1", OD, 64, TB["dh1"], spread_carry)
            add_pool(pool, "dh1")
            pool.wait_ge(S["back_made"], 1)
            spread_pool(pool, "back", OD, 67, NODE[4], XF)
            pool.wait_ge(S["back_kept"], 16)
            spread_first_pool(pool, "back", OD, 67, TB["dst"], spread_carry)
            add_pool(pool, "back")
            ends_pool(pool, "back", OD, 1)
            pool.wait_ge(S["hin_kept"], 16)
            gather_pool(pool, "mean", TB["hin"], 32)
            ends_pool(pool, "mean", OD, 32)

        @block.sync
        def _(sp):
            sp.dma_start(weights[:], weights_in).then_inc(S["weights"], 16)
            sp.dma_start(vectors[:], vectors_in.broadcast_to([P, VCOLS])).then_inc(S["weights"], 16)
            sp.dma_start(T[:, 0:J].bitcast(I32), src_in).then_inc(S["edges"], 16)
            sp.dma_start(T[:, J:2 * J].bitcast(I32), dst_in).then_inc(S["edges"], 16)
            sp.dma_start(M[:, 0:IT * P].bitcast(I32), src_t_in).then_inc(S["edges"], 16)
            sp.dma_start(w_d[:], w_in).then_inc(S["edges"], 16)
            sp.wait_ge(S["zeros"], 1)
            keys_sp(sp, OD)
            sp.dma_start(XQ[0:EP, :].rearrange("(p j) f -> p (j f)", j=J).rearrange("p (f j) -> p f j", j=J),
                         G[0][:, 0:J].unsqueeze(1).broadcast_to([P, 32, J])).then_inc(S["filled"], 16)
            sp.dma_start(XA[0:EP, :].rearrange("(p j) f -> p (j f)", j=J), G[0][:, 0:J]).then_inc(S["filled"], 16)
            firsts = list(FIRSTS)
            for f in R:
                name = firsts.pop(0) if firsts else "filled"
                sp.dma_start(R[f][EP:EP + P, :], G[0][:, 0:f]).then_inc(S[name], CREDIT)
                sp.dma_start(R[f][EP + P:EP + P + 1, :], G[0][0:1, 0:f]).then_inc(S["filled"], 16)
            upto_sp(sp, OD)
            sp.wait_ge(S["room"], 1)
            sp.dma_start(flat(0, 32), by_node(x_in)).then_inc(S["back"], 16)
            store_node(sp, "kv", TB["kv"], 2, 64)
            store_node(sp, "q", TB["q"], 3, 32)
            store_node(sp, "res0", TB["res0"], 0, 32)
            sp.wait_ge(S["scores_spread"], 16 * NT)
            feed_sp(sp, "scores", src_in, [(XQ, 32, X)])
            load_node(sp, "res0", TB["res0"], 3, 32, "res0_kept")
            store_node(sp, "res1", TB["res1"], 3, 32)
            for layer in range(1, 6):
                f = 32 if layer in (1, 5) else 64
                name = f"gcn{layer}"
                sp.wait_ge(S["gcn_made"], layer)
                sp.dma_start(by_node(TB[name]), own(layer).rearrange("p t f -> p (t f)")).then_inc(S["gcn_kept"], 16)
                if layer == 2:
                    sp.wait_ge(S["clear_zeros"], 1)
                feed_sp(sp, name, src_in, clear={2: X64, 3: XF}.get(layer))
                if layer > 1:
                    clear_sp(sp, layer - 2)
                if layer == 1:
                    sp.wait_ge(S["add_rows_made"], 1)
                    sp.dma_start(ADD_ROWS, HB[:, J:2 * J].bitcast(I32)).then_inc(S["add_rows_kept"], 16)
            load_node(sp, "res1", TB["res1"], 3, 32, "res1_kept")
            store_node(sp, "res2", TB["res2"], 3, 32)
            store_node(sp, "za", TB["za"], 4, 65)
            sp.dma_start(by_node(TB["ad"]), scalars(5)).then_inc(S["ad_kept"], 16)
            sp.wait_ge(S["attend_spread"], 16 * NT)
            feed_sp(sp, "attend", src_in, [(XA, 1, X)], saved=True)
            store_node(sp, "h", TB["h"], 1, 64)
            ka = TB["ka"].rearrange("(p t) f -> p t f", t=NT)
            sp.wait_ge(S["A1_made"], 1)
            sp.dma_start(ka[:, :, 64:128], nodes(3, 64)).then_inc(S["A1_kept"], 16)
            sp.wait_ge(S["A2_made"], 1)
            sp.dma_start(by_node(TB["a2"]), BESIDE[:, 0:NT * 64]).then_inc(S["A2_kept"], 16)
            feed_sp(sp, "hsum", src_in)
            sp.wait_ge(S["k01_made"], 1)
            sp.dma_start(by_node(TB["k0"]), flat(2, 64)).then_inc(S["k0_kept"], 16)
            sp.dma_start(by_node(TB["k1"]), flat(3, 64)).then_inc(S["k1_kept"], 16)
            sp.wait_ge(S["KW_made"], 1)
            sp.dma_start(ka[:, :, 0:64], nodes(5, 64)).then_inc(S["KW_kept"], 16)
            sp.wait_ge(S["umlp_spread"], 16 * NT)
            feed_sp(sp, "umlp", src_in, [(X64, 64, X)])
            for b in range(2):
                sp.wait_ge(S[f"stored{b}"], STORED["upair"])
            feed_sp(sp, "upair", None, [(UD, 129, G)])
            load_sums_sp(sp, "upair")
            load_node(sp, "k1", TB["k1"], 7, 64, "k1_kept")
            load_node(sp, "k0", TB["k0"], 4, 64, "k0_kept")
            store_node(sp, "dh1", TB["dh1"], 6, 64)
            store_node(sp, "dhu", TB["w2"], 5, 64)
            sp.wait_ge(S["dh1_spread"], 16 * NT)
            feed_sp(sp, "dh1", None, [(X64, 64, X)])
            load_sums_sp(sp, "dh1")
            load_node(sp, "dhu", TB["w2"], 2, 64, "dhu_kept")
            load_node(sp, "h", TB["h"], 3, 64, "h_kept")
            sp.wait_ge(S["back_made"], 1)
            sp.dma_start(by_node(TB["dst"]), flat(4, 67)).then_inc(S["back_kept"], 16)
            sp.wait_ge(S["back_spread"], 16 * NT)
            feed_sp(sp, "back", None, [(ZA, 65, G), (XF, 67, X)])
            load_sums_sp(sp, "back")
            load_node(sp, "res2", TB["res2"], 6, 32, "res2_kept")
            store_node(sp, "res3", TB["res3"], 6, 32)
            store_node(sp, "hin", TB["hin"], 1, 32)
            feed_sp(sp, "mean", src_in)
            load_node(sp, "hin", TB["hin"], 1, 32, "hin_kept")
            load_node(sp, "res3", TB["res3"], 5, 32, "res3_kept")
            sp.wait_ge(S["result"], 1)
            sp.dma_start(out.rearrange("(p t) f -> p (t f)", t=NT), NODE[4][0:N // NT, 0:NT * 32]).then_inc(S["out"], 16)
            sp.wait_ge(S["out"], 16)


def kernel(**inputs):
    import numpy as np
    import concourse.bacc as bacc
    from concourse.bass_utils import run_bass_kernel_spmd as run

    def edges(a, fill):
        padded = np.full((EP,), fill, a.dtype)
        padded[:E] = a
        return padded.reshape(P, J)

    x = np.zeros((NR, 32), np.float32)
    x[:N] = inputs["x"]
    places, width = weight_places()
    weights = np.zeros((P, width), np.float32)
    for name, source, transposed, rows, cols in weight_plan():
        parts = [np.asarray(inputs[s]) for s in (source if isinstance(source, tuple) else (source,))]
        w = np.concatenate([p.T if transposed else p for p in parts], axis=1)
        for i in range(P // rows):
            at = places[name][0] + i * cols
            weights[i * rows:(i + 1) * rows, at:at + cols] = w
    src_t = edges(np.asarray(inputs["src"]), PAD).reshape(P, IT, 2 * CJ).transpose(2, 1, 0).reshape(2 * CJ, IT * P)
    src_t = np.concatenate([src_t, src_t])
    places, width = vector_places()
    vectors = np.zeros((1, width), np.float32)
    for name in VECTORS:
        at, size = places[name]
        vectors[0, at:at + size] = np.asarray(inputs[name]).reshape(-1)
    arrays = {"x": x, "src": edges(np.asarray(inputs["src"]), PAD), "dst": edges(np.asarray(inputs["dst"]), PAD),
              "src_t": src_t, "w": edges(np.asarray(inputs["edge_weight"]), 0), "weights": weights, "vectors": vectors}
    nc = bacc.Bacc("TRN2", target_bir_lowering=False, num_devices=1)
    args = [nc.dram_tensor(f"in_{k}", a.shape, mybir.dt.from_np(a.dtype), kind="ExternalInput").ap()
            for k, a in arrays.items()]
    out = nc.dram_tensor("out_x", (N, 32), F32, kind="ExternalOutput").ap()
    build(nc, *args, out)
    r = run(nc, [{f"in_{k}": a for k, a in arrays.items()}], core_ids=[0])
    return r.results[0]["out_x"]
```
